# Optimizing a Trainium2 kernel written in Bass

```python
import numpy as np
import jax
import jax.numpy as jnp

def _softmax(x, axis=-1):
    return jax.nn.softmax(x, axis=axis)

def _gelu(x):
    return jax.nn.gelu(x, approximate=True)

def _silu(x):
    return jax.nn.silu(x)

def _sigmoid(x):
    return jax.nn.sigmoid(x)

def _layernorm(x, axis=-1, eps=1e-05):
    m = jnp.mean(x, axis=axis, keepdims=True)
    v = jnp.var(x, axis=axis, keepdims=True)
    return (x - m) / jnp.sqrt(v + eps)

def _scatter_add(tgt, idx, src, axis=0):
    return tgt.at[idx].add(src)

def _segment_sum(src, seg, n):
    return jax.ops.segment_sum(src, seg, n)
kernel_name = 'mk_flamingo_gated_d2_seqx_r8_9a86ac'

def setup_inputs(seed: int=0):
    np.random.seed(seed)
    _w = jnp.asarray

    def _rec_inputs():
        import jax
        import jax.numpy as jnp
        _rk = jax.random.key(seed)
        x = 0.01048 + 0.1018 * jax.random.normal(jax.random.fold_in(_rk, 1), (4, 256, 256), jnp.float32)
        _lenS = 256 - jax.random.randint(jax.random.fold_in(_rk, 7), (4,), 0, max(1, 256 // 4) + 1, jnp.int32)
        _lenS2 = 256 - jax.random.randint(jax.random.fold_in(_rk, 8), (4,), 0, max(1, 256 // 4) + 1, jnp.int32)
        _ctx_512P = jax.random.normal(jax.random.fold_in(_rk, 11), (4, 16, 64), jnp.float32)
        _ctx_512c = jax.random.dirichlet(jax.random.fold_in(_rk, 511), 0.3 * jnp.ones((16,), jnp.float32), (4, 256))
        _ctx_512t = jnp.einsum('bsk,bkd->bsd', _ctx_512c, _ctx_512P)
        _ctx_512t = _ctx_512t * jax.lax.rsqrt(jnp.mean(jnp.square(_ctx_512t)) + 1e-12) * 0.953939
        ctx_512 = -0.000292821 + 1.00034 * (_ctx_512t + 0.3 * jax.random.normal(jax.random.fold_in(_rk, 611), (4, 256, 64), jnp.float32))
        _g = jax.random.normal(jax.random.fold_in(_rk, 9001), (2, 2), jnp.float32)
        _g = jnp.sign(_g) * jnp.maximum(jnp.abs(_g), 1.0) + (_g == 0) * 1.0
        g_xattn = _g[0]
        g_ffn = _g[1]
        return (x, ctx_512, g_xattn, g_ffn)
    x, ctx_512, g_xattn, g_ffn = _rec_inputs()

    def _L0_xattn_setup():
        import jax, jax.numpy as jnp
        import numpy as np
        LRELU_ALPHA = 0.2
        MASK_VAL = -10000000000.0
        B, N, F_IN = (4, 256, 64)
        H, F_OUT = (8, 32)
        F_HID = H * F_OUT

        def gat_layer(x, adj, W, a_self, a_neigh, b):
            feat = jnp.einsum('nf,hfo->hno', x, W)
            attn_self = jnp.einsum('hno,ho->hn', feat, a_self)
            attn_neigh = jnp.einsum('hno,ho->hn', feat, a_neigh)
            e = attn_self[:, :, None] + attn_neigh[:, None, :]
            e = jax.nn.leaky_relu(e, LRELU_ALPHA)
            e = e + MASK_VAL * (1.0 - adj)[None, :, :]
            alpha = jax.nn.softmax(e, axis=-1)
            out = jnp.einsum('hnm,hmo->hno', alpha, feat) + b[:, None, :]
            out = jnp.transpose(out, (1, 0, 2)).reshape(out.shape[1], -1)
            return jax.nn.elu(out)
        key = jax.random.key(seed)
        ks = jax.random.split(key, 10)
        feats = jax.random.normal(ks[0], (B, N, F_IN), dtype=jnp.float32)
        a = (jax.random.uniform(ks[1], (B, N, N)) < 0.01).astype(jnp.float32)
        adj = jnp.maximum(a, jnp.eye(N, dtype=jnp.float32)[None])
        s0 = 1.0 / np.sqrt(F_IN)
        s1 = 1.0 / np.sqrt(F_HID)
        return {'feats': feats, 'adj': adj, 'W0': jax.random.normal(ks[2], (H, F_IN, F_OUT), dtype=jnp.float32) * s0, 'a_self0': jax.random.normal(ks[3], (H, F_OUT), dtype=jnp.float32) * 0.1, 'a_neigh0': jax.random.normal(ks[4], (H, F_OUT), dtype=jnp.float32) * 0.1, 'b0': jnp.zeros((H, F_OUT), dtype=jnp.float32), 'W1': jax.random.normal(ks[5], (H, F_HID, F_OUT), dtype=jnp.float32) * s1, 'a_self1': jax.random.normal(ks[6], (H, F_OUT), dtype=jnp.float32) * 0.1, 'a_neigh1': jax.random.normal(ks[7], (H, F_OUT), dtype=jnp.float32) * 0.1, 'b1': jnp.zeros((H, F_OUT), dtype=jnp.float32)}
    _L0_xattn_all = _L0_xattn_setup()
    _L0_xattn_in = {k: v for k, v in _L0_xattn_all.items() if k in ('W0', 'a_self0', 'a_neigh0', 'b0', 'W1', 'a_self1', 'a_neigh1', 'b1')}
    del _L0_xattn_all

    def _L0_ffn_setup():
        import jax, jax.numpy as jnp
        import numpy as np
        HIDDEN = 256
        INTER = 704
        B, S = (2, 256)

        def _ternary(key, shape):
            return jax.random.randint(key, shape, -1, 2).astype(jnp.float32)
        key = jax.random.key(seed)
        ks = jax.random.split(key, 7)
        x = jax.random.normal(ks[0], (B, S, HIDDEN), dtype=jnp.float32)
        gate_w = _ternary(ks[1], (INTER, HIDDEN))
        up_w = _ternary(ks[2], (INTER, HIDDEN))
        down_w = _ternary(ks[3], (HIDDEN, INTER))
        gate_s = jax.random.uniform(ks[4], (INTER,), minval=0.01, maxval=0.1, dtype=jnp.float32)
        up_s = jax.random.uniform(ks[5], (INTER,), minval=0.01, maxval=0.1, dtype=jnp.float32)
        down_s = jax.random.uniform(ks[6], (HIDDEN,), minval=0.01, maxval=0.1, dtype=jnp.float32)
        return {'x': x, 'gate_w': gate_w, 'up_w': up_w, 'down_w': down_w, 'gate_s': gate_s, 'up_s': up_s, 'down_s': down_s}
    _L0_ffn_all = _L0_ffn_setup()
    _L0_ffn_in = {k: v for k, v in _L0_ffn_all.items() if k in ('gate_w', 'up_w', 'down_w', 'gate_s', 'up_s', 'down_s')}
    del _L0_ffn_all

    def _L1_xattn_setup():
        import jax, jax.numpy as jnp
        import numpy as np
        B, N, D = (16, 256, 64)
        H = 4
        TOP_K_RATIO = 0.3
        key = jax.random.key(seed)
        k1, k2, k3, k4 = jax.random.split(key, 4)
        h = jax.random.normal(k1, (B, N, D), dtype=jnp.float32)
        adj_raw = jax.random.uniform(k2, (B, N, N), dtype=jnp.float32)
        lim = 1.0 / np.sqrt(D)
        Wq = jax.random.uniform(k3, (D, D), minval=-lim, maxval=lim, dtype=jnp.float32)
        Wk = jax.random.uniform(k4, (D, D), minval=-lim, maxval=lim, dtype=jnp.float32)
        gamma_raw = jnp.float32(-0.85)
        return {'h': h, 'adj_raw': adj_raw, 'Wq': Wq, 'Wk': Wk, 'gamma_raw': gamma_raw}
    _L1_xattn_all = _L1_xattn_setup()
    _L1_xattn_in = {k: v for k, v in _L1_xattn_all.items() if k in ('Wq', 'Wk', 'gamma_raw')}
    del _L1_xattn_all

    def _L1_ffn_setup():
        import jax, jax.numpy as jnp
        import numpy as np
        E = 8
        H = 256
        F = 512
        B, S = (2, 128)
        JITTER = 0.01
        TOP_K = 2

        def _masked_sampling_omp(scores):
            vals, idx = jax.lax.top_k(scores, TOP_K)
            abs_s = jnp.abs(scores)
            thr1 = vals[:, 0:1]
            factor1 = jnp.maximum(abs_s, thr1)
            mask1 = (thr1 - scores) / factor1 > 2.0 * JITTER
            p1 = jax.nn.softmax(jnp.where(mask1, -jnp.inf, scores), axis=-1)
            m1 = jnp.take_along_axis(p1, idx[:, 0:1], axis=-1)
            thr2 = vals[:, 1:2]
            factor2 = jnp.maximum(abs_s, thr2)
            mask2 = (thr2 - scores) / factor2 > 2.0 * JITTER
            is_top1 = jnp.arange(scores.shape[-1])[None, :] == idx[:, 0:1]
            p2 = jax.nn.softmax(jnp.where(is_top1 | mask2, -jnp.inf, scores), axis=-1)
            m2 = jnp.take_along_axis(p2, idx[:, 1:2], axis=-1)
            return (jnp.concatenate([m1, m2], axis=-1), idx)
        key = jax.random.key(seed)
        k0, k1, k2, k3, k4 = jax.random.split(key, 5)
        s = 0.02
        return {'hidden_states': jax.random.normal(k0, (B, S, H), jnp.float32), 'gate_w': jax.random.normal(k1, (E, H), jnp.float32) * s, 'w1': jax.random.normal(k2, (E, F, H), jnp.float32) * s, 'w2': jax.random.normal(k3, (E, H, F), jnp.float32) * s, 'w3': jax.random.normal(k4, (E, F, H), jnp.float32) * s}
    _L1_ffn_all = _L1_ffn_setup()
    _L1_ffn_in = {k: v for k, v in _L1_ffn_all.items() if k in ('gate_w', 'w1', 'w2', 'w3')}
    del _L1_ffn_all
    return {'x': x, 'ctx_512': ctx_512, 'g_xattn': g_xattn, 'g_ffn': g_ffn, 'L0_xattn_W0': _L0_xattn_in['W0'], 'L0_xattn_a_self0': _L0_xattn_in['a_self0'], 'L0_xattn_a_neigh0': _L0_xattn_in['a_neigh0'], 'L0_xattn_b0': _L0_xattn_in['b0'], 'L0_xattn_W1': _L0_xattn_in['W1'], 'L0_xattn_a_self1': _L0_xattn_in['a_self1'], 'L0_xattn_a_neigh1': _L0_xattn_in['a_neigh1'], 'L0_xattn_b1': _L0_xattn_in['b1'], 'L0_ffn_gate_w': _L0_ffn_in['gate_w'], 'L0_ffn_up_w': _L0_ffn_in['up_w'], 'L0_ffn_down_w': _L0_ffn_in['down_w'], 'L0_ffn_gate_s': _L0_ffn_in['gate_s'], 'L0_ffn_up_s': _L0_ffn_in['up_s'], 'L0_ffn_down_s': _L0_ffn_in['down_s'], 'L1_xattn_Wq': _L1_xattn_in['Wq'], 'L1_xattn_Wk': _L1_xattn_in['Wk'], 'L1_xattn_gamma_raw': _L1_xattn_in['gamma_raw'], 'L1_ffn_gate_w': _L1_ffn_in['gate_w'], 'L1_ffn_w1': _L1_ffn_in['w1'], 'L1_ffn_w2': _L1_ffn_in['w2'], 'L1_ffn_w3': _L1_ffn_in['w3']}

def reference(x, ctx_512, g_xattn, g_ffn, L0_xattn_W0, L0_xattn_a_self0, L0_xattn_a_neigh0, L0_xattn_b0, L0_xattn_W1, L0_xattn_a_self1, L0_xattn_a_neigh1, L0_xattn_b1, L0_ffn_gate_w, L0_ffn_up_w, L0_ffn_down_w, L0_ffn_gate_s, L0_ffn_up_s, L0_ffn_down_s, L1_xattn_Wq, L1_xattn_Wk, L1_xattn_gamma_raw, L1_ffn_gate_w, L1_ffn_w1, L1_ffn_w2, L1_ffn_w3):
    import jax
    import jax.numpy as jnp

    def _L0_xattn_ref(feats, adj, W0, a_self0, a_neigh0, b0, W1, a_self1, a_neigh1, b1):
        import jax, jax.numpy as jnp
        import numpy as np
        LRELU_ALPHA = 0.2
        MASK_VAL = -10000000000.0
        B, N, F_IN = (4, 256, 64)
        H, F_OUT = (8, 32)
        F_HID = H * F_OUT

        def gat_layer(x, adj, W, a_self, a_neigh, b):
            feat = jnp.einsum('nf,hfo->hno', x, W)
            attn_self = jnp.einsum('hno,ho->hn', feat, a_self)
            attn_neigh = jnp.einsum('hno,ho->hn', feat, a_neigh)
            e = attn_self[:, :, None] + attn_neigh[:, None, :]
            e = jax.nn.leaky_relu(e, LRELU_ALPHA)
            e = e + MASK_VAL * (1.0 - adj)[None, :, :]
            alpha = jax.nn.softmax(e, axis=-1)
            out = jnp.einsum('hnm,hmo->hno', alpha, feat) + b[:, None, :]
            out = jnp.transpose(out, (1, 0, 2)).reshape(out.shape[1], -1)
            return jax.nn.elu(out)

        def per_graph(x, a):
            h = gat_layer(x, a, W0, a_self0, a_neigh0, b0)
            return gat_layer(h, a, W1, a_self1, a_neigh1, b1)
        return jax.vmap(per_graph)(feats, adj)

    def _L0_ffn_ref(x, gate_w, up_w, down_w, gate_s, up_s, down_s):
        import jax, jax.numpy as jnp
        import numpy as np
        HIDDEN = 256
        INTER = 704
        B, S = (2, 256)

        def _ternary(key, shape):
            return jax.random.randint(key, shape, -1, 2).astype(jnp.float32)
        b, s, h = x.shape
        xf = x.reshape(b * s, h)
        g = jnp.einsum('th,ih->ti', xf, gate_w) * gate_s
        u = jnp.einsum('th,ih->ti', xf, up_w) * up_s
        hdn = jax.nn.silu(g) * u
        out = jnp.einsum('ti,hi->th', hdn, down_w) * down_s
        return out.reshape(b, s, -1)

    def _L1_xattn_ref(h, adj_raw, Wq, Wk, gamma_raw):
        import jax, jax.numpy as jnp
        import numpy as np
        B, N, D = (16, 256, 64)
        H = 4
        TOP_K_RATIO = 0.3
        b, n, dm = h.shape
        d = dm // H
        Q = (h @ Wq.T).reshape(b, n, H, d).transpose(0, 2, 1, 3)
        K = (h @ Wk.T).reshape(b, n, H, d).transpose(0, 2, 1, 3)
        sim = jnp.einsum('bhnd,bhmd->bnm', Q, K) / (jnp.sqrt(jnp.float32(d)) * H)
        k = max(1, int(n * TOP_K_RATIO))
        topk_vals = jax.lax.top_k(sim, k)[0]
        threshold = topk_vals[:, :, -1:]
        sparse_mask = (sim >= threshold).astype(sim.dtype)
        A_learned = jax.nn.sigmoid(sim) * sparse_mask
        A_learned = (A_learned + jnp.swapaxes(A_learned, -1, -2)) * 0.5
        gamma = jax.nn.sigmoid(gamma_raw)
        return (1.0 - gamma) * adj_raw + gamma * A_learned

    def _L1_ffn_ref(hidden_states, gate_w, w1, w2, w3):
        import jax, jax.numpy as jnp
        import numpy as np
        E = 8
        H = 256
        F = 512
        B, S = (2, 128)
        JITTER = 0.01
        TOP_K = 2

        def _masked_sampling_omp(scores):
            vals, idx = jax.lax.top_k(scores, TOP_K)
            abs_s = jnp.abs(scores)
            thr1 = vals[:, 0:1]
            factor1 = jnp.maximum(abs_s, thr1)
            mask1 = (thr1 - scores) / factor1 > 2.0 * JITTER
            p1 = jax.nn.softmax(jnp.where(mask1, -jnp.inf, scores), axis=-1)
            m1 = jnp.take_along_axis(p1, idx[:, 0:1], axis=-1)
            thr2 = vals[:, 1:2]
            factor2 = jnp.maximum(abs_s, thr2)
            mask2 = (thr2 - scores) / factor2 > 2.0 * JITTER
            is_top1 = jnp.arange(scores.shape[-1])[None, :] == idx[:, 0:1]
            p2 = jax.nn.softmax(jnp.where(is_top1 | mask2, -jnp.inf, scores), axis=-1)
            m2 = jnp.take_along_axis(p2, idx[:, 1:2], axis=-1)
            return (jnp.concatenate([m1, m2], axis=-1), idx)
        Bd, Sd, Hd = hidden_states.shape
        x = hidden_states.reshape(-1, Hd)
        scores = x @ gate_w.T
        mult, sel = _masked_sampling_omp(scores)
        h = jax.nn.silu(jnp.einsum('th,efh->etf', x, w1)) * jnp.einsum('th,efh->etf', x, w3)
        y = jnp.einsum('etf,ehf->eth', h, w2)
        coef = (jax.nn.one_hot(sel, gate_w.shape[0], dtype=x.dtype) * mult[..., None]).sum(axis=1)
        out = jnp.einsum('te,eth->th', coef, y)
        return out.reshape(Bd, Sd, Hd)
    x = x + jnp.tanh(g_xattn[0]) * _L0_xattn_ref(ctx_512, _layernorm(x, axis=-1), L0_xattn_W0, L0_xattn_a_self0, L0_xattn_a_neigh0, L0_xattn_b0, L0_xattn_W1, L0_xattn_a_self1, L0_xattn_a_neigh1, L0_xattn_b1)
    x = x + jnp.tanh(g_ffn[0]) * _L0_ffn_ref(_layernorm(x, axis=-1), L0_ffn_gate_w, L0_ffn_up_w, L0_ffn_down_w, L0_ffn_gate_s, L0_ffn_up_s, L0_ffn_down_s)
    x = x + jnp.tanh(g_xattn[1]) * _L1_xattn_ref(ctx_512, _layernorm(x, axis=-1), L1_xattn_Wq, L1_xattn_Wk, L1_xattn_gamma_raw)
    x = x + jnp.tanh(g_ffn[1]) * _L1_ffn_ref(_layernorm(x, axis=-1), L1_ffn_gate_w, L1_ffn_w1, L1_ffn_w2, L1_ffn_w3)
    return x

_drawn_inputs = setup_inputs


def setup_inputs(seed=0):
    import zlib

    import numpy as np

    out = dict(_drawn_inputs(seed))
    spreads = {'g_ffn': (-1.0, 0.2), 'L0_xattn_b0': (0.0, 0.1), 'L0_xattn_b1': (0.0, 0.1)}
    factors = {}
    for name, (base, spread) in spreads.items():
        noise = np.random.default_rng([zlib.crc32(name.encode()), seed]).standard_normal(out[name].shape)
        drawn = base * np.exp(spread * noise) if base else spread * noise
        out[name] = jnp.asarray(drawn.astype(out[name].dtype))
    for name, factor in factors.items():
        out[name] = (out[name] * factor).astype(out[name].dtype)
    return out
```

```python
from contextlib import ExitStack

import concourse.bass as bass
from concourse import mybir

F32, I32, U32 = mybir.dt.float32, mybir.dt.int32, mybir.dt.uint32
ALU = mybir.AluOpType
ACT = mybir.ActivationFunctionType
AX = mybir.AxisListType

P = 128
B, N, C = 4, 256, 256
T = B * N // P
D = 64
H, FO = 8, 32
WX = H * FO + 2 * H
INTER = 704
IT = -(-INTER // P)
E, F = 8, 512
TOPK = max(1, int(N * 0.3))
ROUNDS = -(-TOPK // 8)
SLOTS = 2 * B * N
NB = SLOTS // P + E - 1
NL = NB + 2
PAIRS = (NB - 1) // 2
PAD = 4096
HT = T // 2
HN = HT * P
EPS = 1e-5
BIG = 1e10
LEAD, ULPS, LOGIT = 2e4, 2.0 ** -21, 2000.0


def rows(ap):
    n = 1
    for s in ap.shape:
        n *= s
    flat = ap if len(ap.shape) == 1 else ap.rearrange("a b -> (a b)")
    return flat.rearrange("(a n) -> a n", a=1).to_broadcast([P, n])


def build(nc, x_in, ctx_in, ctxT_in, g_xattn, g_ffn, gamma, w0_in, as0, an0, b0_in, w1_in, as1, an1,
          b1_in, gw_in, uw_in, dw_in, gs_in, us_in, ds_in, wq_in, wk_in, rg_in, e1_in, e3_in, e2_in,
          out, force_general=False):
    xn3_dram = nc.dram_tensor("xn3_rows", [B * N, C], F32, kind="Internal").ap()
    ctx = ExitStack()
    with ctx:
        def sb(name, shape, dt=F32):
            return ctx.enter_context(nc.sbuf_tensor(name, shape, dt))

        def sem(name):
            return ctx.enter_context(nc.semaphore(name))

        PS = ctx.enter_context(nc.psum_tensor("PS", [P, 8, 512], F32))

        ident = sb("ident", [P, P])
        ones = sb("ones", [P, P])
        before = sb("before", [P, P])
        iota_p = sb("iota_p", [P, P])
        iota_e = sb("iota_e", [P, E])
        iota_q = sb("iota_q", [P, E])
        iota_b = sb("iota_b", [P, NL])
        token = sb("token", [P, 2 * T])
        nhalf = sb("nhalf", [P, HT])
        x = sb("x", [P, T, C])
        ctx_s = sb("ctx_s", [P, T, D])
        ctxT = sb("ctxT", [D, B * N])
        w0x = sb("w0x", [D, WX])
        w1x = sb("w1x", [P, 2, WX])
        b0 = sb("b0", [P, 2])
        b1 = sb("b1", [P, C])
        gates = sb("gates", [P, 5])
        tg = sb("tg", [P, 5])
        cc = sb("cc", [P, 4])
        e1 = sb("e1", [P, E * 1024])
        e3 = sb("e3", [P, E * 1024])
        e2 = sb("e2", [P, E * 1024])
        gw = e1[:, 5 * 1024:5 * 1024 + 2 * INTER].rearrange("p (k n) -> p k n", k=2)
        uw = e3[:, 5 * 1024:5 * 1024 + 2 * INTER].rearrange("p (k n) -> p k n", k=2)
        dw = e2[:, 5 * 1024:5 * 1024 + IT * C].rearrange("p (k n) -> p k n", k=IT)
        gs = sb("gs", [P, IT])
        us = sb("us", [P, IT])
        hgs = sb("hgs", [P, IT])
        cgu = sb("cgu", [P, IT])
        dsr = sb("dsr", [P, C])
        wq = sb("wq", [D, D])
        wk = sb("wk", [D, D])
        rg = sb("rg", [P, 2, E])
        xr = x
        mask = e1[:, 7 * 1024:8 * 1024].rearrange("p (t c) -> p t c", t=HT)
        hot = e3[:, 7 * 1024:8 * 1024].rearrange("p (t c) -> p t c", t=HT)
        hotT = e2[:, 7 * 1024:8 * 1024].rearrange("p (b m c) -> p b m c", b=2, m=2)
        g0T = sb("g0T", [D, HN])
        h0T = sb("h0T", [P, 2, HN])
        feat = sb("feat", [P, HT, WX])
        st0 = sb("st0", [P, T, 2 * H])
        za = sb("za", [P, HT * C])
        zb = sb("zb", [P, HT * C])
        zc = sb("zc", [P, HT * C])
        xn = sb("xn", [P, HT, C])
        xnT = sb("xnT", [P, 2, 2, HN])
        th = sb("th", [P, 2, F])
        wbuf = sb("wbuf", [P, 2, F])
        hT = sb("hT", [P, IT, HN])
        avec = hT[:, 0:2, :].rearrange("p a (b n) -> p (a b) n", b=2)
        qk = zc
        sim = sb("sim", [P, T, N])
        work = sb("work", [P, N])
        a2 = sb("a2", [P, T, N])
        t8 = sb("t8", [P, 8])
        stat = sb("stat", [P, HT, 6])
        mv = sb("mv", [P, HT, 2])
        veps = sb("veps", [P, HT])
        rstd = sb("rstd", [P, HT])
        top = sb("top", [P, HT, 8])
        good = sb("good", [P, HT + 2 * HT * 2 * H])
        gsm = sb("gsm", [P, 2 * HT * 2 * H])
        gmin = sb("gmin", [P, 2])
        flag = sb("flag", [P, 2], I32)
        gctxT = sb("gctxT", [D, N])
        gfeat = feat[:, 0:2, :]
        gD = sb("gD", [P, 2, P])
        gEa = h0T[:, 0, :].rearrange("p (a n) -> p a n", a=2)
        gEb = h0T[:, 1, :].rearrange("p (a n) -> p a n", a=2)
        gnm = sb("gnm", [P, 2])
        gsum = sb("gsum", [P, 2])
        grs = sb("grs", [P, 2])
        gout = feat[:, 2:4, 0:C]
        sc = sb("sc", [P, T, E])
        mx8 = sb("mx8", [P, T, 8])
        ix8 = sb("ix8", [P, T, 8], U32)
        idxf = sb("idxf", [P, T, 2])
        O = sb("O", [P, 2, T, E])
        Os = sb("Os", [P, T, E])
        Dk = sb("Dk", [P, 2, T, E])
        Fk = sb("Fk", [P, 2, T, E])
        Ek = sb("Ek", [P, 2, T, E])
        ab = sb("ab", [P, T, E])
        mk = sb("mk", [P, 2 * T])
        nb = sb("nb", [P, E, E])
        nblk = sb("nblk", [P, E])
        incl = sb("incl", [P, E])
        base = sb("base", [P, E])
        one8 = sb("one8", [P, E])
        ecmp = sb("ecmp", [P, NL, E])
        eblk = sb("eblk", [P, NL])
        eoff = sb("eoff", [P, NL], I32)
        rk = sb("rk", [P, T, E])
        slf = sb("slf", [P, 2 * T])
        sli = sb("sli", [P, 2 * T], I32)
        sji = sb("sji", [P, 2 * T], I32)
        spi = sb("spi", [P, 2 * T], I32)
        sjf = sb("sjf", [P, 2 * T])
        spf = sb("spf", [P, 2 * T])
        RH = sim[:, :, :].rearrange("p t n -> p (t n)")[:, 0:6 * T * NL].rearrange("p (a b) -> p a b", a=2 * T)
        Ph = sb("Ph", [P, 2, P])
        lst = sb("lst", [P, NL])
        idsu = sb("idsu", [P, NL], U32)
        coef = sb("coef", [P, NL])
        gidx = [sb(f"gidx{q}", [P, 1], U32) for q in range(2)]
        sidx = [sb(f"sidx{q}", [P, 1], U32) for q in range(2)]
        xg = [zc[:, q * C:(q + 1) * C] for q in range(2)]
        hh = [hT[:, q, :] for q in range(2)]
        hhT = [hT[:, 2 + q, :] for q in range(2)]
        yv = [hT[:, 4, q * C:(q + 1) * C] for q in range(2)]
        xgT = [hT[:, 5, q * C:(q + 1) * C].rearrange("p (k n) -> p k n", k=2) for q in range(2)]

        x_loaded = [sem(f"x_loaded{h}") for h in range(2)]
        ctx_loaded = sem("ctx_loaded")
        qk_loaded = sem("qk_loaded")
        gat_loaded = sem("gat_loaded")
        ffn_loaded = sem("ffn_loaded")
        router_loaded = sem("router_loaded")
        experts_loaded = sem("experts_loaded")
        consts = sem("consts")
        gates_tanh = sem("gates_tanh")
        dve_done = sem("dve_done")
        act_done = sem("act_done")
        pool_done = sem("pool_done")
        pool_passed = sem("pool_passed")
        var_ready = sem("var_ready")
        rstd_ready = sem("rstd_ready")
        qk_done = sem("qk_done")
        qk_copied = sem("qk_copied")
        sim_done = sem("sim_done")
        sim_copied = sem("sim_copied")
        sig_ready = sem("sig_ready")
        a2_ready = sem("a2_ready")
        a2T_done = sem("a2T_done")
        x3_ready = sem("x3_ready")
        wx_ready = sem("wx_ready")
        st0_done = sem("st0_done")
        st0_copied = sem("st0_copied")
        hot_ready = sem("hot_ready")
        hotT_done = sem("hotT_done")
        hotT_copied = sem("hotT_copied")
        g0_done = sem("g0_done")
        g0_copied = sem("g0_copied")
        h0_done = sem("h0_done")
        h0_min = sem("h0_min")
        h0_exp = sem("h0_exp")
        h0_ready = sem("h0_ready")
        feat_done = sem("feat_done")
        feat_copied = sem("feat_copied")
        out1_done = sem("out1_done")
        out1_read = sem("out1_read")
        out1_min = sem("out1_min")
        out1_exp = sem("out1_exp")
        good_ready = sem("good_ready")
        graph_over = sem("graph_over")
        bad_counted = sem("bad_counted")
        flag_ready = sem("flag_ready")
        general = [sem(f"general{h}") for h in range(2)]
        xn_ready = sem("xn_ready")
        xnT_done = sem("xnT_done")
        xnT_copied = sem("xnT_copied")
        ffn_g_done = sem("ffn_g_done")
        ffn_u_done = sem("ffn_u_done")
        ffn_tanh = sem("ffn_tanh")
        ffn_h_ready = sem("ffn_h_ready")
        down_done = sem("down_done")
        down_read = sem("down_read")
        rows_stored = sem("rows_stored")
        out_stored = sem("out_stored")
        scores_done = sem("scores_done")
        scores_read = sem("scores_read")
        d_ready = sem("d_ready")
        ek_ready = sem("ek_ready")
        onehots_ready = sem("onehots_ready")
        count_done = sem("count_done")
        rank_done = sem("rank_done")
        rh_ready = sem("rh_ready")
        ph_ready = sem("ph_ready")
        ph_used = sem("ph_used")
        eoff_ready = sem("eoff_ready")
        list_done = sem("list_done")
        list_ready = sem("list_ready")
        xg_clear = sem("xg_clear")
        gidx_set = sem("gidx_set")
        gathered = [sem(f"gathered{q}") for q in range(2)]
        xgT_done = sem("xgT_done")
        xgT_copied = sem("xgT_copied")
        up1_done = sem("up1_done")
        up3_done = sem("up3_done")
        silu_tanh = sem("silu_tanh")
        w_ready = sem("w_ready")
        gated = sem("gated")
        hhT_done = sem("hhT_done")
        hhT_copied = sem("hhT_copied")
        y_done = sem("y_done")
        y_scaled = sem("y_scaled")
        sidx_set = sem("sidx_set")
        scattered = [sem(f"scattered{q}") for q in range(2)]

        CONSTS = 10
        LN = {("graph", 0): 0, ("ffn", 0): 1, ("graph", 1): 2, ("ffn", 1): 3,
              ("attn", 0): 4, ("moe", 0): 5, ("attn", 1): 6, ("moe", 1): 7}
        XT = {("ffn", 0): 0, ("ffn", 1): 1, ("moe", 0): 2, ("moe", 1): 3}
        SCHEDULE = ([("graph_hot", 0), ("sims", 0), ("graph_first", 0), ("graph_hidden", 0), ("graph_feat", 0),
                     ("graph_out", 0), ("graph_check", 0), ("ffn_norm", 0)]
                    + [s for it, g in enumerate(["graph_hot", "graph_first", "graph_hidden", "graph_feat",
                                                 "graph_out", "graph_check"])
                       for s in [("ffn_up", 0, it), (g, 1)]]
                    + [("ffn_down", 0), ("ffn_norm", 1), ("ffn_up", 1, 0), ("ffn_up", 1, 1),
                       ("attn", 0), ("ffn_up", 1, 2), ("ffn_up", 1, 3), ("router", 0),
                       ("ffn_up", 1, 4), ("ffn_up", 1, 5), ("ffn_down", 1), ("attn", 1), ("router", 1)])

        HEAD_STEPS = 12
        PRE_STEPS, MID_STEPS, POST_STEPS = 3, 7, 5
        BATCH_STEPS = PRE_STEPS + MID_STEPS + POST_STEPS + 2 * H * HEAD_STEPS

        block = ctx.enter_context(nc.Block())

        @block.sync
        def _(sp):
            xv = x_in.rearrange("(t p) c -> p t c", p=P)
            sp.dma_start(x[:, 0:HT, :], xv[:, 0:HT, :]).then_inc(x_loaded[0], 16)
            sp.dma_start(ctxT[:, :], ctxT_in).then_inc(qk_loaded, 16)
            sp.dma_start(wq[:, :], wq_in).then_inc(qk_loaded, 16)
            sp.dma_start(wk[:, :], wk_in).then_inc(qk_loaded, 16)
            sp.dma_start(ctx_s[:, :, :], ctx_in.rearrange("(t p) d -> p t d", p=P)).then_inc(ctx_loaded, 16)
            sp.dma_start(w0x[:, 0:H * FO], w0_in).then_inc(gat_loaded, 16)
            sp.dma_start(w1x[:, :, 0:H * FO], w1_in.rearrange("(k p) n -> p k n", p=P)).then_inc(gat_loaded, 16)
            for n, a in enumerate((as0, an0, as1, an1)):
                sp.dma_start(avec[:, n, :], rows(a)).then_inc(gat_loaded, 16)
            sp.dma_start(b0[:, :], b0_in).then_inc(gat_loaded, 16)
            sp.dma_start(b1[:, :], rows(b1_in)).then_inc(gat_loaded, 16)
            sp.dma_start(gates[:, 0:2], rows(g_xattn)).then_inc(gat_loaded, 16)
            sp.dma_start(gates[:, 2:4], rows(g_ffn)).then_inc(gat_loaded, 16)
            sp.dma_start(gates[:, 4:5], rows(gamma)).then_inc(gat_loaded, 16)
            sp.dma_start(x[:, HT:T, :], xv[:, HT:T, :]).then_inc(x_loaded[1], 16)
            full = INTER // P
            for w, src in ((gw, gw_in), (uw, uw_in)):
                sp.dma_start(w[:, :, :], src.rearrange("(k p) n -> p k n", p=P)).then_inc(ffn_loaded, 16)
            for v, src in ((gs, gs_in), (us, us_in)):
                sp.dma_start(v[:, :], src).then_inc(ffn_loaded, 16)
            sp.dma_start(dw[:, 0:full, :], dw_in[0:full * P, :].rearrange("(k p) n -> p k n", p=P))\
              .then_inc(ffn_loaded, 16)
            sp.dma_start(dw[0:INTER - full * P, full, :], dw_in[full * P:INTER, :]).then_inc(ffn_loaded, 16)
            sp.dma_start(dsr[:, :], rows(ds_in)).then_inc(ffn_loaded, 16)
            sp.dma_start(rg[:, :, :], rg_in.rearrange("(k p) n -> p k n", p=P)).then_inc(router_loaded, 16)
            def load_expert(e):
                for w, src in ((e1, e1_in), (e3, e3_in), (e2, e2_in)):
                    sp.dma_start(w[:, e * 1024:(e + 1) * 1024], src[e]).then_inc(experts_loaded, 16)

            for e in range(5):
                load_expert(e)
            sp.wait_ge(graph_over, 2)
            load_expert(7)
            for h in range(2):
                if h == 1:
                    sp.wait_ge(down_done, 2)
                    load_expert(5)
                    load_expert(6)
                sp.wait_ge(x3_ready, h + 1)
                sp.dma_start(out.rearrange("(t p) c -> p t c", p=P)[:, h * HT:(h + 1) * HT, :],
                             xr[:, h * HT:(h + 1) * HT, :]).then_inc(out_stored, 16)
                sp.wait_ge(xn_ready, XT["moe", h] + 1)
                sp.dma_start(xn3_dram.rearrange("(t p) c -> p t c", p=P)[:, h * HT:(h + 1) * HT, :],
                             xn[:, :, :]).then_inc(rows_stored, 16)
            sp.wait_ge(out_stored, 32)
            sp.wait_ge(rows_stored, 32)

        @block.gpsimd
        def _(pool):
            done = [0]

            def own(ins):
                done[0] += 1
                ins.then_inc(pool_done, 1)
                pool.wait_ge(pool_done, done[0])

            pool.memset(ones[:, :], 1.0).then_inc(consts, 1)
            pool.memset(nhalf[:, :], -0.5).then_inc(consts, 1)
            pool.memset(one8[:, :], 1.0).then_inc(consts, 1)
            own(pool.memset(ident[:, :], 0.0))
            pool.affine_select(out=ident[:, :], in_=ident[:, :], compare_op=ALU.not_equal, fill=1.0,
                               base=0, pattern=[[-1, P]], channel_multiplier=1).then_inc(consts, 1)
            own(pool.memset(before[:, :], 1.0))
            pool.affine_select(out=before[:, :], in_=before[:, :], compare_op=ALU.is_gt, fill=0.0,
                               base=0, pattern=[[1, P]], channel_multiplier=-1).then_inc(consts, 1)
            small = dict(allow_small_or_imprecise_dtypes=True)
            pool.iota(iota_p[:, :], [[1, P]], base=0, channel_multiplier=0, **small).then_inc(consts, 1)
            pool.iota(iota_e[:, :], [[1, E]], base=0, channel_multiplier=0, **small).then_inc(consts, 1)
            pool.iota(iota_q[:, :], [[P, E]], base=0, channel_multiplier=0, **small).then_inc(consts, 1)
            pool.iota(iota_b[:, :], [[1, NL]], base=0, channel_multiplier=0, **small).then_inc(consts, 1)
            pool.iota(token[:, :], [[0, 2], [P, T]], base=0, channel_multiplier=1, **small).then_inc(consts, 1)
            pool.wait_ge(consts, CONSTS)
            for n in range(8):
                pool.wait_ge(var_ready, n + 1)
                pool.tensor_tensor(rstd[:, :], veps[:, :], nhalf[:, :], ALU.pow).then_inc(rstd_ready, 1)

            def gather(j, q):
                pool.tensor_copy(gidx[q][:, :], idsu[:, bass.ds(j, 1)]).then_inc(gidx_set, 1)
                pool.wait_ge(gidx_set, j + 1)
                pool.sem_inc(pool_passed)
                pool.indirect_dma_start(
                    out=xg[q], out_offset=None, in_=xn3_dram,
                    in_offset=bass.IndirectOffsetOnAxis(ap=gidx[q][:, 0:1], axis=0),
                    bounds_check=bound, oob_is_err=False).then_inc(gathered[q], 16)

            def scatter(j, q):
                pool.tensor_copy(sidx[q][:, :], idsu[:, bass.ds(j, 1)]).then_inc(sidx_set, 1)
                pool.wait_ge(sidx_set, j + 1)
                pool.wait_ge(y_scaled, j + 1)
                pool.sem_inc(pool_passed)
                pool.indirect_dma_start(
                    out=out, out_offset=bass.IndirectOffsetOnAxis(ap=sidx[q][:, 0:1], axis=0),
                    in_=yv[q], in_offset=None,
                    bounds_check=bound, oob_is_err=False, compute_op=ALU.add).then_inc(scattered[q], 16)

            bound = pool.to_reg(B * N - 1)
            pool.wait_ge(list_ready, 1)
            pool.wait_ge(rows_stored, 32)
            pool.wait_ge(out_stored, 32)
            gather(0, 0)
            gather(1, 1)
            pool.wait_ge(xgT_done, 1)
            pool.wait_ge(gathered[0], 16)
            gather(2, 0)

            def pair(i, first=False):
                j = i * 2 + 1
                pool.wait_ge(xgT_done, j + 1)
                pool.wait_ge(gathered[1], i * 16 + 16)
                gather(j + 2, 1)
                if not first:
                    pool.wait_ge(scattered[1], i * 16)
                scatter(j - 1, 0)
                pool.wait_ge(xgT_done, j + 2)
                pool.wait_ge(gathered[0], i * 16 + 32)
                gather(j + 3, 0)
                pool.wait_ge(scattered[0], i * 16 + 16)
                scatter(j, 1)

            pair(0, first=True)
            with pool.Fori(1, PAIRS) as i:
                pair(i)
            pool.wait_ge(scattered[1], 16 * PAIRS)
            scatter(NB - 1, 0)
            pool.wait_ge(scattered[0], 16 * (PAIRS + 1))
            pool.wait_ge(gathered[0], 16 * (PAIRS + 2))

        @block.scalar
        def _(act):
            copy = ACT.Copy

            def sims(h):
                for q in range(2):
                    act.wait_ge(qk_done, q + 1)
                    act.activation(qk[0:D, q * 512:(q + 1) * 512].rearrange("p (a n) -> p a n", a=1),
                                   PS[0:D, q:q + 1, :], copy).then_inc(qk_copied, 1)
                for q in range(2):
                    act.wait_ge(qk_done, q + 3)
                    act.activation(zb[0:D, q * 512:(q + 1) * 512], PS[0:D, 2 + q, :], copy).then_inc(qk_copied, 1)
                for q in range(4):
                    act.wait_ge(sim_done, q + 1)
                    act.activation(sim[:, 2 * q:2 * q + 2, :], PS[:, q, :].rearrange("p (a n) -> p a n", a=2),
                                   copy, scale=1.0 / 16.0).then_inc(sim_copied, 1)
                act.wait_ge(sim_copied, 4)
                act.activation(a2[:, :, :], sim[:, :, :], ACT.Tanh, scale=0.5).then_inc(sig_ready, 1)
                act.wait_ge(st0_done, 1)
                act.activation(st0[:, :, :], PS[:, 4, 0:T * 2 * H].rearrange("p (t n) -> p t n", t=T),
                               copy).then_inc(st0_copied, 1)

            def graph_hot(h):
                if h == 0:
                    act.wait_ge(gat_loaded, 16 * 11)
                    act.activation(tg[:, 0:4], gates[:, 0:4], ACT.Tanh).then_inc(act_done, 1)
                    act.wait_ge(act_done, 1)
                    act.activation(tg[:, 4:5], gates[:, 4:5], ACT.Tanh, scale=0.5).then_inc(gates_tanh, 1)
                for b in range(2):
                    act.wait_ge(hotT_done, 2 * h + b + 1)
                    if h == 1:
                        act.wait_ge(out1_done, 1)
                    act.activation(hotT[:, b, :, :], PS[:, 6 + b, :].rearrange("p (m n) -> p m n", m=2),
                                   copy).then_inc(hotT_copied, 1)

            def graph_first(h):
                act.wait_ge(g0_done, h + 1)
                if h == 1:
                    act.wait_ge(h0_done, 1)
                act.activation(g0T[:, :], PS[0:D, 6, :], copy).then_inc(g0_copied, 1)

            def graph_hidden(h):
                act.wait_ge(h0_min, h + 1)
                act.activation(zb[:, :], za[:, :], ACT.Exp).then_inc(h0_exp, 1)

            def graph_feat(h):
                for i in range(HT):
                    act.wait_ge(feat_done, HT * h + i + 1)
                    if h == 1:
                        act.wait_ge(out1_done, 1)
                        act.wait_ge(good_ready, 1)
                    act.activation(feat[:, i, :], PS[:, 6 + i % 2, 0:WX], copy).then_inc(feat_copied, 1)

            def graph_out(h):
                act.wait_ge(out1_min, h + 1)
                act.activation(zb[:, :], za[:, :], ACT.Exp).then_inc(out1_exp, 1)

            def general_path(h):
                sem_g = general[h]
                with act.Fori(0, 2) as b:
                    start = b * BATCH_STEPS + 1
                    for at in (PRE_STEPS, PRE_STEPS + H * HEAD_STEPS + MID_STEPS):
                        with act.Fori(0, H) as hd:
                            act.wait_ge(sem_g, start + hd * HEAD_STEPS + (at + 6))
                            act.activation(gEa[:, 0, :], gEb[:, 0, :], ACT.Exp, bias=gnm[:, 0:1],
                                           accum_out=gsum[:, 0:1])
                            act.activation(gEa[:, 1, :], gEb[:, 1, :], ACT.Exp, bias=gnm[:, 1:2],
                                           accum_out=gsum[:, 1:2]).then_inc(sem_g, 1)
                        if at == PRE_STEPS:
                            act.wait_ge(sem_g, start + (at + H * HEAD_STEPS + 2))
                        else:
                            act.wait_ge(sem_g, start + (at + H * HEAD_STEPS + 2))
                        act.activation(gEb[:, :, :], gEa[:, :, :], ACT.Exp).then_inc(sem_g, 1)
                act.wait_ge(sem_g, 1 + 2 * BATCH_STEPS)

            def graph_check(h):
                act.wait_ge(flag_ready, h + 1)
                r = act.value_load(flag[0:1, h:h + 1], min_val=0, max_val=1)
                with act.If(r):
                    general_path(h)

            def transposed(n):
                act.wait_ge(xnT_done, n + 1)
                if n >= 2:
                    act.wait_ge(ffn_u_done, IT * (n - 1))
                act.activation(xnT[:, n % 2, :, :], PS[:, 6:8, :], copy).then_inc(xnT_copied, 1)

            def ffn_norm(h):
                transposed(XT["ffn", h])

            def ffn_up(h, it):
                n = h * IT + it
                M = min(P, INTER - it * P)
                act.wait_ge(ffn_g_done, n + 1)
                if n == 0:
                    act.wait_ge(ffn_loaded, 16 * 7)
                    act.wait_ge(wx_ready, 2)
                if n >= 2:
                    act.wait_ge(ffn_h_ready, n - 1)
                act.activation(th[0:M, n % 2, :], PS[0:M, n % 2, :], ACT.Tanh,
                               scale=hgs[0:M, it:it + 1]).then_inc(ffn_tanh, 1)

            def router(h):
                transposed(XT["moe", h])

            steps = dict(sims=sims, graph_hot=graph_hot, graph_first=graph_first, graph_hidden=graph_hidden,
                         graph_feat=graph_feat, graph_out=graph_out, graph_check=graph_check,
                         ffn_norm=ffn_norm, ffn_up=ffn_up, router=router)
            for name, *at in SCHEDULE:
                if name in steps:
                    steps[name](*at)
            act.wait_ge(d_ready, 1)
            act.activation(Ek[:, :, :, :].rearrange("p k t e -> p (k t e)"),
                           Dk[:, :, :, :].rearrange("p k t e -> p (k t e)"), ACT.Exp, scale=-1.0)\
               .then_inc(ek_ready, 1)

            def copy_xgT(j, q):
                act.wait_ge(xgT_done, j + 1)
                act.activation(xgT[q], PS[:, 4, q * 256:(q + 1) * 256].rearrange("p (k n) -> p k n", k=2),
                               copy).then_inc(xgT_copied, 1)

            def silu(j, q):
                act.wait_ge(up1_done, j + 1)
                act.activation(th[:, q, :], PS[:, q, :], ACT.Tanh, scale=0.5).then_inc(silu_tanh, 1)

            def copy_hhT(j, q):
                act.wait_ge(hhT_done, j + 1)
                act.activation(hhT[q], PS[:, 5, :], copy).then_inc(hhT_copied, 1)

            def scale_y(j, q):
                act.wait_ge(y_done, j + 1)
                act.activation(yv[q], PS[:, 6 + q, 0:C], copy,
                               scale=coef[:, bass.ds(j, 1)]).then_inc(y_scaled, 1)

            copy_xgT(0, 0)
            silu(0, 0)
            copy_xgT(1, 1)

            def pair(i, first=False):
                for q in range(2):
                    j = i * 2 + (1 + q)
                    me, other = (q + 1) % 2, q
                    if q or not first:
                        act.wait_ge(gated, j - 1)
                    silu(j, me)
                    copy_hhT(j - 1, other)
                    act.wait_ge(up3_done, j)
                    copy_xgT(j + 1, other)
                    if not first:
                        act.wait_ge(scattered[other], i * 16)
                    scale_y(j - 1, other)

            pair(0, first=True)
            with act.Fori(1, PAIRS) as i:
                pair(i)
            copy_hhT(NB - 1, 0)
            act.wait_ge(scattered[0], 16 * PAIRS)
            scale_y(NB - 1, 0)

        @block.vector
        def _(dve):
            done = [0]

            def own(ins):
                done[0] += 1
                ins.then_inc(dve_done, 1)
                dve.wait_ge(dve_done, done[0])

            def stats(src, n):
                for i in range(HT):
                    own(dve.bn_stats(stat[:, i, :], src[:, i, :]))
                    own(dve.bn_aggr(mv[:, i, :], stat[:, i, :]))
                dve.tensor_scalar(veps[:, :], mv[:, :, 1], EPS, None, ALU.add).then_inc(var_ready, 1)
                dve.wait_ge(rstd_ready, n + 1)

            def half(t, h):
                return t[:, h * HT:(h + 1) * HT, :]

            def top_rows(t):
                src = sim[:, t, :]
                for r in range(ROUNDS):
                    own(dve.max(out=t8[:, :], in_=src))
                    if r < ROUNDS - 1:
                        own(dve.match_replace(out=work[:, :], in_to_replace=t8[:, :], in_values=src,
                                              imm_value=-3.4e38))
                        src = work[:, :]
                k = (TOPK - 1) % 8
                own(dve.scalar_tensor_tensor(out=a2[:, t, :], in0=sim[:, t, :], scalar=t8[:, k:k + 1],
                                             in1=a2[:, t, :], op0=ALU.is_ge, op1=ALU.mult))

            def graph_hot(h):
                if h == 0:
                    dve.wait_ge(consts, CONSTS)
                dve.wait_ge(x_loaded[h], 16)
                stats(half(x, h), LN["graph", h])
                for i in range(HT):
                    own(dve.tensor_scalar(za[:, i * C:(i + 1) * C], x[:, h * HT + i, :], mv[:, i, 0:1],
                                          rstd[:, i:i + 1], ALU.subtract, ALU.mult))
                own(dve.tensor_scalar(mask[:, :, :].rearrange("p a b -> p (a b)"), za[:, :], 1.0, BIG,
                                      ALU.subtract, ALU.mult))
                for i in range(HT):
                    own(dve.max(out=top[:, i, :], in_=mask[:, i, :]))
                if h == 1:
                    dve.wait_ge(hotT_done, 2)
                for i in range(HT):
                    ins = dve.tensor_scalar(hot[:, i, :], mask[:, i, :], top[:, i, 0:1], None, ALU.is_ge)
                    ins.then_inc(hot_ready, 1)
                own(dve.scalar_tensor_tensor(out=good[:, 4:8], in0=top[:, :, 0], scalar=-1.0,
                                             in1=top[:, :, 0], op0=ALU.mult, op1=ALU.max))
                own(dve.tensor_scalar(good[:, 8:12], good[:, 4:8], ULPS, LEAD, ALU.mult, ALU.add))
                own(dve.tensor_tensor(good[:, 4:8], top[:, :, 0], top[:, :, 1], ALU.subtract))
                own(dve.tensor_tensor(good[:, 0:4], good[:, 4:8], good[:, 8:12], ALU.is_gt))
                if h == 0:
                    setup()

            def setup():
                dve.wait_ge(gat_loaded, 16 * 11)
                HF = H * FO
                for n in range(2):
                    own(dve.tensor_tensor(wbuf[0:D, 0, 0:HF], w0x[:, 0:HF], avec[0:D, n, :], ALU.mult))
                    own(dve.tensor_reduce(w0x[:, HF + n * H:HF + (n + 1) * H],
                                          wbuf[0:D, 0, 0:HF].rearrange("p (h o) -> p h o", h=H), AX.X, ALU.add))
                for n in range(2):
                    for k in range(2):
                        own(dve.tensor_tensor(wbuf[:, 0, 0:HF], w1x[:, k, 0:HF], avec[:, 2 + n, :], ALU.mult))
                        own(dve.tensor_reduce(w1x[:, k, HF + n * H:HF + (n + 1) * H],
                                              wbuf[:, 0, 0:HF].rearrange("p (h o) -> p h o", h=H), AX.X, ALU.add))
                dve.wait_ge(gates_tanh, 1)
                own(dve.tensor_scalar(cc[:, 0:1], tg[:, 4:5], 0.5, 0.5, ALU.mult, ALU.add))
                own(dve.tensor_scalar(cc[:, 1:2], cc[:, 0:1], -1.0, 1.0, ALU.mult, ALU.add))
                own(dve.tensor_tensor(cc[:, 2:3], cc[:, 1:2], tg[:, 1:2], ALU.mult))
                own(dve.tensor_scalar(cc[:, 3:4], cc[:, 0:1], tg[:, 1:2], 0.25, ALU.mult, ALU.mult))
                dve.memset(good[:, 0:0 + 1], 1.0).then_inc(wx_ready, 1) if False else \
                    dve.tensor_copy(wbuf[:, 0, 0:1], cc[:, 3:4]).then_inc(wx_ready, 1)

            def setup_ffn():
                dve.wait_ge(ffn_loaded, 16 * 7)
                own(dve.tensor_scalar(hgs[:, :], gs[:, :], 0.5, None, ALU.mult))
                own(dve.tensor_tensor(cgu[:, :], hgs[:, :], us[:, :], ALU.mult))
                dve.tensor_scalar(dsr[:, :], dsr[:, :], tg[:, 2:3], None, ALU.mult).then_inc(wx_ready, 1)

            def sims(h):
                dve.wait_ge(sig_ready, 1)
                own(dve.tensor_scalar(a2[:, :, :], a2[:, :, :], 1.0, None, ALU.add))
                top_rows(0)
                setup_ffn()

            def graph_hidden(h):
                dve.wait_ge(h0_done, h + 1)
                for k in range(2):
                    ins = dve.tensor_scalar(za[:, k * HN:(k + 1) * HN], PS[:, 6 + k, :], b0[:, k:k + 1], 0.0,
                                            ALU.add, ALU.min)
                ins.then_inc(h0_min, 1)
                dve.wait_ge(h0_exp, h + 1)
                own(dve.tensor_scalar(za[:, :], zb[:, :], -1.0, None, ALU.add))
                if h == 1:
                    dve.wait_ge(feat_done, HT)
                for k in range(2):
                    ins = dve.scalar_tensor_tensor(out=h0T[:, k, :], in0=PS[:, 6 + k, :], scalar=b0[:, k:k + 1],
                                                   in1=za[:, k * HN:(k + 1) * HN], op0=ALU.add, op1=ALU.max)
                ins.then_inc(h0_ready, 1)
                top_rows(1 + 2 * h)

            def graph_feat(h):
                dve.wait_ge(feat_copied, HT * (h + 1))
                dve.wait_ge(st0_copied, 1)
                n = HT * 2 * H
                own(dve.scalar_tensor_tensor(out=gsm[:, 0:n].rearrange("p (t n) -> p t n", t=HT),
                                             in0=half(st0, h), scalar=-1.0, in1=half(st0, h),
                                             op0=ALU.mult, op1=ALU.max))
                own(dve.scalar_tensor_tensor(out=gsm[:, n:2 * n].rearrange("p (t n) -> p t n", t=HT),
                                             in0=feat[:, :, H * FO:WX], scalar=-1.0, in1=feat[:, :, H * FO:WX],
                                             op0=ALU.mult, op1=ALU.max))
                own(dve.tensor_scalar(good[:, HT:HT + 2 * n], gsm[:, :], LOGIT, None, ALU.is_le))
                own(dve.tensor_reduce(gmin[:, 0:1], good[:, :], AX.X, ALU.min))
                dve.tensor_scalar(gmin[:, 1:2], gmin[:, 0:1], -1.0, 1.0 if not force_general else 2.0,
                                  ALU.mult, ALU.add).then_inc(good_ready, 1)

            def graph_out(h):
                dve.wait_ge(out1_done, h + 1)
                z3 = zc[:, :].rearrange("p (t c) -> p t c", t=HT)
                dve.tensor_tensor(z3, PS[:, 6:8, :].rearrange("p b (t c) -> p (b t) c", t=2),
                                  b1[:, :].unsqueeze(1).to_broadcast([P, HT, C]), ALU.add).then_inc(out1_read, 1)
                dve.wait_ge(out1_read, h + 1)
                dve.tensor_scalar(za[:, :], zc[:, :], 0.0, None, ALU.min).then_inc(out1_min, 1)
                dve.wait_ge(out1_exp, h + 1)
                own(dve.scalar_tensor_tensor(out=za[:, :], in0=zb[:, :], scalar=-1.0, in1=zc[:, :],
                                             op0=ALU.add, op1=ALU.max))

            def add_graph(h):
                xh = half(xr, h).rearrange("p t c -> p (t c)")
                dve.scalar_tensor_tensor(out=xh, in0=za[:, :], scalar=tg[:, 0:1], in1=xh,
                                         op0=ALU.mult, op1=ALU.add).then_inc(graph_over, 1)
                dve.wait_ge(graph_over, h + 1)

            def general_path(h):
                g = general[h]
                dve.memset(gnm[:, :], 0.0).then_inc(g, 1)

                def step(at, ins):
                    ins.then_inc(g, 1)

                def heads(start, at, b):
                    with dve.Fori(0, H) as hd:
                        k = start + hd * HEAD_STEPS + at
                        dve.wait_ge(g, k)
                        for m in range(2):
                            ins = dve.tensor_scalar(gD[:, m, :], ident[:, :],
                                                    gfeat[:, m, bass.ds(hd + (H * FO + H), 1)], None, ALU.mult)
                        ins.then_inc(g, 1)
                        dve.wait_ge(g, k + 2)
                        for m in range(2):
                            ins = dve.tensor_scalar(gEa[:, m, :], PS[:, 6, 0:N],
                                                    gfeat[:, m, bass.ds(hd + H * FO, 1)], None, ALU.add)
                        ins.then_inc(g, 1)
                        dve.wait_ge(g, k + 3)
                        dve.scalar_tensor_tensor(out=gEb[:, :, :], in0=gEa[:, :, :], scalar=0.2, in1=gEa[:, :, :],
                                                 op0=ALU.mult, op1=ALU.max).then_inc(g, 1)
                        dve.wait_ge(g, k + 4)
                        dve.tensor_tensor(gEb[:, :, :].rearrange("p a b -> p (a b)"),
                                          gEb[:, :, :].rearrange("p a b -> p (a b)"),
                                          mask[:, :, :].rearrange("p a b -> p (a b)")[:, bass.ds(b * (2 * N), 2 * N)],
                                          ALU.add).then_inc(g, 1)
                        dve.wait_ge(g, k + 5)
                        dve.tensor_reduce(gnm[:, :], gEb[:, :, :], AX.X, ALU.max, negate=True).then_inc(g, 1)
                        dve.wait_ge(g, k + 7)
                        dve.reciprocal(grs[:, :], gsum[:, :]).then_inc(g, 1)
                        dve.wait_ge(g, k + 9)
                        dve.tensor_copy(gEb[:, :, :], PS[:, 7, :].rearrange("p (a b) -> p a b", a=2)).then_inc(g, 1)
                        dve.wait_ge(g, k + 11)
                        for m in range(2):
                            ins = dve.tensor_scalar(gout[:, m, bass.ds(hd * FO, FO)],
                                                    PS[:, 6, m * FO:(m + 1) * FO], grs[:, m:m + 1], None, ALU.mult)
                        ins.then_inc(g, 1)

                with dve.Fori(0, 2) as b:
                    start = b * BATCH_STEPS + 1
                    dve.wait_ge(g, start)
                    dve.tensor_copy(gctxT[:, :], ctxT[:, bass.ds(b * N + h * HN, N)]).then_inc(g, 1)
                    dve.wait_ge(g, start + 2)
                    dve.tensor_copy(gfeat[:, :, :], PS[:, 6:8, 0:WX]).then_inc(g, 1)
                    heads(start, PRE_STEPS, b)
                    k = start + (PRE_STEPS + H * HEAD_STEPS)
                    dve.wait_ge(g, k + 1)
                    for m in range(2):
                        ins = dve.tensor_scalar(gEa[:, m, :], PS[:, 6, m * N:(m + 1) * N], b0[:, m:m + 1], 0.0,
                                                ALU.add, ALU.min)
                    ins.then_inc(g, 1)
                    dve.wait_ge(g, k + 3)
                    dve.tensor_scalar(gEa[:, :, :], gEb[:, :, :], -1.0, None, ALU.add).then_inc(g, 1)
                    dve.wait_ge(g, k + 4)
                    for m in range(2):
                        ins = dve.scalar_tensor_tensor(out=gout[:, m, :], in0=PS[:, 6, m * N:(m + 1) * N],
                                                       scalar=b0[:, m:m + 1], in1=gEa[:, m, :],
                                                       op0=ALU.add, op1=ALU.max)
                    ins.then_inc(g, 1)
                    dve.wait_ge(g, k + 6)
                    dve.tensor_copy(gfeat[:, :, :], PS[:, 6:8, 0:WX]).then_inc(g, 1)
                    heads(start, PRE_STEPS + H * HEAD_STEPS + MID_STEPS, b)
                    k = start + (PRE_STEPS + 2 * H * HEAD_STEPS + MID_STEPS)
                    dve.wait_ge(g, k)
                    dve.tensor_tensor(gout[:, :, :], gout[:, :, :], b1[:, :].unsqueeze(1).to_broadcast([P, 2, C]),
                                      ALU.add).then_inc(g, 1)
                    dve.wait_ge(g, k + 1)
                    dve.tensor_scalar(gEa[:, :, :], gout[:, :, :], 0.0, None, ALU.min).then_inc(g, 1)
                    dve.wait_ge(g, k + 3)
                    dve.tensor_scalar(gEa[:, :, :], gEb[:, :, :], -1.0, None, ALU.add).then_inc(g, 1)
                    dve.wait_ge(g, k + 4)
                    dve.tensor_tensor(za[:, bass.ds(b * (2 * C), 2 * C)].rearrange("p (a c) -> p a c", a=2),
                                      gEa[:, :, :], gout[:, :, :], ALU.max).then_inc(g, 1)
                dve.wait_ge(g, 1 + 2 * BATCH_STEPS)

            def graph_check(h):
                dve.wait_ge(bad_counted, h + 1)
                dve.tensor_scalar(flag[:, h:h + 1], PS[:, 6, 0:1], 1.0, None, ALU.min).then_inc(flag_ready, 1)
                dve.wait_ge(flag_ready, h + 1)
                r = dve.value_load(flag[0:1, h:h + 1], min_val=0, max_val=1)
                with dve.If(r):
                    general_path(h)
                add_graph(h)

            def normalise(h, n, scale=None):
                stats(half(xr, h), n)
                r = rstd
                if scale is not None:
                    own(dve.tensor_scalar(veps[:, :], rstd[:, :], scale, None, ALU.mult))
                    r = veps
                for i in range(HT):
                    ins = dve.tensor_scalar(xn[:, i, :], xr[:, h * HT + i, :], mv[:, i, 0:1], r[:, i:i + 1],
                                            ALU.subtract, ALU.mult)
                    if i < HT - 1 or scale is not None:
                        own(ins)
                return ins

            def ffn_norm(h):
                if h == 1:
                    dve.wait_ge(xnT_done, 1)
                normalise(h, LN["ffn", h]).then_inc(xn_ready, 1)
                top_rows(4 * h + 2 - 2 * h) if h == 0 else None

            def ffn_up(h, it):
                n = h * IT + it
                M = min(P, INTER - it * P)
                dve.wait_ge(ffn_tanh, n + 1)
                own(dve.scalar_tensor_tensor(out=wbuf[0:M, n % 2, :], in0=th[0:M, n % 2, :], scalar=1.0,
                                             in1=PS[0:M, n % 2, :], op0=ALU.add, op1=ALU.mult))
                dve.wait_ge(ffn_u_done, n + 1)
                if h == 1:
                    dve.wait_ge(down_done, 1)
                dve.scalar_tensor_tensor(out=hT[0:M, it, :], in0=wbuf[0:M, n % 2, :], scalar=cgu[0:M, it:it + 1],
                                         in1=PS[0:M, 2 + n % 2, :], op0=ALU.mult, op1=ALU.mult)\
                   .then_inc(ffn_h_ready, 1)
                if h == 1 and it < 4:
                    top_rows(4 + it)

            def ffn_down(h):
                dve.wait_ge(down_done, h + 1)
                dve.tensor_tensor(za[:, :].rearrange("p (t c) -> p t c", t=HT),
                                  PS[:, 4:6, :].rearrange("p b (t c) -> p (b t) c", t=2),
                                  dsr[:, :].unsqueeze(1).to_broadcast([P, HT, C]), ALU.mult).then_inc(down_read, 1)
                dve.wait_ge(down_read, h + 1)
                own(dve.tensor_tensor(half(xr, h).rearrange("p t c -> p (t c)"),
                                      half(xr, h).rearrange("p t c -> p (t c)"), za[:, :], ALU.add))

            def attn(h):
                dve.tensor_copy(wbuf[:, 0, 0:1], cc[:, 3:4]).then_inc(a2_ready, 1)
                dve.wait_ge(a2_ready, h + 1)
                if h == 1:
                    dve.wait_ge(rows_stored, 16)
                    dve.wait_ge(xnT_done, XT["moe", 0] + 1)
                else:
                    dve.wait_ge(xnT_done, 2)
                normalise(h, LN["attn", h], scale=cc[:, 2:3])
                xh = half(xr, h).rearrange("p t c -> p (t c)")
                own(dve.tensor_tensor(xh, xh, xn[:, :, :].rearrange("p t c -> p (t c)"), ALU.add))
                dve.wait_ge(a2T_done, h + 1)
                own(dve.tensor_tensor(za[:, :], half(a2, h).rearrange("p t c -> p (t c)"),
                                      PS[:, 6:8, :].rearrange("p b c -> p (b c)"), ALU.add))
                dve.scalar_tensor_tensor(out=xh, in0=za[:, :], scalar=cc[:, 3:4], in1=xh,
                                         op0=ALU.mult, op1=ALU.add).then_inc(x3_ready, 1)
                dve.wait_ge(x3_ready, h + 1)

            def router(h):
                normalise(h, LN["moe", h]).then_inc(xn_ready, 1)
                dve.wait_ge(scores_done, h + 1)
                dve.tensor_copy(half(sc, h), PS[:, 6, 0:HT * E].rearrange("p (t e) -> p t e", t=HT))\
                   .then_inc(scores_read, 1)
                dve.wait_ge(scores_read, h + 1)
                for t in range(h * HT, (h + 1) * HT):
                    own(dve.max(out=mx8[:, t, :], in_=sc[:, t, :]))
                    own(dve.max_index(out=ix8[:, t, :], in_max=mx8[:, t, :], in_values=sc[:, t, :]))

            steps = dict(sims=sims, graph_hot=graph_hot, graph_hidden=graph_hidden,
                         graph_feat=graph_feat, graph_out=graph_out, graph_check=graph_check,
                         ffn_norm=ffn_norm, ffn_up=ffn_up, ffn_down=ffn_down, attn=attn, router=router)
            for name, *at in SCHEDULE:
                if name in steps:
                    steps[name](*at)

            own(dve.tensor_copy(idxf[:, :, :], ix8[:, :, 0:2]))
            kt = lambda ap: ap.rearrange("p t k -> p k t").unsqueeze(3).to_broadcast([P, 2, T, E])
            ee = iota_e[:, :].unsqueeze(1).to_broadcast([P, T, E])
            for k in range(2):
                own(dve.tensor_tensor(O[:, k], ee, idxf[:, :, k].unsqueeze(2).to_broadcast([P, T, E]), ALU.is_equal))
            dve.tensor_tensor(Os[:, :, :], O[:, 0], O[:, 1], ALU.add).then_inc(onehots_ready, 1)
            for k in range(2):
                own(dve.tensor_tensor(Dk[:, k], mx8[:, :, k].unsqueeze(2).to_broadcast([P, T, E]), sc[:, :, :],
                                      ALU.subtract))
            own(dve.tensor_scalar(Dk[:, :, :, :].rearrange("p k t e -> p (k t e)"),
                                  Dk[:, :, :, :].rearrange("p k t e -> p (k t e)"), 0.0, None, ALU.max))
            dve.tensor_copy(t8[:, 0:1], Dk[:, 0, 0, 0:1]).then_inc(d_ready, 1)
            own(dve.scalar_tensor_tensor(out=ab[:, :, :], in0=sc[:, :, :], scalar=-1.0, in1=sc[:, :, :],
                                         op0=ALU.mult, op1=ALU.max))
            for k in range(2):
                own(dve.tensor_tensor(Fk[:, k], mx8[:, :, k].unsqueeze(2).to_broadcast([P, T, E]), ab[:, :, :],
                                      ALU.max))
            flat4 = lambda a: a[:, :, :, :].rearrange("p k t e -> p (k t e)")
            own(dve.scalar_tensor_tensor(out=flat4(Fk), in0=flat4(Fk), scalar=0.02, in1=flat4(Dk),
                                         op0=ALU.mult, op1=ALU.is_ge))
            own(dve.scalar_tensor_tensor(out=Fk[:, 1], in0=O[:, 0], scalar=0.5, in1=Fk[:, 1],
                                         op0=ALU.is_lt, op1=ALU.mult))
            dve.wait_ge(ek_ready, 1)
            own(dve.tensor_tensor(flat4(Ek), flat4(Ek), flat4(Fk), ALU.mult))
            own(dve.tensor_reduce(mk[:, :], Ek[:, :, :, :].rearrange("p k t e -> p (k t) e"), AX.X, ALU.add))
            own(dve.reciprocal(mk[:, :], mk[:, :]))
            own(dve.tensor_scalar(mk[:, :], mk[:, :], tg[:, 3:4], 0.5, ALU.mult, ALU.mult))
            dve.wait_ge(count_done, 1)
            own(dve.tensor_tensor(nb[:, :, :], PS[:, 4, 0:E].unsqueeze(2).to_broadcast([P, E, E]),
                                  iota_q[:, :].unsqueeze(1).to_broadcast([P, E, E]), ALU.is_gt))
            own(dve.tensor_reduce(nblk[:, :], nb[:, :, :], AX.X, ALU.add))
            own(dve.tensor_tensor_scan(incl[:, :], one8[:, :], nblk[:, :], 0.0, ALU.mult, ALU.add))
            own(dve.tensor_tensor(base[:, :], incl[:, :], nblk[:, :], ALU.subtract))
            own(dve.tensor_scalar(base[:, :], base[:, :], float(P), None, ALU.mult))
            own(dve.tensor_tensor(ecmp[:, :, :], iota_b[:, :].unsqueeze(2).to_broadcast([P, NL, E]),
                                  incl[:, :].unsqueeze(1).to_broadcast([P, NL, E]), ALU.is_ge))
            own(dve.tensor_reduce(eblk[:, :], ecmp[:, :, :], AX.X, ALU.add))
            dve.tensor_scalar(eoff[:, :], eblk[:, :], float(E - 1), 1024.0, ALU.min, ALU.mult).then_inc(eoff_ready, 1)
            dve.wait_ge(rank_done, 1)
            own(dve.tensor_tensor(rk[:, :, :], PS[:, 5, 0:T * E].rearrange("p (t e) -> p t e", t=T),
                                  base[:, :].unsqueeze(1).to_broadcast([P, T, E]), ALU.add))
            for k in range(2):
                own(dve.tensor_tensor(O[:, k], O[:, k], rk[:, :, :], ALU.mult))
            own(dve.tensor_reduce(slf[:, :], O[:, :, :, :].rearrange("p k t e -> p (k t) e"), AX.X, ALU.add))
            own(dve.tensor_copy(sli[:, :], slf[:, :]))
            own(dve.tensor_scalar(sji[:, :], sli[:, :], 7, None, ALU.logical_shift_right))
            own(dve.tensor_scalar(spi[:, :], sli[:, :], P - 1, None, ALU.bitwise_and))
            own(dve.tensor_copy(sjf[:, :], sji[:, :]))
            own(dve.tensor_copy(spf[:, :], spi[:, :]))
            own(dve.tensor_tensor(RH[:, :, 0:NL], iota_b[:, :].unsqueeze(1).to_broadcast([P, 2 * T, NL]),
                                  sjf[:, :].unsqueeze(2).to_broadcast([P, 2 * T, NL]), ALU.is_equal))
            for n, v in ((1, token), (2, mk)):
                ins = dve.tensor_tensor(RH[:, :, n * NL:(n + 1) * NL], RH[:, :, 0:NL],
                                        v[:, :].unsqueeze(2).to_broadcast([P, 2 * T, NL]), ALU.mult)
            ins.then_inc(rh_ready, 1)
            for n in range(2 * T):
                if n >= 2:
                    dve.wait_ge(ph_used, n - 1)
                dve.tensor_scalar(Ph[:, n % 2, :], iota_p[:, :], spf[:, n:n + 1], None, ALU.is_equal)\
                   .then_inc(ph_ready, 1)
            dve.wait_ge(list_done, 1)
            own(dve.tensor_copy(coef[:, :], PS[:, 6, 2 * NL:3 * NL]))
            own(dve.tensor_scalar(lst[:, :], PS[:, 6, 0:NL], float(-PAD), float(PAD), ALU.mult, ALU.add))
            dve.tensor_tensor(idsu[:, :], PS[:, 6, NL:2 * NL], lst[:, :], ALU.add).then_inc(list_ready, 1)

            def gate(j, me):
                dve.wait_ge(silu_tanh, j + 1)
                dve.scalar_tensor_tensor(out=wbuf[:, me, :], in0=th[:, me, :], scalar=1.0, in1=PS[:, me, :],
                                         op0=ALU.add, op1=ALU.mult).then_inc(w_ready, 1)
                dve.wait_ge(w_ready, j + 1)
                dve.wait_ge(up3_done, j + 1)
                dve.tensor_tensor(hh[me], wbuf[:, me, :], PS[:, 2 + me, :], ALU.mult).then_inc(gated, 1)

            gate(0, 0)

            def pair(i, first=False):
                for q in range(2):
                    j = i * 2 + (1 + q)
                    if q or not first:
                        dve.wait_ge(hhT_done, j - 1)
                    gate(j, (q + 1) % 2)

            pair(0, first=True)
            with dve.Fori(1, PAIRS) as i:
                pair(i)

        @block.tensor
        def _(pe):
            def sims(h):
                pe.wait_ge(qk_loaded, 48)
                for n, w in ((0, wq), (1, wk)):
                    for q in range(2):
                        pe.matmul(PS[0:D, 2 * n + q, :], w[:, :], ctxT[:, q * 512:(q + 1) * 512],
                                  start=True, stop=True).then_inc(qk_done, 1)
                pe.wait_ge(qk_copied, 4)
                for t in range(T):
                    b = t // 2
                    mm = pe.matmul(PS[:, t // 2, (t % 2) * N:(t % 2 + 1) * N], qk[0:D, t * P:(t + 1) * P],
                                   zb[0:D, b * N:(b + 1) * N], start=True, stop=True)
                    if t % 2:
                        mm.then_inc(sim_done, 1)
                pe.wait_ge(wx_ready, 1)
                for t in range(T):
                    mm = pe.matmul(PS[:, 4, t * 2 * H:(t + 1) * 2 * H], ctxT[:, t * P:(t + 1) * P],
                                   w0x[:, H * FO:WX], start=True, stop=True)
                mm.then_inc(st0_done, 1)

            def graph_hot(h):
                for b in range(2):
                    pe.wait_ge(hot_ready, HT * h + 2 * b + 2)
                    for m in range(2):
                        for n in range(2):
                            mm = pe.transpose(PS[:, 6 + b, m * 256 + n * P:m * 256 + (n + 1) * P],
                                              hot[:, 2 * b + n, m * P:(m + 1) * P], ident[:, :])
                    mm.then_inc(hotT_done, 1)

            def graph_first(h):
                pe.wait_ge(ctx_loaded, 16)
                pe.wait_ge(hotT_copied, 2 * h + 2)
                for b in range(2):
                    for m in range(2):
                        mm = pe.matmul(PS[0:D, 6, b * 256:(b + 1) * 256], ctx_s[:, h * HT + 2 * b + m, :],
                                       hotT[:, b, m, :], start=(m == 0), stop=(m == 1))
                mm.then_inc(g0_done, 1)

            def graph_hidden(h):
                pe.wait_ge(g0_copied, h + 1)
                for k in range(2):
                    mm = pe.matmul(PS[:, 6 + k, :], w0x[:, k * P:(k + 1) * P], g0T[:, :], start=True, stop=True)
                mm.then_inc(h0_done, 1)

            def graph_feat(h):
                pe.wait_ge(h0_ready, h + 1)
                pe.wait_ge(wx_ready, 1)
                for i in range(HT):
                    if i >= 2:
                        pe.wait_ge(feat_copied, HT * h + i - 1)
                    for k in range(2):
                        mm = pe.matmul(PS[:, 6 + i % 2, 0:WX], h0T[:, k, i * P:(i + 1) * P], w1x[:, k, :],
                                       start=(k == 0), stop=(k == 1))
                    mm.then_inc(feat_done, 1)

            def graph_out(h):
                pe.wait_ge(feat_copied, HT * (h + 1))
                for i in range(HT):
                    b, n = i // 2, i % 2
                    for m in range(2):
                        mm = pe.matmul(PS[:, 6 + b, n * 256:(n + 1) * 256], hotT[:, b, m, n * P:(n + 1) * P],
                                       feat[:, 2 * b + m, 0:H * FO], start=(m == 0), stop=(m == 1))
                mm.then_inc(out1_done, 1)

            def general_path(h):
                g = general[h]

                def heads(start, at):
                    with pe.Fori(0, H) as hd:
                        k = start + hd * HEAD_STEPS + at
                        pe.wait_ge(g, k + 1)
                        for m in range(2):
                            mm = pe.matmul(PS[:, 6, m * P:(m + 1) * P], ones[:, :], gD[:, m, :], start=True, stop=True)
                        mm.then_inc(g, 1)
                        pe.wait_ge(g, k + 8)
                        for m in range(2):
                            for n in range(2):
                                mm = pe.transpose(PS[:, 7, m * 256 + n * P:m * 256 + (n + 1) * P],
                                                  gEa[:, n, m * P:(m + 1) * P], ident[:, :])
                        mm.then_inc(g, 1)
                        pe.wait_ge(g, k + 10)
                        for n in range(2):
                            for m in range(2):
                                mm = pe.matmul(PS[:, 6, n * FO:(n + 1) * FO], gEb[:, m, n * P:(n + 1) * P],
                                               gfeat[:, m, bass.ds(hd * FO, FO)], start=(m == 0), stop=(m == 1))
                        mm.then_inc(g, 1)

                with pe.Fori(0, 2) as b:
                    start = b * BATCH_STEPS + 1
                    pe.wait_ge(g, start + 1)
                    for m in range(2):
                        mm = pe.matmul(PS[:, 6 + m, 0:WX], gctxT[:, m * P:(m + 1) * P], w0x[:, :],
                                       start=True, stop=True)
                    mm.then_inc(g, 1)
                    heads(start, PRE_STEPS)
                    k = start + (PRE_STEPS + H * HEAD_STEPS)
                    pe.wait_ge(g, k)
                    for m in range(2):
                        for n in range(2):
                            mm = pe.transpose(PS[:, 6, m * 256 + n * P:m * 256 + (n + 1) * P],
                                              gout[:, n, m * P:(m + 1) * P], ident[:, :])
                    mm.then_inc(g, 1)
                    pe.wait_ge(g, k + 5)
                    for m in range(2):
                        for kk in range(2):
                            mm = pe.matmul(PS[:, 6 + m, 0:WX], gout[:, kk, m * P:(m + 1) * P], w1x[:, kk, :],
                                           start=(kk == 0), stop=(kk == 1))
                    mm.then_inc(g, 1)
                    heads(start, PRE_STEPS + H * HEAD_STEPS + MID_STEPS)
                pe.wait_ge(g, 1 + 2 * BATCH_STEPS)

            def graph_check(h):
                pe.wait_ge(good_ready, h + 1)
                pe.wait_ge(out1_read, h + 1)
                pe.matmul(PS[:, 6, 0:1], ones[:, :], gmin[:, 1:2], start=True, stop=True).then_inc(bad_counted, 1)
                pe.wait_ge(flag_ready, h + 1)
                r = pe.value_load(flag[0:1, h:h + 1], min_val=0, max_val=1)
                with pe.If(r):
                    general_path(h)

            def turn_tokens(n):
                pe.wait_ge(xn_ready, n + 1)
                for i in range(HT):
                    for k in range(2):
                        mm = pe.transpose(PS[:, 6 + k, i * P:(i + 1) * P], xn[:, i, k * P:(k + 1) * P], ident[:, :])
                mm.then_inc(xnT_done, 1)

            def ffn_norm(h):
                turn_tokens(XT["ffn", h])
                pe.wait_ge(xnT_copied, XT["ffn", h] + 1)
                if h == 0:
                    pe.wait_ge(ffn_loaded, 16 * 7)
                    pe.wait_ge(sim_copied, 4)

            def ffn_up(h, it):
                n = h * IT + it
                M = min(P, INTER - it * P)
                if n >= 2:
                    pe.wait_ge(ffn_h_ready, n - 1)
                for w, bank, ready in ((gw, n % 2, ffn_g_done), (uw, 2 + n % 2, ffn_u_done)):
                    for k in range(2):
                        mm = pe.matmul(PS[0:M, bank, :], w[:, k, it * P:it * P + M], xnT[:, h, k, :],
                                       start=(k == 0), stop=(k == 1))
                    mm.then_inc(ready, 1)

            def ffn_down(h):
                pe.wait_ge(ffn_h_ready, IT * (h + 1))
                if h == 0:
                    pe.wait_ge(st0_copied, 1)
                else:
                    pe.wait_ge(down_read, 1)
                for i in range(HT):
                    for it in range(IT):
                        K = min(P, INTER - it * P)
                        mm = pe.matmul(PS[:, 4 + i // 2, (i % 2) * 256:(i % 2 + 1) * 256],
                                       hT[0:K, it, i * P:(i + 1) * P], dw[0:K, it, :],
                                       start=(it == 0), stop=(it == IT - 1))
                mm.then_inc(down_done, 1)

            def attn(h):
                pe.wait_ge(a2_ready, h + 1)
                for b in range(2):
                    for m in range(2):
                        for n in range(2):
                            mm = pe.transpose(PS[:, 6 + b, m * 256 + n * P:m * 256 + (n + 1) * P],
                                              a2[:, h * HT + 2 * b + n, m * P:(m + 1) * P], ident[:, :])
                mm.then_inc(a2T_done, 1)

            def router(h):
                turn_tokens(XT["moe", h])
                pe.wait_ge(xnT_copied, XT["moe", h] + 1)
                pe.wait_ge(router_loaded, 16)
                for i in range(HT):
                    for k in range(2):
                        mm = pe.matmul(PS[:, 6, i * E:(i + 1) * E], xnT[:, h, k, i * P:(i + 1) * P], rg[:, k, :],
                                       start=(k == 0), stop=(k == 1))
                mm.then_inc(scores_done, 1)

            steps = dict(sims=sims, graph_hot=graph_hot, graph_first=graph_first, graph_hidden=graph_hidden,
                         graph_feat=graph_feat, graph_out=graph_out, graph_check=graph_check,
                         ffn_norm=ffn_norm, ffn_up=ffn_up, ffn_down=ffn_down, attn=attn, router=router)
            pe.wait_ge(consts, CONSTS)
            for name, *at in SCHEDULE:
                if name in steps:
                    steps[name](*at)

            pe.wait_ge(onehots_ready, 1)
            pe.wait_ge(down_read, 2)
            for t in range(T):
                mm = pe.matmul(PS[:, 4, 0:E], ones[:, :], Os[:, t, :], start=(t == 0), stop=(t == T - 1))
            mm.then_inc(count_done, 1)
            for t in range(T - 1):
                rest = T - 1 - t
                pe.matmul(PS[:, 5, (t + 1) * E:T * E], ones[:, :], Os[:, t:t + 1, :].to_broadcast([P, rest, E]),
                          start=(t == 0), stop=False, skip_group_check=True)
            pe.matmul(PS[:, 5, 0:T * E], before[:, :], Os[:, :, :].rearrange("p t e -> p (t e)"),
                      start=False, stop=True, skip_group_check=True).then_inc(rank_done, 1)
            pe.wait_ge(rh_ready, 1)
            pe.wait_ge(scores_read, 2)
            for n in range(2 * T):
                pe.wait_ge(ph_ready, n + 1)
                mm = pe.matmul(PS[:, 6, 0:3 * NL], Ph[:, n % 2, :], RH[:, n, :], start=(n == 0), stop=(n == 2 * T - 1))
                mm.then_inc(ph_used, 1)
            pe.matmul(PS[:, 7, 0:1], ones[:, :], one8[:, 0:1], start=True, stop=True).then_inc(list_done, 1)

            def turn_x(j, q):
                for k in range(2):
                    mm = pe.transpose(PS[:, 4, q * 256 + k * P:q * 256 + (k + 1) * P], xg[q][:, k * P:(k + 1) * P],
                                      ident[:, :])
                mm.then_inc(xgT_done, 1)

            def up(w, bank, q, at, ready):
                for k in range(2):
                    mm = pe.matmul(PS[:, bank + q, :], xgT[q][:, k, :], w[:, bass.ds(at + k * F, F)],
                                   start=(k == 0), stop=(k == 1))
                mm.then_inc(ready, 1)

            def turn_h(j, q):
                pe.wait_ge(gated, j + 1)
                for k in range(4):
                    mm = pe.transpose(PS[:, 5, k * P:(k + 1) * P], hh[q][:, k * P:(k + 1) * P], ident[:, :])
                mm.then_inc(hhT_done, 1)

            def down(j, q, at):
                pe.wait_ge(hhT_copied, j + 1)
                for k in range(4):
                    mm = pe.matmul(PS[:, 6 + q, 0:C], hhT[q][:, k * P:(k + 1) * P],
                                   e2[:, bass.ds(at + k * C, C)], start=(k == 0), stop=(k == 3))
                mm.then_inc(y_done, 1)

            def expert(j):
                return pe.value_load(eoff[0:1, bass.ds(j, 1)], min_val=0, max_val=(E - 1) * 1024)

            pe.wait_ge(eoff_ready, 1)
            pe.wait_ge(rank_done, 1)
            pe.wait_ge(list_ready, 1)
            pe.wait_ge(experts_loaded, 16 * 3 * E)
            pe.wait_ge(gathered[0], 16)
            turn_x(0, 0)
            pe.wait_ge(xgT_copied, 1)
            at = expert(0)
            up(e1, 0, 0, at, up1_done)
            pe.wait_ge(gathered[1], 16)
            turn_x(1, 1)
            up(e3, 2, 0, at, up3_done)

            def pair(i, first=False):
                for q in range(2):
                    j = i * 2 + (1 + q)
                    me, other = (q + 1) % 2, q
                    at = expert(j)
                    pe.wait_ge(xgT_copied, j + 1)
                    if q or not first:
                        pe.wait_ge(gated, j - 1)
                    up(e1, 0, me, at, up1_done)
                    if q or not first:
                        pe.wait_ge(hhT_copied, j - 1)
                    turn_h(j - 1, other)
                    pe.wait_ge(gathered[other], i * 16 + 32)
                    turn_x(j + 1, other)
                    up(e3, 2, me, at, up3_done)
                    last = expert(j - 1)
                    if not first:
                        pe.wait_ge(y_scaled, j - 2)
                    down(j - 1, other, last)

            pair(0, first=True)
            with pe.Fori(1, PAIRS) as i:
                pair(i)
            pe.wait_ge(hhT_copied, NB - 1)
            turn_h(NB - 1, 0)
            pe.wait_ge(y_scaled, NB - 2)
            down(NB - 1, 0, expert(NB - 1))


_OUT = "out_0_dram"


def kernel(**inputs):
    import numpy as np
    import concourse.bacc as bacc
    from concourse.bass_utils import run_bass_kernel_spmd as run

    i = {k: np.asarray(v) for k, v in inputs.items()}
    pad = IT * P - INTER

    def columns(v):
        return np.concatenate([v, np.zeros(pad, v.dtype)]).reshape(IT, P).T

    def expert(w, k):
        e, n, kp = w.shape
        return w.reshape(e, n, k, P).transpose(0, 3, 2, 1).reshape(e, P, k * n)

    arrays = {
        "x_in": i["x"].reshape(B * N, C),
        "ctx_in": i["ctx_512"].reshape(B * N, D),
        "ctxT_in": i["ctx_512"].reshape(B * N, D).T,
        "g_xattn": i["g_xattn"], "g_ffn": i["g_ffn"], "gamma": i["L1_xattn_gamma_raw"].reshape(1),
        "w0_in": i["L0_xattn_W0"].transpose(1, 0, 2).reshape(D, H * FO),
        "as0": i["L0_xattn_a_self0"], "an0": i["L0_xattn_a_neigh0"],
        "b0_in": i["L0_xattn_b0"].reshape(2, P).T,
        "w1_in": i["L0_xattn_W1"].transpose(1, 0, 2).reshape(C, H * FO),
        "as1": i["L0_xattn_a_self1"], "an1": i["L0_xattn_a_neigh1"], "b1_in": i["L0_xattn_b1"],
        "gw_in": i["L0_ffn_gate_w"].T, "uw_in": i["L0_ffn_up_w"].T, "dw_in": i["L0_ffn_down_w"].T,
        "gs_in": columns(i["L0_ffn_gate_s"]), "us_in": columns(i["L0_ffn_up_s"]), "ds_in": i["L0_ffn_down_s"],
        "wq_in": i["L1_xattn_Wq"].T, "wk_in": i["L1_xattn_Wk"].T, "rg_in": i["L1_ffn_gate_w"].T,
        "e1_in": expert(i["L1_ffn_w1"], 2), "e3_in": expert(i["L1_ffn_w3"], 2),
        "e2_in": expert(i["L1_ffn_w2"], 4),
    }
    arrays = {k: np.ascontiguousarray(v) for k, v in arrays.items()}
    nc = bacc.Bacc("TRN2", target_bir_lowering=False, num_devices=1)
    args = [nc.dram_tensor(k, v.shape, mybir.dt.from_np(v.dtype), kind="ExternalInput").ap()
            for k, v in arrays.items()]
    args.append(nc.dram_tensor(_OUT, [B * N, C], F32, kind="ExternalOutput").ap())
    build(nc, *args)
    r = run(nc, [arrays], core_ids=[0])
    return r.results[0][_OUT].reshape(B, N, C)
```

```python
from contextlib import ExitStack

import concourse.bass as bass
from concourse import mybir

F32, I32, U32 = mybir.dt.float32, mybir.dt.int32, mybir.dt.uint32
ALU = mybir.AluOpType
ACT = mybir.ActivationFunctionType
AX = mybir.AxisListType

P = 128
B, N, C = 4, 256, 256
T = B * N // P
D = 64
H, FO = 8, 32
WX = H * FO + 2 * H
INTER = 704
IT = -(-INTER // P)
E, F = 8, 512
TOPK = max(1, int(N * 0.3))
ROUNDS = -(-TOPK // 8)
SLOTS = 2 * B * N
NB = SLOTS // P + E - 1
NL = NB + 2
PAIRS_MIN, PAIRS_MAX = SLOTS // P // 2, (NB - 1) // 2
PAD = 4096
HT = T // 2
HN = HT * P
EPS = 1e-5
BIG = 1e10
LEAD, ULPS, LOGIT = 2e4, 2.0 ** -21, 2000.0


def rows(ap):
    n = 1
    for s in ap.shape:
        n *= s
    flat = ap if len(ap.shape) == 1 else ap.rearrange("a b -> (a b)")
    return flat.rearrange("(a n) -> a n", a=1).to_broadcast([P, n])


def build(nc, x_in, ctx_in, ctxT_in, g_xattn, g_ffn, gamma, w0_in, w0T_in, b0_in, w1_in, w1T_in, a_in, b1_in,
          gw_in, uw_in, dw_in, gs_in, us_in, ds_in, wq_in, wk_in, rg_in, e1_in, e3_in, e2_in,
          out, force_general=False):
    xn3_dram = nc.dram_tensor("xn3_rows", [B * N, C], F32, kind="Internal").ap()
    ctx = ExitStack()
    with ctx:
        def sb(name, shape, dt=F32):
            return ctx.enter_context(nc.sbuf_tensor(name, shape, dt))

        def sem(name):
            return ctx.enter_context(nc.semaphore(name))

        PS = ctx.enter_context(nc.psum_tensor("PS", [P, 8, 512], F32))

        ident = sb("ident", [P, P])
        ones = sb("ones", [P, P])
        before = sb("before", [P, P])
        iota_p = sb("iota_p", [P, P])
        iota_e = sb("iota_e", [P, E])
        iota_q = sb("iota_q", [P, E])
        iota_b = sb("iota_b", [P, NL])
        token = sb("token", [P, 2 * T])
        nhalf = sb("nhalf", [P, HT])
        x = sb("x", [P, T, C])
        ctx_s = sb("ctx_s", [P, T, D])
        ctxT = sb("ctxT", [D, B * N])
        w0x = sb("w0x", [D, WX])
        w1x = sb("w1x", [P, 2, WX])
        b0 = sb("b0", [P, 2])
        b1 = sb("b1", [P, C])
        gates = sb("gates", [P, 5])
        tg = sb("tg", [P, 5])
        cc = sb("cc", [P, 4])
        e1 = sb("e1", [P, E * 1024])
        e3 = sb("e3", [P, E * 1024])
        e2 = sb("e2", [P, E * 1024])
        gw = e1[:, 5 * 1024:5 * 1024 + 2 * INTER].rearrange("p (k n) -> p k n", k=2)
        uw = e3[:, 5 * 1024:5 * 1024 + 2 * INTER].rearrange("p (k n) -> p k n", k=2)
        dw = e2[:, 5 * 1024:5 * 1024 + IT * C].rearrange("p (k n) -> p k n", k=IT)
        gs = sb("gs", [P, IT])
        us = sb("us", [P, IT])
        hgs = sb("hgs", [P, IT])
        cgu = sb("cgu", [P, IT])
        dsr = sb("dsr", [P, C])
        wq = sb("wq", [D, D])
        wk = sb("wk", [D, D])
        rg = sb("rg", [P, 2, E])
        xr = x
        at = (7 * 1024, 3 * 1024)
        mask = [e1[:, a:a + 1024].rearrange("p (t c) -> p t c", t=HT) for a in at]
        hot = [e3[:, a:a + 1024].rearrange("p (t c) -> p t c", t=HT) for a in at]
        hotT = [e2[:, a:a + 1024].rearrange("p (b m c) -> p b m c", b=2, m=2) for a in at]
        g0T = [sb("g0T", [D, HN]), e3[0:D, 4 * 1024:4 * 1024 + HN]]
        h0T = [sb("h0T", [P, 2, HN]), e2[:, 4 * 1024:5 * 1024].rearrange("p (k n) -> p k n", k=2)]
        feat = [sb("feat", [P, HT, WX]), sb("feat1", [P, HT, WX])]
        st0 = sb("st0", [P, T, 2 * H])
        zb = sb("zb", [P, HT * C])
        zc = sb("zc", [P, HT * C])
        xn = sb("xn", [P, HT, C])
        xnT = sb("xnT", [P, 2, 2, HN])
        th = sb("th", [P, 2, F])
        wbuf = sb("wbuf", [P, 2, F])
        hT = sb("hT", [P, IT, HN])
        w0T = wbuf[:, 0, 0:2 * D].rearrange("p (k n) -> p k n", k=2)
        avec = wbuf[:, 0, 2 * D:2 * D + 4 * 2 * H].rearrange("p (l k n) -> p l k n", l=2, k=2)
        w1T = wbuf[:, 1, :].rearrange("p (k n) -> p k n", k=2)
        z = [zb, zc]
        qk = zc
        sim = sb("sim", [P, T, N])
        work = sb("work", [P, 2, N])
        a2 = sb("a2", [P, T, N])
        top8 = sb("top8", [P, 2, 8])
        rs = sb("rs", [P, 3, HT])
        stat = sb("stat", [P, HT, 6])
        mv = sb("mv", [P, HT, 2])
        veps = sb("veps", [P, HT])
        rstd = sb("rstd", [P, HT])
        top = sb("top", [P, HT, 8])
        lead = sb("lead", [P, 2, HT])
        good = sb("good", [P, 2, HT + 2 * HT * 2 * H])
        gsm = sb("gsm", [P, 2 * HT * 2 * H])
        gmin = sb("gmin", [P, 2, 2])
        flag = sb("flag", [P, 2], I32)
        gctxT = sb("gctxT", [D, N])
        gfeat = feat[0][:, 0:2, :]
        gD = sb("gD", [P, 2, P])
        gEa = h0T[0][:, 0, :].rearrange("p (a n) -> p a n", a=2)
        gEb = h0T[0][:, 1, :].rearrange("p (a n) -> p a n", a=2)
        gnm = sb("gnm", [P, 2])
        gsum = sb("gsum", [P, 2])
        grs = sb("grs", [P, 2])
        gout = feat[0][:, 2:4, 0:C]
        sc = sb("sc", [P, T, E])
        mx8 = sb("mx8", [P, T, 8])
        ix8 = sb("ix8", [P, T, 8], U32)
        idxf = sb("idxf", [P, T, 2])
        O = sb("O", [P, 2, T, E])
        Os = sb("Os", [P, E, T])
        Dk = sb("Dk", [P, 2, T, E])
        Fk = sb("Fk", [P, 2, T, E])
        Ek = sb("Ek", [P, 2, T, E])
        ab = sb("ab", [P, T, E])
        mk = sb("mk", [P, 2 * T])
        nb = sb("nb", [P, E, E])
        nblk = sb("nblk", [P, E])
        incl = sb("incl", [P, E])
        base = sb("base", [P, E])
        one8 = sb("one8", [P, E])
        ecmp = sb("ecmp", [P, NL, E])
        eblk = sb("eblk", [P, NL])
        eoff = sb("eoff", [P, NL], I32)
        blocks = sb("blocks", [P, 2], I32)
        run = sb("run", [P, E, T])
        same_e = sb("same_e", [P, E, T])
        slf = sb("slf", [P, 2 * T])
        sli = sb("sli", [P, 2 * T], I32)
        sji = sb("sji", [P, 2 * T], I32)
        spi = sb("spi", [P, 2 * T], I32)
        sjf = sb("sjf", [P, 2 * T])
        spf = sb("spf", [P, 2 * T])
        RH = sim[:, :, :].rearrange("p t n -> p (t n)")[:, 0:4 * T * NL].rearrange("p (a b) -> p a b", a=2 * T)
        places = a2[:, :, :].rearrange("p t n -> p (t n)").rearrange("p (a b) -> p a b", a=2 * T)
        lst = sb("lst", [P, NL])
        idsu = sb("idsu", [P, NL], U32)
        coef = sb("coef", [P, NL])
        gidx = [sb(f"gidx{q}", [P, 1], U32) for q in range(2)]
        sidx = [sb(f"sidx{q}", [P, 1], U32) for q in range(2)]
        xg = [zc[:, q * C:(q + 1) * C] for q in range(2)]
        hh = [hT[:, q, :] for q in range(2)]
        hhT = [hT[:, 2 + q, :] for q in range(2)]
        yv = [hT[:, 4, q * C:(q + 1) * C] for q in range(2)]
        xgT = [hT[:, 5, q * C:(q + 1) * C].rearrange("p (k n) -> p k n", k=2) for q in range(2)]

        x_loaded = [sem(f"x_loaded{h}") for h in range(2)]
        ctx_loaded = sem("ctx_loaded")
        qk_loaded = sem("qk_loaded")
        gates_loaded = sem("gates_loaded")
        logits_loaded = sem("logits_loaded")
        gat_loaded = sem("gat_loaded")
        ffn_loaded = sem("ffn_loaded")
        router_loaded = sem("router_loaded")
        experts_loaded = sem("experts_loaded")
        consts = sem("consts")
        gates_tanh = sem("gates_tanh")
        dve_done = sem("dve_done")
        act_done = sem("act_done")
        pool_done = sem("pool_done")
        pool_passed = sem("pool_passed")
        var_ready = sem("var_ready")
        rstd_ready = sem("rstd_ready")
        qk_done = sem("qk_done")
        qk_copied = sem("qk_copied")
        sim_done = sem("sim_done")
        sim_copied = sem("sim_copied")
        sig_ready = sem("sig_ready")
        a2_ready = sem("a2_ready")
        a2T_done = sem("a2T_done")
        x3_ready = sem("x3_ready")
        wa_done = sem("wa_done")
        wa_copied = sem("wa_copied")
        scales_ready = sem("scales_ready")
        st0_done = sem("st0_done")
        st0_copied = sem("st0_copied")
        hot_ready = sem("hot_ready")
        hotT_done = sem("hotT_done")
        hotT_copied = sem("hotT_copied")
        g0_done = sem("g0_done")
        g0_copied = sem("g0_copied")
        h0_done = sem("h0_done")
        h0_exp = sem("h0_exp")
        h0_ready = sem("h0_ready")
        feat_done = sem("feat_done")
        feat_copied = sem("feat_copied")
        out1_done = sem("out1_done")
        out1_read = sem("out1_read")
        out1_exp = sem("out1_exp")
        good_ready = sem("good_ready")
        graph_over = sem("graph_over")
        bad_counted = sem("bad_counted")
        flag_ready = sem("flag_ready")
        general = [sem(f"general{h}") for h in range(2)]
        xn_ready = sem("xn_ready")
        xnT_done = sem("xnT_done")
        xnT_copied = sem("xnT_copied")
        ffn_g_done = sem("ffn_g_done")
        ffn_u_done = sem("ffn_u_done")
        ffn_tanh = sem("ffn_tanh")
        ffn_h_ready = sem("ffn_h_ready")
        down_done = sem("down_done")
        down_read = sem("down_read")
        rows_stored = sem("rows_stored")
        out_stored = sem("out_stored")
        scores_done = sem("scores_done")
        scores_read = sem("scores_read")
        d_ready = sem("d_ready")
        ek_ready = sem("ek_ready")
        onehots_ready = sem("onehots_ready")
        count_done = sem("count_done")
        rank_done = sem("rank_done")
        rh_ready = sem("rh_ready")
        ph_ready = sem("ph_ready")
        eoff_ready = sem("eoff_ready")
        blocks_ready = sem("blocks_ready")
        list_done = sem("list_done")
        list_ready = sem("list_ready")
        coef_ready = sem("coef_ready")
        gidx_set = sem("gidx_set")
        gathered = [sem(f"gathered{q}") for q in range(2)]
        xgT_done = sem("xgT_done")
        xgT_copied = sem("xgT_copied")
        up1_done = sem("up1_done")
        up3_done = sem("up3_done")
        silu_tanh = sem("silu_tanh")
        w_ready = sem("w_ready")
        gated = sem("gated")
        hhT_done = sem("hhT_done")
        hhT_copied = sem("hhT_copied")
        y_done = sem("y_done")
        y_scaled = sem("y_scaled")
        sidx_set = sem("sidx_set")
        scattered = [sem(f"scattered{q}") for q in range(2)]

        CONSTS = 12
        BANK = (6, 4)
        PARTS = ((0, HT), (HT, HT // 2), (HT + HT // 2, HT // 2))
        TURN_BANK = (6, 0, 2)
        SCHEDULE = ([("sims", 0), ("graph_hot", 0), ("graph_first", 0), ("logits", 0), ("sigmoids", 0),
                     ("graph_hot", 1), ("graph_hidden", 0), ("graph_first", 1), ("graph_feat", 0),
                     ("graph_hidden", 1), ("graph_out", 0), ("graph_feat", 1), ("graph_elu", 0), ("graph_out", 1),
                     ("graph_check", 0), ("norm_ffn", 0), ("turn_ffn", 0), ("graph_elu", 1), ("graph_check", 1)]
                    + [("ffn_up", 0, 0), ("norm_ffn", 1), ("ffn_up", 0, 1), ("ffn_up", 0, 2), ("turn_ffn", 1)]
                    + [("ffn_up", 0, it) for it in range(3, IT)]
                    + [("ffn_down", 0), ("ffn_up", 1, 0), ("kept", 0), ("attn", 0), ("ffn_up", 1, 1),
                       ("norm_moe", 0), ("ffn_up", 1, 2), ("turn_moe", 0), ("ffn_up", 1, 3), ("router", 0),
                       ("ffn_up", 1, 4), ("choices", 0), ("ffn_up", 1, 5)]
                    + [("ffn_down", 1), ("ffn_down", 2), ("kept", 1), ("attn", 1), ("norm_moe", 1), ("turn_moe", 1), ("attn", 2),
                       ("norm_moe", 2), ("router", 1), ("turn_moe", 2), ("router", 2), ("choices", 1), ("choices", 2)])
        order = lambda names: {stage: n for n, stage in enumerate(s for s in SCHEDULE if s[0] in names)}
        LN = order(("graph_hot", "norm_ffn", "attn", "norm_moe"))
        XT = order(("turn_ffn", "turn_moe"))

        HEAD_STEPS = 12
        PRE_STEPS, MID_STEPS, POST_STEPS = 3, 7, 5
        BATCH_STEPS = PRE_STEPS + MID_STEPS + POST_STEPS + 2 * H * HEAD_STEPS

        def pairs_in_use(engine):
            engine.wait_ge(blocks_ready, 1)
            return engine.value_load(blocks[0:1, 1:2], min_val=PAIRS_MIN, max_val=PAIRS_MAX)

        block = ctx.enter_context(nc.Block())

        @block.sync
        def _(sp):
            xv = x_in.rearrange("(t p) c -> p t c", p=P)
            sp.dma_start(x[:, 0:HT, :], xv[:, 0:HT, :]).then_inc(x_loaded[0], 16)
            sp.dma_start(ctxT[:, :], ctxT_in).then_inc(qk_loaded, 16)
            sp.dma_start(ctx_s[:, :, :], ctx_in.rearrange("(t p) d -> p t d", p=P)).then_inc(ctx_loaded, 16)
            sp.dma_start(w0x[:, 0:H * FO], w0_in).then_inc(gat_loaded, 16)
            sp.dma_start(w1x[:, :, 0:H * FO], w1_in.rearrange("(k p) n -> p k n", p=P)).then_inc(gat_loaded, 16)
            sp.dma_start(b0[:, :], b0_in).then_inc(gat_loaded, 16)
            sp.dma_start(b1[:, :], rows(b1_in)).then_inc(gat_loaded, 16)
            sp.dma_start(x[:, HT:T, :], xv[:, HT:T, :]).then_inc(x_loaded[1], 16)
            full = INTER // P
            for w, src in ((gw, gw_in), (uw, uw_in)):
                sp.dma_start(w[:, :, :], src.rearrange("(k p) n -> p k n", p=P)).then_inc(ffn_loaded, 16)
            for v, src in ((gs, gs_in), (us, us_in)):
                sp.dma_start(v[:, :], src).then_inc(ffn_loaded, 16)
            sp.dma_start(dw[:, 0:full, :], dw_in[0:full * P, :].rearrange("(k p) n -> p k n", p=P))\
              .then_inc(ffn_loaded, 16)
            sp.dma_start(dw[0:INTER - full * P, full, :], dw_in[full * P:INTER, :]).then_inc(ffn_loaded, 16)
            sp.dma_start(dsr[:, :], rows(ds_in)).then_inc(ffn_loaded, 16)
            sp.dma_start(rg[:, :, :], rg_in.rearrange("(k p) n -> p k n", p=P)).then_inc(router_loaded, 16)
            def load_expert(e):
                for w, src in ((e1, e1_in), (e3, e3_in), (e2, e2_in)):
                    sp.dma_start(w[:, e * 1024:(e + 1) * 1024], src[e]).then_inc(experts_loaded, 16)

            for e in range(3):
                load_expert(e)
            sp.wait_ge(graph_over, 2)
            for e in (3, 4, 7):
                load_expert(e)
            for p, (t, n) in enumerate(PARTS):
                if p == 1:
                    sp.wait_ge(down_done, len(PARTS))
                    load_expert(5)
                    load_expert(6)
                sp.wait_ge(x3_ready, p + 1)
                sp.dma_start(out.rearrange("(t p) c -> p t c", p=P)[:, t:t + n, :],
                             xr[:, t:t + n, :]).then_inc(out_stored, 16)
                sp.wait_ge(xn_ready, XT["turn_moe", p] + 1)
                sp.dma_start(xn3_dram.rearrange("(t p) c -> p t c", p=P)[:, t:t + n, :],
                             xn[:, t % HT:t % HT + n, :]).then_inc(rows_stored, 16)
            sp.wait_ge(out_stored, 16 * len(PARTS))
            sp.wait_ge(rows_stored, 16 * len(PARTS))

        @block.gpsimd
        def _(pool):
            done = [0]

            def own(ins):
                done[0] += 1
                ins.then_inc(pool_done, 1)
                pool.wait_ge(pool_done, done[0])

            pool.memset(ones[:, :], 1.0).then_inc(consts, 1)
            pool.memset(nhalf[:, :], -0.5).then_inc(consts, 1)
            pool.memset(one8[:, :], 1.0).then_inc(consts, 1)
            own(pool.memset(ident[:, :], 0.0))
            pool.affine_select(out=ident[:, :], in_=ident[:, :], compare_op=ALU.not_equal, fill=1.0,
                               base=0, pattern=[[-1, P]], channel_multiplier=1).then_inc(consts, 1)
            own(pool.memset(before[:, :], 1.0))
            pool.affine_select(out=before[:, :], in_=before[:, :], compare_op=ALU.is_gt, fill=0.0,
                               base=0, pattern=[[1, P]], channel_multiplier=-1).then_inc(consts, 1)
            small = dict(allow_small_or_imprecise_dtypes=True)
            pool.iota(iota_p[:, :], [[1, P]], base=0, channel_multiplier=0, **small).then_inc(consts, 1)
            pool.iota(iota_e[:, :], [[1, E]], base=0, channel_multiplier=0, **small).then_inc(consts, 1)
            pool.iota(iota_q[:, :], [[P, E]], base=0, channel_multiplier=0, **small).then_inc(consts, 1)
            pool.iota(iota_b[:, :], [[1, NL]], base=0, channel_multiplier=0, **small).then_inc(consts, 1)
            own(pool.memset(same_e[:, :, :], 1.0))
            pool.memset(same_e[:, :, 0], 0.0).then_inc(consts, 1)
            pool.iota(token[:, :], [[0, 2], [P, T]], base=1, channel_multiplier=1, **small).then_inc(consts, 1)
            pool.memset(zc[:, 0:2 * C], 0.0).then_inc(consts, 1)
            pool.wait_ge(consts, CONSTS)
            for n in range(len(LN)):
                pool.wait_ge(var_ready, n + 1)
                pool.tensor_tensor(rstd[:, :], veps[:, :], nhalf[:, :], ALU.pow).then_inc(rstd_ready, 1)

            def gather(j, q):
                pool.tensor_copy(gidx[q][:, :], idsu[:, bass.ds(j, 1)]).then_inc(gidx_set, 1)
                pool.wait_ge(gidx_set, j + 1)
                pool.sem_inc(pool_passed)
                pool.indirect_dma_start(
                    out=xg[q], out_offset=None, in_=xn3_dram,
                    in_offset=bass.IndirectOffsetOnAxis(ap=gidx[q][:, 0:1], axis=0),
                    bounds_check=bound, oob_is_err=False).then_inc(gathered[q], 16)

            def scatter(j, q):
                pool.tensor_copy(sidx[q][:, :], idsu[:, bass.ds(j, 1)]).then_inc(sidx_set, 1)
                pool.wait_ge(sidx_set, j + 1)
                pool.wait_ge(y_scaled, j + 1)
                pool.sem_inc(pool_passed)
                pool.indirect_dma_start(
                    out=out, out_offset=bass.IndirectOffsetOnAxis(ap=sidx[q][:, 0:1], axis=0),
                    in_=yv[q], in_offset=None,
                    bounds_check=bound, oob_is_err=False, compute_op=ALU.add).then_inc(scattered[q], 16)

            bound = pool.to_reg(B * N - 1)
            pool.wait_ge(list_ready, 1)
            pool.wait_ge(rows_stored, 16 * len(PARTS))
            pool.wait_ge(out_stored, 16 * len(PARTS))
            gather(0, 0)
            gather(1, 1)
            pool.wait_ge(xgT_done, 1)
            pool.wait_ge(gathered[0], 16)
            gather(2, 0)

            def pair(i, first=False):
                j = i * 2 + 1
                pool.wait_ge(xgT_done, j + 1)
                pool.wait_ge(gathered[1], i * 16 + 16)
                gather(j + 2, 1)
                if not first:
                    pool.wait_ge(scattered[1], i * 16)
                scatter(j - 1, 0)
                pool.wait_ge(xgT_done, j + 2)
                pool.wait_ge(gathered[0], i * 16 + 32)
                gather(j + 3, 0)
                pool.wait_ge(scattered[0], i * 16 + 16)
                scatter(j, 1)

            pair(0, first=True)
            pairs = pairs_in_use(pool)
            with pool.Fori(1, pairs) as i:
                pair(i)
            pool.wait_ge(scattered[1], pairs * 16)
            scatter(pairs * 2, 0)
            pool.wait_ge(scattered[0], pairs * 16 + 16)
            pool.wait_ge(gathered[0], pairs * 16 + 32)

        @block.scalar
        def _(act):
            copy = ACT.Copy

            act.dma_start(wq[:, :], wq_in).then_inc(qk_loaded, 16)
            act.dma_start(wk[:, :], wk_in).then_inc(qk_loaded, 16)
            act.dma_start(gates[:, 0:2], rows(g_xattn)).then_inc(gates_loaded, 16)
            act.dma_start(gates[:, 2:4], rows(g_ffn)).then_inc(gates_loaded, 16)
            act.dma_start(gates[:, 4:5], rows(gamma)).then_inc(gates_loaded, 16)
            act.dma_start(avec, a_in.rearrange("l (k p) n -> p l k n", p=P)).then_inc(logits_loaded, 16)
            act.dma_start(w0T, w0T_in.rearrange("(k p) n -> p k n", p=P)).then_inc(logits_loaded, 16)
            act.dma_start(w1T, w1T_in.rearrange("(k p) n -> p k n", p=P)).then_inc(logits_loaded, 16)
            act.wait_ge(gates_loaded, 48)
            act.activation(tg[:, 0:4], gates[:, 0:4], ACT.Tanh)
            act.activation(tg[:, 4:5], gates[:, 4:5], ACT.Tanh, scale=0.5).then_inc(gates_tanh, 1)

            def sims(h):
                for q in range(2):
                    act.wait_ge(qk_done, q + 1)
                    act.activation(qk[0:D, q * 512:(q + 1) * 512].rearrange("p (a n) -> p a n", a=1),
                                   PS[0:D, q:q + 1, :], copy).then_inc(qk_copied, 1)
                for q in range(2):
                    act.wait_ge(qk_done, q + 3)
                    act.activation(zb[0:D, q * 512:(q + 1) * 512], PS[0:D, 2 + q, :], copy).then_inc(qk_copied, 1)
                for q in range(4):
                    act.wait_ge(sim_done, q + 1)
                    act.activation(sim[:, 2 * q:2 * q + 2, :], PS[:, q, :].rearrange("p (a n) -> p a n", a=2),
                                   copy, scale=1.0 / 16.0).then_inc(sim_copied, 1)

            def logits(h):
                act.wait_ge(gat_loaded, 16 * 4)
                act.wait_ge(wa_done, 1)
                act.activation(w0x[:, H * FO:WX], PS[0:D, 0, 0:2 * H], copy)
                act.activation(w1x[:, :, H * FO:WX], PS[:, 0, 2 * H:6 * H].rearrange("p (k n) -> p k n", k=2),
                               copy).then_inc(wa_copied, 1)
                act.wait_ge(st0_done, 1)
                act.activation(st0[:, :, :], PS[:, 1, 0:T * 2 * H].rearrange("p (t n) -> p t n", t=T),
                               copy).then_inc(st0_copied, 1)

            def sigmoids(h):
                act.wait_ge(sim_copied, 4)
                act.activation(a2[:, :, :], sim[:, :, :], ACT.Tanh, scale=0.5).then_inc(act_done, 1)
                act.wait_ge(act_done, 1)
                act.activation(a2[:, :, :], a2[:, :, :], copy, bias=1.0).then_inc(sig_ready, 1)

            def graph_hot(h):
                for b in range(2):
                    act.wait_ge(hotT_done, 2 * h + b + 1)
                    act.activation(hotT[h][:, b, :, :], PS[:, BANK[h] + b, :].rearrange("p (m n) -> p m n", m=2),
                                   copy).then_inc(hotT_copied, 1)

            def graph_first(h):
                act.wait_ge(g0_done, h + 1)
                act.activation(g0T[h][:, :], PS[0:D, BANK[h], :], copy).then_inc(g0_copied, 1)

            def graph_hidden(h):
                act.wait_ge(h0_done, h + 1)
                for k in range(2):
                    ins = act.activation(z[h][:, k * HN:(k + 1) * HN], PS[:, BANK[h] + k, :], ACT.Exp, bias=b0[:, k:k + 1])
                ins.then_inc(h0_exp, 1)

            def graph_feat(h):
                for i in range(HT):
                    act.wait_ge(feat_done, HT * h + i + 1)
                    act.activation(feat[h][:, i, :], PS[:, BANK[h] + i % 2, 0:WX], copy).then_inc(feat_copied, 1)

            def graph_out(h):
                act.wait_ge(out1_done, h + 1)
                act.activation(z[h][:, :], PS[:, BANK[h]:BANK[h] + 2, :].rearrange("p b n -> p (b n)"), ACT.Exp).then_inc(out1_exp, 1)

            def general_path(h):
                sem_g = general[h]
                with act.Fori(0, 2) as b:
                    start = b * BATCH_STEPS + 1
                    for at in (PRE_STEPS, PRE_STEPS + H * HEAD_STEPS + MID_STEPS):
                        with act.Fori(0, H) as hd:
                            act.wait_ge(sem_g, start + hd * HEAD_STEPS + (at + 6))
                            act.activation(gEa[:, 0, :], gEb[:, 0, :], ACT.Exp, bias=gnm[:, 0:1],
                                           accum_out=gsum[:, 0:1])
                            act.activation(gEa[:, 1, :], gEb[:, 1, :], ACT.Exp, bias=gnm[:, 1:2],
                                           accum_out=gsum[:, 1:2]).then_inc(sem_g, 1)
                        act.wait_ge(sem_g, start + (at + H * HEAD_STEPS + 2))
                        act.activation(gEb[:, :, :], gEa[:, :, :], ACT.Exp).then_inc(sem_g, 1)
                act.wait_ge(sem_g, 1 + 2 * BATCH_STEPS)

            def graph_check(h):
                act.wait_ge(flag_ready, h + 1)
                r = act.value_load(flag[0:1, h:h + 1], min_val=0, max_val=1)
                with act.If(r):
                    general_path(h)

            def turn_ffn(h):
                act.wait_ge(xnT_done, XT["turn_ffn", h] + 1)
                act.activation(xnT[:, h, :, :], PS[:, 6:8, :], copy).then_inc(xnT_copied, 1)

            def turn_moe(p):
                t, n = PARTS[p]
                bank, at = TURN_BANK[p], (t % HT) * P
                act.wait_ge(xnT_done, XT["turn_moe", p] + 1)
                act.wait_ge(ffn_u_done, IT * (t // HT + 1))
                act.activation(xnT[:, t // HT, :, at:at + n * P], PS[:, bank:bank + 2, 0:n * P], copy)\
                   .then_inc(xnT_copied, 1)

            def ffn_up(h, it):
                n = h * IT + it
                M = min(P, INTER - it * P)
                act.wait_ge(ffn_g_done, n + 1)
                if n == 0:
                    act.wait_ge(scales_ready, 1)
                if n >= 2:
                    act.wait_ge(ffn_h_ready, n - 1)
                act.activation(th[0:M, n % 2, :], PS[0:M, n % 2, :], ACT.Tanh,
                               scale=hgs[0:M, it:it + 1]).then_inc(ffn_tanh, 1)

            steps = dict(sims=sims, logits=logits, sigmoids=sigmoids, graph_hot=graph_hot, graph_first=graph_first,
                         graph_hidden=graph_hidden, graph_feat=graph_feat, graph_out=graph_out,
                         graph_check=graph_check, turn_ffn=turn_ffn, ffn_up=ffn_up, turn_moe=turn_moe)
            for name, *at in SCHEDULE:
                if name in steps:
                    steps[name](*at)
            act.wait_ge(d_ready, 1)
            act.activation(Ek[:, :, :, :].rearrange("p k t e -> p (k t e)"),
                           Dk[:, :, :, :].rearrange("p k t e -> p (k t e)"), ACT.Exp, scale=-1.0)\
               .then_inc(ek_ready, 1)

            def copy_xgT(j, q):
                act.wait_ge(xgT_done, j + 1)
                act.activation(xgT[q], PS[:, 4, q * 256:(q + 1) * 256].rearrange("p (k n) -> p k n", k=2),
                               copy).then_inc(xgT_copied, 1)

            def silu(j, q):
                act.wait_ge(up1_done, j + 1)
                act.activation(th[:, q, :], PS[:, q, :], ACT.Tanh, scale=0.5).then_inc(silu_tanh, 1)

            def copy_hhT(j, q):
                act.wait_ge(hhT_done, j + 1)
                act.activation(hhT[q], PS[:, 5, :], copy).then_inc(hhT_copied, 1)

            def scale_y(j, q):
                act.wait_ge(y_done, j + 1)
                act.wait_ge(coef_ready, 1)
                act.activation(yv[q], PS[:, 6 + q, 0:C], copy,
                               scale=coef[:, bass.ds(j, 1)]).then_inc(y_scaled, 1)

            copy_xgT(0, 0)
            silu(0, 0)
            copy_xgT(1, 1)

            def pair(i, first=False):
                for q in range(2):
                    j = i * 2 + (1 + q)
                    me, other = (q + 1) % 2, q
                    if q or not first:
                        act.wait_ge(gated, j - 1)
                    silu(j, me)
                    copy_hhT(j - 1, other)
                    act.wait_ge(up3_done, j)
                    copy_xgT(j + 1, other)
                    if not first:
                        act.wait_ge(scattered[other], i * 16)
                    scale_y(j - 1, other)

            pair(0, first=True)
            pairs = pairs_in_use(act)
            with act.Fori(1, pairs) as i:
                pair(i)
            copy_hhT(pairs * 2, 0)
            act.wait_ge(scattered[0], pairs * 16)
            scale_y(pairs * 2, 0)

        @block.vector
        def _(dve):
            done = [0]

            def own(ins):
                done[0] += 1
                ins.then_inc(dve_done, 1)
                dve.wait_ge(dve_done, done[0])

            def mark(ins):
                done[0] += 1
                ins.then_inc(dve_done, 1)
                return done[0]

            def after(n):
                dve.wait_ge(dve_done, n)

            def stats(src, n, tiles=HT):
                for i in range(tiles):
                    ins = dve.bn_stats(stat[:, i, :], src[:, i, :])
                own(ins)
                for i in range(tiles):
                    ins = dve.bn_aggr(mv[:, i, :], stat[:, i, :])
                own(ins)
                dve.tensor_scalar(veps[:, :], mv[:, :, 1], EPS, None, ALU.add).then_inc(var_ready, 1)
                search(FILL.get(("deviation", n), 0))
                dve.wait_ge(rstd_ready, n + 1)

            FILL = {("graph_hot", 1): 7, ("graph_hidden", 0): 3, ("graph_hidden", 1): 1, ("graph_feat", 1): 1,
                    ("graph_check", 0): 0, ("graph_check", 1): 1, ("norm_ffn", 0): 3,
                    ("norm_ffn", 1): 1, ("ffn_down", 0): 1, ("attn", 0): 1}
            FILL.update({("ffn_up", h, it): 1 for h in range(2) for it in range(IT)})
            FILL.update({("ffn_up", 0, IT - 1): 7, ("ffn_up", 1, IT - 1): 7})
            FILL.update({("deviation", n): 1 for n in range(1, 8)})

            def half(t, h):
                return t[:, h * HT:(h + 1) * HT, :]

            def thresholds():
                k = (TOPK - 1) % 8
                for t in range(0, T, 2):
                    removed = [None, None]
                    for r in range(ROUNDS):
                        found = []
                        for q in range(2):
                            if r:
                                after(removed[q])
                            src = work[:, q, :] if r else sim[:, t + q, :]
                            found.append(mark(dve.max(out=top8[:, q, :], in_=src)))
                        for q in range(2):
                            after(found[q])
                            if r < ROUNDS - 1:
                                src = work[:, q, :] if r else sim[:, t + q, :]
                                removed[q] = mark(dve.match_replace(out=work[:, q, :], in_to_replace=top8[:, q, :],
                                                                    in_values=src, imm_value=-3.4e38))
                            else:
                                if t == 0 and q == 0:
                                    dve.wait_ge(sig_ready, 1)
                                dve.scalar_tensor_tensor(out=a2[:, t + q, :], in0=sim[:, t + q, :],
                                                         scalar=top8[:, q, k:k + 1], in1=a2[:, t + q, :],
                                                         op0=ALU.is_ge, op1=ALU.mult).then_inc(a2_ready, 1)
                        yield

            searching = thresholds()
            rounds_done = [0]

            def search(n):
                for _ in range(n):
                    if rounds_done[0] < ROUNDS * T // 2:
                        if rounds_done[0] == 0:
                            dve.wait_ge(sim_copied, 4)
                        if rounds_done[0] and rounds_done[0] % ROUNDS == 0:
                            dve.wait_ge(a2_ready, 2 * (rounds_done[0] // ROUNDS))
                        next(searching)
                        rounds_done[0] += 1

            def graph_hot(h):
                if h == 0:
                    dve.wait_ge(consts, CONSTS)
                dve.wait_ge(x_loaded[h], 16)
                stats(half(x, h), LN["graph_hot", h])
                for i in range(HT):
                    ins = dve.tensor_scalar(mask[h][:, i, :], x[:, h * HT + i, :], mv[:, i, 0:1],
                                            rstd[:, i:i + 1], ALU.subtract, ALU.mult)
                own(ins)
                flat = mask[h].rearrange("p a b -> p (a b)")
                own(dve.tensor_scalar(flat, flat, 1.0, BIG, ALU.subtract, ALU.mult))
                for i in range(HT):
                    ins = dve.max(out=top[:, i, :], in_=mask[h][:, i, :])
                own(ins)
                for i in range(HT):
                    ins = dve.tensor_scalar(hot[h][:, i, :], mask[h][:, i, :], top[:, i, 0:1], None, ALU.is_ge)
                    ins.then_inc(hot_ready, 1)
                own(dve.scalar_tensor_tensor(out=lead[:, 0, :], in0=top[:, :, 0], scalar=-1.0,
                                             in1=top[:, :, 0], op0=ALU.mult, op1=ALU.max))
                dve.tensor_tensor(lead[:, 1, :], top[:, :, 0], top[:, :, 1], ALU.subtract)
                own(dve.tensor_scalar(lead[:, 0, :], lead[:, 0, :], ULPS, LEAD, ALU.mult, ALU.add))
                own(dve.tensor_tensor(good[:, h, 0:HT], lead[:, 1, :], lead[:, 0, :], ALU.is_gt))
                if h == 0:
                    setup()

            def setup():
                dve.wait_ge(gates_tanh, 1)
                own(dve.tensor_scalar(cc[:, 0:1], tg[:, 4:5], 0.5, 0.5, ALU.mult, ALU.add))
                own(dve.tensor_scalar(cc[:, 1:2], cc[:, 0:1], -1.0, 1.0, ALU.mult, ALU.add))
                own(dve.tensor_tensor(cc[:, 2:3], cc[:, 1:2], tg[:, 1:2], ALU.mult))
                own(dve.tensor_scalar(cc[:, 3:4], cc[:, 0:1], tg[:, 1:2], 0.25, ALU.mult, ALU.mult))
                dve.wait_ge(ffn_loaded, 16 * 7)
                own(dve.tensor_scalar(hgs[:, :], gs[:, :], 0.5, None, ALU.mult))
                own(dve.tensor_tensor(cgu[:, :], hgs[:, :], us[:, :], ALU.mult))
                dve.tensor_scalar(dsr[:, :], dsr[:, :], tg[:, 2:3], None, ALU.mult).then_inc(scales_ready, 1)

            def graph_hidden(h):
                dve.wait_ge(h0_exp, h + 1)
                own(dve.tensor_scalar(z[h][:, :], z[h][:, :], 1.0, 1.0, ALU.min, ALU.subtract))
                for k in range(2):
                    ins = dve.scalar_tensor_tensor(out=h0T[h][:, k, :], in0=PS[:, BANK[h] + k, :],
                                                   scalar=b0[:, k:k + 1], in1=z[h][:, k * HN:(k + 1) * HN], op0=ALU.add, op1=ALU.max)
                ins.then_inc(h0_ready, 1)

            def graph_feat(h):
                dve.wait_ge(feat_copied, HT * (h + 1))
                dve.wait_ge(st0_copied, 1)
                n = HT * 2 * H
                own(dve.scalar_tensor_tensor(out=gsm[:, 0:n].rearrange("p (t n) -> p t n", t=HT),
                                             in0=half(st0, h), scalar=-1.0, in1=half(st0, h),
                                             op0=ALU.mult, op1=ALU.max))
                own(dve.scalar_tensor_tensor(out=gsm[:, n:2 * n].rearrange("p (t n) -> p t n", t=HT),
                                             in0=feat[h][:, :, H * FO:WX], scalar=-1.0, in1=feat[h][:, :, H * FO:WX],
                                             op0=ALU.mult, op1=ALU.max))
                own(dve.tensor_scalar(good[:, h, HT:HT + 2 * n], gsm[:, :], LOGIT, None, ALU.is_le))
                own(dve.tensor_reduce(gmin[:, h, 0:1], good[:, h, :], AX.X, ALU.min))
                dve.tensor_scalar(gmin[:, h, 1:2], gmin[:, h, 0:1], -1.0, 1.0 if not force_general else 2.0,
                                  ALU.mult, ALU.add).then_inc(good_ready, 1)

            def graph_elu(h):
                dve.wait_ge(out1_exp, h + 1)
                own(dve.tensor_scalar(z[h][:, :], z[h][:, :], 1.0, 1.0, ALU.min, ALU.subtract))
                own(dve.tensor_tensor(z[h][:, :], PS[:, BANK[h]:BANK[h] + 2, :].rearrange("p b n -> p (b n)"),
                                      z[h][:, :], ALU.max))

            def add_graph(h):
                xh = half(xr, h).rearrange("p t c -> p (t c)")
                dve.scalar_tensor_tensor(out=xh, in0=z[h][:, :], scalar=tg[:, 0:1], in1=xh,
                                         op0=ALU.mult, op1=ALU.add).then_inc(graph_over, 1)
                dve.wait_ge(graph_over, h + 1)

            def general_path(h):
                g = general[h]
                dve.memset(gnm[:, :], 0.0).then_inc(g, 1)

                def step(at, ins):
                    ins.then_inc(g, 1)

                def heads(start, at, b):
                    with dve.Fori(0, H) as hd:
                        k = start + hd * HEAD_STEPS + at
                        dve.wait_ge(g, k)
                        for m in range(2):
                            ins = dve.tensor_scalar(gD[:, m, :], ident[:, :],
                                                    gfeat[:, m, bass.ds(hd + (H * FO + H), 1)], None, ALU.mult)
                        ins.then_inc(g, 1)
                        dve.wait_ge(g, k + 2)
                        for m in range(2):
                            ins = dve.tensor_scalar(gEa[:, m, :], PS[:, 6, 0:N],
                                                    gfeat[:, m, bass.ds(hd + H * FO, 1)], None, ALU.add)
                        ins.then_inc(g, 1)
                        dve.wait_ge(g, k + 3)
                        dve.scalar_tensor_tensor(out=gEb[:, :, :], in0=gEa[:, :, :], scalar=0.2, in1=gEa[:, :, :],
                                                 op0=ALU.mult, op1=ALU.max).then_inc(g, 1)
                        dve.wait_ge(g, k + 4)
                        dve.tensor_tensor(gEb[:, :, :].rearrange("p a b -> p (a b)"),
                                          gEb[:, :, :].rearrange("p a b -> p (a b)"),
                                          mask[h].rearrange("p a b -> p (a b)")[:, bass.ds(b * (2 * N), 2 * N)],
                                          ALU.add).then_inc(g, 1)
                        dve.wait_ge(g, k + 5)
                        dve.tensor_reduce(gnm[:, :], gEb[:, :, :], AX.X, ALU.max, negate=True).then_inc(g, 1)
                        dve.wait_ge(g, k + 7)
                        dve.reciprocal(grs[:, :], gsum[:, :]).then_inc(g, 1)
                        dve.wait_ge(g, k + 9)
                        dve.tensor_copy(gEb[:, :, :], PS[:, 7, :].rearrange("p (a b) -> p a b", a=2)).then_inc(g, 1)
                        dve.wait_ge(g, k + 11)
                        for m in range(2):
                            ins = dve.tensor_scalar(gout[:, m, bass.ds(hd * FO, FO)],
                                                    PS[:, 6, m * FO:(m + 1) * FO], grs[:, m:m + 1], None, ALU.mult)
                        ins.then_inc(g, 1)

                with dve.Fori(0, 2) as b:
                    start = b * BATCH_STEPS + 1
                    dve.wait_ge(g, start)
                    dve.tensor_copy(gctxT[:, :], ctxT[:, bass.ds(b * N + h * HN, N)]).then_inc(g, 1)
                    dve.wait_ge(g, start + 2)
                    dve.tensor_copy(gfeat[:, :, :], PS[:, 6:8, 0:WX]).then_inc(g, 1)
                    heads(start, PRE_STEPS, b)
                    k = start + (PRE_STEPS + H * HEAD_STEPS)
                    dve.wait_ge(g, k + 1)
                    for m in range(2):
                        ins = dve.tensor_scalar(gEa[:, m, :], PS[:, 6, m * N:(m + 1) * N], b0[:, m:m + 1], 0.0,
                                                ALU.add, ALU.min)
                    ins.then_inc(g, 1)
                    dve.wait_ge(g, k + 3)
                    dve.tensor_scalar(gEa[:, :, :], gEb[:, :, :], -1.0, None, ALU.add).then_inc(g, 1)
                    dve.wait_ge(g, k + 4)
                    for m in range(2):
                        ins = dve.scalar_tensor_tensor(out=gout[:, m, :], in0=PS[:, 6, m * N:(m + 1) * N],
                                                       scalar=b0[:, m:m + 1], in1=gEa[:, m, :],
                                                       op0=ALU.add, op1=ALU.max)
                    ins.then_inc(g, 1)
                    dve.wait_ge(g, k + 6)
                    dve.tensor_copy(gfeat[:, :, :], PS[:, 6:8, 0:WX]).then_inc(g, 1)
                    heads(start, PRE_STEPS + H * HEAD_STEPS + MID_STEPS, b)
                    k = start + (PRE_STEPS + 2 * H * HEAD_STEPS + MID_STEPS)
                    dve.wait_ge(g, k)
                    dve.tensor_tensor(gout[:, :, :], gout[:, :, :], b1[:, :].unsqueeze(1).to_broadcast([P, 2, C]),
                                      ALU.add).then_inc(g, 1)
                    dve.wait_ge(g, k + 1)
                    dve.tensor_scalar(gEa[:, :, :], gout[:, :, :], 0.0, None, ALU.min).then_inc(g, 1)
                    dve.wait_ge(g, k + 3)
                    dve.tensor_scalar(gEa[:, :, :], gEb[:, :, :], -1.0, None, ALU.add).then_inc(g, 1)
                    dve.wait_ge(g, k + 4)
                    dve.tensor_tensor(z[h][:, bass.ds(b * (2 * C), 2 * C)].rearrange("p (a c) -> p a c", a=2),
                                      gEa[:, :, :], gout[:, :, :], ALU.max).then_inc(g, 1)
                dve.wait_ge(g, 1 + 2 * BATCH_STEPS)

            def graph_check(h):
                dve.wait_ge(bad_counted, h + 1)
                dve.tensor_scalar(flag[:, h:h + 1], PS[:, 3, 0:1], 1.0, None, ALU.min).then_inc(flag_ready, 1)
                dve.wait_ge(flag_ready, h + 1)
                r = dve.value_load(flag[0:1, h:h + 1], min_val=0, max_val=1)
                with dve.If(r):
                    general_path(h)
                add_graph(h)

            def normalise(t, tiles, at, n):
                stats(xr[:, t:t + tiles, :], n, tiles)
                for i in range(tiles):
                    ins = dve.tensor_scalar(xn[:, at + i, :], xr[:, t + i, :], mv[:, i, 0:1], rstd[:, i:i + 1],
                                            ALU.subtract, ALU.mult)
                return ins

            def norm_ffn(h):
                if h == 1:
                    dve.wait_ge(xnT_done, 1)
                normalise(h * HT, HT, 0, LN["norm_ffn", h]).then_inc(xn_ready, 1)

            def ffn_up(h, it):
                n = h * IT + it
                M = min(P, INTER - it * P)
                dve.wait_ge(ffn_tanh, n + 1)
                own(dve.scalar_tensor_tensor(out=wbuf[0:M, n % 2, :], in0=th[0:M, n % 2, :], scalar=1.0,
                                             in1=PS[0:M, n % 2, :], op0=ALU.add, op1=ALU.mult))
                dve.wait_ge(ffn_u_done, n + 1)
                if h == 1:
                    dve.wait_ge(down_done, 1)
                dve.scalar_tensor_tensor(out=hT[0:M, it, :], in0=wbuf[0:M, n % 2, :], scalar=cgu[0:M, it:it + 1],
                                         in1=PS[0:M, 2 + n % 2, :], op0=ALU.mult, op1=ALU.mult)\
                   .then_inc(ffn_h_ready, 1)

            def ffn_down(p):
                t, n = PARTS[p]
                bank = 4 + (t % HT) // 2
                y = z[t // HT][:, 0:n * C]
                xp = xr[:, t:t + n, :].rearrange("p t c -> p (t c)")
                dve.wait_ge(down_done, p + 1)
                dve.tensor_tensor(y.rearrange("p (t c) -> p t c", t=n),
                                  PS[:, bank:bank + n // 2, :].rearrange("p b (t c) -> p (b t) c", t=2),
                                  dsr[:, :].unsqueeze(1).to_broadcast([P, n, C]), ALU.mult).then_inc(down_read, 1)
                dve.wait_ge(down_read, p + 1)
                own(dve.tensor_tensor(xp, xp, y, ALU.add))

            def attn(p):
                t, n = PARTS[p]
                while rounds_done[0] < ROUNDS * HT // 2 * (t // HT + 1):
                    search(1)
                stats(xr[:, t:t + n, :], LN["attn", p], n)
                own(dve.tensor_scalar(rs[:, 0, 0:n], rstd[:, 0:n], cc[:, 2:3], None, ALU.mult))
                dve.scalar_tensor_tensor(out=rs[:, 1, 0:n], in0=mv[:, 0:n, 0], scalar=-1.0, in1=rs[:, 0, 0:n],
                                         op0=ALU.mult, op1=ALU.mult)
                own(dve.tensor_scalar(rs[:, 2, 0:n], rs[:, 0, 0:n], 1.0, None, ALU.add))
                for i in range(n):
                    ins = dve.tensor_scalar(xr[:, t + i, :], xr[:, t + i, :], rs[:, 2, i:i + 1],
                                            rs[:, 1, i:i + 1], ALU.mult, ALU.add)
                own(ins)
                dve.wait_ge(a2T_done, t // HT + 1)
                xp = xr[:, t:t + n, :].rearrange("p t c -> p (t c)")
                bank = 6 + (t % HT) // 2
                dve.scalar_tensor_tensor(out=xp, in0=PS[:, bank:bank + n // 2, :].rearrange("p b c -> p (b c)"),
                                         scalar=cc[:, 3:4], in1=xp, op0=ALU.mult, op1=ALU.add)\
                   .then_inc(x3_ready, 1)
                dve.wait_ge(x3_ready, p + 1)

            def norm_moe(p):
                t, n = PARTS[p]
                if p == 0:
                    dve.wait_ge(xnT_done, XT["turn_ffn", 1] + 1)
                else:
                    dve.wait_ge(rows_stored, 16)
                    dve.wait_ge(xnT_done, XT["turn_moe", 0] + 1)
                normalise(t, n, t % HT, LN["norm_moe", p]).then_inc(xn_ready, 1)

            def choices(p):
                t0, n = PARTS[p]
                dve.wait_ge(scores_done, p + 1)
                dve.tensor_copy(sc[:, t0:t0 + n, :], PS[:, TURN_BANK[p], 0:n * E].rearrange("p (t e) -> p t e", t=n))\
                   .then_inc(scores_read, 1)
                dve.wait_ge(scores_read, p + 1)
                for t in range(t0, t0 + n):
                    ins = dve.max(out=mx8[:, t, :], in_=sc[:, t, :])
                own(ins)
                for t in range(t0, t0 + n):
                    ins = dve.max_index(out=ix8[:, t, :], in_max=mx8[:, t, :], in_values=sc[:, t, :])
                own(ins)

            steps = dict(graph_hot=graph_hot, graph_hidden=graph_hidden, graph_feat=graph_feat,
                         graph_elu=graph_elu, graph_check=graph_check, norm_ffn=norm_ffn, ffn_up=ffn_up,
                         ffn_down=ffn_down, attn=attn, norm_moe=norm_moe, choices=choices)
            for stage in SCHEDULE:
                name, *at = stage
                if name in steps:
                    steps[name](*at)
                search(FILL.get(stage, 0))

            own(dve.tensor_copy(idxf[:, :, :], ix8[:, :, 0:2]))
            by_choice = lambda ap: ap.rearrange("p t k -> p k t").unsqueeze(3).to_broadcast([P, 2, T, E])
            flat4 = lambda a: a[:, :, :, :].rearrange("p k t e -> p (k t e)")
            both = lambda a: a.unsqueeze(1).to_broadcast([P, 2, T, E])
            for k in range(2):
                ins = dve.tensor_tensor(O[:, k], iota_e[:, :].unsqueeze(1).to_broadcast([P, T, E]),
                                        idxf[:, :, k].unsqueeze(2).to_broadcast([P, T, E]), ALU.is_equal)
            own(ins)
            dve.tensor_tensor(Os[:, :, :].rearrange("p e t -> p t e"), O[:, 0], O[:, 1], ALU.add)\
               .then_inc(onehots_ready, 1)
            for k in range(2):
                ins = dve.tensor_tensor(Dk[:, k], mx8[:, :, k].unsqueeze(2).to_broadcast([P, T, E]), sc[:, :, :],
                                        ALU.subtract)
            own(ins)
            dve.tensor_scalar(flat4(Dk), flat4(Dk), 0.0, None, ALU.max).then_inc(d_ready, 1)
            own(dve.scalar_tensor_tensor(out=ab[:, :, :], in0=sc[:, :, :], scalar=-1.0, in1=sc[:, :, :],
                                         op0=ALU.mult, op1=ALU.max))
            for k in range(2):
                ins = dve.tensor_tensor(Fk[:, k], mx8[:, :, k].unsqueeze(2).to_broadcast([P, T, E]), ab[:, :, :],
                                        ALU.max)
            own(ins)
            own(dve.scalar_tensor_tensor(out=flat4(Fk), in0=flat4(Fk), scalar=0.02, in1=flat4(Dk),
                                         op0=ALU.mult, op1=ALU.is_ge))
            own(dve.scalar_tensor_tensor(out=Fk[:, 1], in0=O[:, 0], scalar=0.5, in1=Fk[:, 1],
                                         op0=ALU.is_lt, op1=ALU.mult))
            dve.wait_ge(count_done, 1)
            own(dve.tensor_tensor_scan(run[:, :, :].rearrange("p e t -> p (e t)"),
                                       same_e[:, :, :].rearrange("p e t -> p (e t)"),
                                       PS[:, 4, 0:E * T], 0.0, ALU.mult, ALU.add))
            own(dve.tensor_tensor(nb[:, :, :], run[:, :, T - 1].unsqueeze(2).to_broadcast([P, E, E]),
                                  iota_q[:, :].unsqueeze(1).to_broadcast([P, E, E]), ALU.is_gt))
            own(dve.tensor_reduce(nblk[:, :], nb[:, :, :], AX.X, ALU.add))
            own(dve.tensor_tensor_scan(incl[:, :], one8[:, :], nblk[:, :], 0.0, ALU.mult, ALU.add))
            own(dve.tensor_tensor(base[:, :], incl[:, :], nblk[:, :], ALU.subtract))
            own(dve.tensor_tensor(run[:, :, :].rearrange("p e t -> p (e t)"),
                                  run[:, :, :].rearrange("p e t -> p (e t)"), PS[:, 4, 0:E * T], ALU.subtract))
            own(dve.scalar_tensor_tensor(out=run[:, :, :], in0=base[:, :].unsqueeze(2).to_broadcast([P, E, T]),
                                         scalar=float(P), in1=run[:, :, :], op0=ALU.mult, op1=ALU.add))
            dve.wait_ge(rank_done, 1)
            own(dve.tensor_tensor(run[:, :, :].rearrange("p e t -> p (e t)"),
                                  run[:, :, :].rearrange("p e t -> p (e t)"), PS[:, 5, 0:E * T], ALU.add))
            for k in range(2):
                ins = dve.tensor_tensor(O[:, k], O[:, k], run[:, :, :].rearrange("p e t -> p t e"), ALU.mult)
            own(ins)
            own(dve.tensor_reduce(slf[:, :], O[:, :, :, :].rearrange("p k t e -> p (k t) e"), AX.X, ALU.add))
            own(dve.tensor_copy(sli[:, :], slf[:, :]))
            dve.tensor_scalar(sji[:, :], sli[:, :], 7, None, ALU.logical_shift_right)
            own(dve.tensor_scalar(spi[:, :], sli[:, :], P - 1, None, ALU.bitwise_and))
            dve.tensor_copy(sjf[:, :], sji[:, :])
            own(dve.tensor_copy(spf[:, :], spi[:, :]))
            own(dve.tensor_tensor(RH[:, :, 0:NL], iota_b[:, :].unsqueeze(1).to_broadcast([P, 2 * T, NL]),
                                  sjf[:, :].unsqueeze(2).to_broadcast([P, 2 * T, NL]), ALU.is_equal))
            dve.wait_ge(ek_ready, 1)
            own(dve.tensor_tensor(flat4(Ek), flat4(Ek), flat4(Fk), ALU.mult))
            own(dve.tensor_reduce(mk[:, :], Ek[:, :, :, :].rearrange("p k t e -> p (k t) e"), AX.X, ALU.add))
            own(dve.reciprocal(mk[:, :], mk[:, :]))
            own(dve.tensor_scalar(mk[:, :], mk[:, :], tg[:, 3:4], 0.5, ALU.mult, ALU.mult))
            dve.tensor_tensor(RH[:, :, NL:2 * NL], RH[:, :, 0:NL],
                              mk[:, :].unsqueeze(2).to_broadcast([P, 2 * T, NL]), ALU.mult)
            dve.tensor_tensor(RH[:, :, 0:NL], RH[:, :, 0:NL],
                              token[:, :].unsqueeze(2).to_broadcast([P, 2 * T, NL]), ALU.mult).then_inc(rh_ready, 1)
            for n in range(0, 2 * T, 4):
                dve.tensor_tensor(places[:, n:n + 4, :], iota_p[:, :].unsqueeze(1).to_broadcast([P, 4, P]),
                                  spf[:, n:n + 4].unsqueeze(2).to_broadcast([P, 4, P]), ALU.is_equal)\
                   .then_inc(ph_ready, 1)
            own(dve.tensor_tensor(ecmp[:, :, :], iota_b[:, :].unsqueeze(2).to_broadcast([P, NL, E]),
                                  incl[:, :].unsqueeze(1).to_broadcast([P, NL, E]), ALU.is_ge))
            own(dve.tensor_reduce(eblk[:, :], ecmp[:, :, :], AX.X, ALU.add))
            dve.tensor_scalar(eoff[:, :], eblk[:, :], float(E - 1), 1024.0, ALU.min, ALU.mult).then_inc(eoff_ready, 1)
            own(dve.tensor_copy(blocks[:, 0:1], incl[:, E - 1:E]))
            dve.tensor_scalar(blocks[:, 1:2], blocks[:, 0:1], 1, None, ALU.logical_shift_right)\
               .then_inc(blocks_ready, 1)
            dve.wait_ge(list_done, 1)
            own(dve.tensor_scalar(lst[:, :], PS[:, 6, 0:NL], 0.5, float(PAD), ALU.is_lt, ALU.mult))
            dve.scalar_tensor_tensor(out=idsu[:, :], in0=PS[:, 6, 0:NL], scalar=-1.0, in1=lst[:, :],
                                     op0=ALU.add, op1=ALU.add).then_inc(list_ready, 1)
            dve.tensor_copy(coef[:, :], PS[:, 6, NL:2 * NL]).then_inc(coef_ready, 1)

            def gate(j, me):
                dve.wait_ge(silu_tanh, j + 1)
                dve.scalar_tensor_tensor(out=wbuf[:, me, :], in0=th[:, me, :], scalar=1.0, in1=PS[:, me, :],
                                         op0=ALU.add, op1=ALU.mult).then_inc(w_ready, 1)
                dve.wait_ge(w_ready, j + 1)
                dve.wait_ge(up3_done, j + 1)
                dve.tensor_tensor(hh[me], wbuf[:, me, :], PS[:, 2 + me, :], ALU.mult).then_inc(gated, 1)

            gate(0, 0)

            def pair(i, first=False):
                for q in range(2):
                    j = i * 2 + (1 + q)
                    if q or not first:
                        dve.wait_ge(hhT_done, j - 1)
                    gate(j, (q + 1) % 2)

            pair(0, first=True)
            with dve.Fori(1, pairs_in_use(dve)) as i:
                pair(i)

        @block.tensor
        def _(pe):
            def sims(h):
                pe.wait_ge(qk_loaded, 48)
                for n, w in ((0, wq), (1, wk)):
                    for q in range(2):
                        pe.matmul(PS[0:D, 2 * n + q, :], w[:, :], ctxT[:, q * 512:(q + 1) * 512],
                                  start=True, stop=True).then_inc(qk_done, 1)
                pe.wait_ge(qk_copied, 4)
                for t in range(T):
                    b = t // 2
                    mm = pe.matmul(PS[:, t // 2, (t % 2) * N:(t % 2 + 1) * N], qk[0:D, t * P:(t + 1) * P],
                                   zb[0:D, b * N:(b + 1) * N], start=True, stop=True)
                    if t % 2:
                        mm.then_inc(sim_done, 1)

            def logits(h):
                pe.wait_ge(logits_loaded, 48)
                pe.wait_ge(sim_copied, 2)
                for k in range(2):
                    pe.matmul(PS[0:D, 0, 0:2 * H], w0T[:, k, :], avec[:, 0, k, :], start=(k == 0), stop=(k == 1))
                for f in range(2):
                    for k in range(2):
                        mm = pe.matmul(PS[:, 0, (f + 1) * 2 * H:(f + 2) * 2 * H], w1T[:, k, f * P:(f + 1) * P],
                                       avec[:, 1, k, :], start=(k == 0), stop=(k == 1))
                mm.then_inc(wa_done, 1)
                pe.wait_ge(wa_copied, 1)
                for t in range(T):
                    mm = pe.matmul(PS[:, 1, t * 2 * H:(t + 1) * 2 * H], ctxT[:, t * P:(t + 1) * P],
                                   w0x[:, H * FO:WX], start=True, stop=True)
                mm.then_inc(st0_done, 1)

            def graph_hot(h):
                for b in range(2):
                    pe.wait_ge(hot_ready, HT * h + 2 * b + 2)
                    for m in range(2):
                        for n in range(2):
                            mm = pe.transpose(PS[:, BANK[h] + b, m * 256 + n * P:m * 256 + (n + 1) * P],
                                              hot[h][:, 2 * b + n, m * P:(m + 1) * P], ident[:, :])
                    mm.then_inc(hotT_done, 1)

            def graph_first(h):
                pe.wait_ge(ctx_loaded, 16)
                pe.wait_ge(hotT_copied, 2 * h + 2)
                for b in range(2):
                    for m in range(2):
                        mm = pe.matmul(PS[0:D, BANK[h], b * 256:(b + 1) * 256], ctx_s[:, h * HT + 2 * b + m, :],
                                       hotT[h][:, b, m, :], start=(m == 0), stop=(m == 1))
                mm.then_inc(g0_done, 1)

            def graph_hidden(h):
                pe.wait_ge(g0_copied, h + 1)
                for k in range(2):
                    mm = pe.matmul(PS[:, BANK[h] + k, :], w0x[:, k * P:(k + 1) * P], g0T[h][:, :], start=True, stop=True)
                mm.then_inc(h0_done, 1)

            def graph_feat(h):
                pe.wait_ge(h0_ready, h + 1)
                for i in range(HT):
                    if i >= 2:
                        pe.wait_ge(feat_copied, HT * h + i - 1)
                    for k in range(2):
                        mm = pe.matmul(PS[:, BANK[h] + i % 2, 0:WX], h0T[h][:, k, i * P:(i + 1) * P], w1x[:, k, :],
                                       start=(k == 0), stop=(k == 1))
                    mm.then_inc(feat_done, 1)

            def graph_out(h):
                pe.wait_ge(feat_copied, HT * (h + 1))
                for i in range(HT):
                    b, n = i // 2, i % 2
                    for m in range(2):
                        mm = pe.matmul(PS[:, BANK[h] + b, n * 256:(n + 1) * 256],
                                       hotT[h][:, b, m, n * P:(n + 1) * P],
                                       feat[h][:, 2 * b + m, 0:H * FO], start=(m == 0), stop=False)
                    mm = pe.matmul(PS[:, BANK[h] + b, n * 256:(n + 1) * 256], ones[0:1, :], b1[0:1, :],
                                   start=False, stop=True)
                mm.then_inc(out1_done, 1)

            def general_path(h):
                g = general[h]

                def heads(start, at):
                    with pe.Fori(0, H) as hd:
                        k = start + hd * HEAD_STEPS + at
                        pe.wait_ge(g, k + 1)
                        for m in range(2):
                            mm = pe.matmul(PS[:, 6, m * P:(m + 1) * P], ones[:, :], gD[:, m, :], start=True, stop=True)
                        mm.then_inc(g, 1)
                        pe.wait_ge(g, k + 8)
                        for m in range(2):
                            for n in range(2):
                                mm = pe.transpose(PS[:, 7, m * 256 + n * P:m * 256 + (n + 1) * P],
                                                  gEa[:, n, m * P:(m + 1) * P], ident[:, :])
                        mm.then_inc(g, 1)
                        pe.wait_ge(g, k + 10)
                        for n in range(2):
                            for m in range(2):
                                mm = pe.matmul(PS[:, 6, n * FO:(n + 1) * FO], gEb[:, m, n * P:(n + 1) * P],
                                               gfeat[:, m, bass.ds(hd * FO, FO)], start=(m == 0), stop=(m == 1))
                        mm.then_inc(g, 1)

                with pe.Fori(0, 2) as b:
                    start = b * BATCH_STEPS + 1
                    pe.wait_ge(g, start + 1)
                    for m in range(2):
                        mm = pe.matmul(PS[:, 6 + m, 0:WX], gctxT[:, m * P:(m + 1) * P], w0x[:, :],
                                       start=True, stop=True)
                    mm.then_inc(g, 1)
                    heads(start, PRE_STEPS)
                    k = start + (PRE_STEPS + H * HEAD_STEPS)
                    pe.wait_ge(g, k)
                    for m in range(2):
                        for n in range(2):
                            mm = pe.transpose(PS[:, 6, m * 256 + n * P:m * 256 + (n + 1) * P],
                                              gout[:, n, m * P:(m + 1) * P], ident[:, :])
                    mm.then_inc(g, 1)
                    pe.wait_ge(g, k + 5)
                    for m in range(2):
                        for kk in range(2):
                            mm = pe.matmul(PS[:, 6 + m, 0:WX], gout[:, kk, m * P:(m + 1) * P], w1x[:, kk, :],
                                           start=(kk == 0), stop=(kk == 1))
                    mm.then_inc(g, 1)
                    heads(start, PRE_STEPS + H * HEAD_STEPS + MID_STEPS)
                pe.wait_ge(g, 1 + 2 * BATCH_STEPS)

            def graph_check(h):
                pe.wait_ge(good_ready, h + 1)
                pe.wait_ge(sim_copied, 4)
                pe.matmul(PS[:, 3, 0:1], ones[:, :], gmin[:, h, 1:2], start=True, stop=True).then_inc(bad_counted, 1)
                if h == 1:
                    pe.wait_ge(xnT_copied, 1)
                pe.wait_ge(flag_ready, h + 1)
                r = pe.value_load(flag[0:1, h:h + 1], min_val=0, max_val=1)
                with pe.If(r):
                    general_path(h)

            def turn_tokens(n, bank, at, tiles):
                pe.wait_ge(xn_ready, n + 1)
                for i in range(tiles):
                    for k in range(2):
                        mm = pe.transpose(PS[:, bank + k, i * P:(i + 1) * P], xn[:, at + i, k * P:(k + 1) * P],
                                          ident[:, :])
                mm.then_inc(xnT_done, 1)

            def turn_ffn(h):
                turn_tokens(XT["turn_ffn", h], 6, 0, HT)
                if h == 0:
                    pe.wait_ge(ffn_loaded, 16 * 7)

            def ffn_up(h, it):
                n = h * IT + it
                M = min(P, INTER - it * P)
                if n >= 2:
                    pe.wait_ge(ffn_h_ready, n - 1)
                if it == 0:
                    pe.wait_ge(xnT_copied, XT["turn_ffn", h] + 1)
                for w, bank, ready in ((gw, n % 2, ffn_g_done), (uw, 2 + n % 2, ffn_u_done)):
                    for k in range(2):
                        mm = pe.matmul(PS[0:M, bank, :], w[:, k, it * P:it * P + M], xnT[:, h, k, :],
                                       start=(k == 0), stop=(k == 1))
                    mm.then_inc(ready, 1)

            def ffn_down(p):
                t, n = PARTS[p]
                pe.wait_ge(ffn_h_ready, IT * (t // HT + 1))
                if p == 1:
                    pe.wait_ge(down_read, 1)
                for i in range(t % HT, t % HT + n):
                    for it in range(IT):
                        K = min(P, INTER - it * P)
                        mm = pe.matmul(PS[:, 4 + i // 2, (i % 2) * 256:(i % 2 + 1) * 256],
                                       hT[0:K, it, i * P:(i + 1) * P], dw[0:K, it, :],
                                       start=(it == 0), stop=(it == IT - 1))
                mm.then_inc(down_done, 1)

            def kept(h):
                pe.wait_ge(xnT_copied, XT["turn_ffn", 1] + 1)
                if h == 1:
                    pe.wait_ge(scores_read, 1)
                pe.wait_ge(a2_ready, HT * (h + 1))
                for b in range(2):
                    pe.matmul(PS[:, 6 + b, :], ident[:, :],
                              a2[:, h * HT + 2 * b:h * HT + 2 * b + 2, :].rearrange("p t n -> p (t n)"),
                              start=True, stop=False, skip_group_check=True)
                    for m in range(2):
                        for n in range(2):
                            mm = pe.matmul(PS[:, 6 + b, m * 256 + n * P:m * 256 + (n + 1) * P],
                                           a2[:, h * HT + 2 * b + n, m * P:(m + 1) * P], ident[:, :],
                                           start=False, stop=(m == 1 and n == 1), skip_group_check=True)
                mm.then_inc(a2T_done, 1)

            def turn_moe(p):
                t, n = PARTS[p]
                turn_tokens(XT["turn_moe", p], TURN_BANK[p], t % HT, n)

            def router(p):
                t, n = PARTS[p]
                pe.wait_ge(xnT_copied, XT["turn_moe", p] + 1)
                pe.wait_ge(router_loaded, 16)
                for i in range(n):
                    at = (t % HT + i) * P
                    for k in range(2):
                        mm = pe.matmul(PS[:, TURN_BANK[p], i * E:(i + 1) * E], xnT[:, t // HT, k, at:at + P],
                                       rg[:, k, :], start=(k == 0), stop=(k == 1))
                mm.then_inc(scores_done, 1)

            steps = dict(sims=sims, logits=logits, graph_hot=graph_hot, graph_first=graph_first,
                         graph_hidden=graph_hidden, graph_feat=graph_feat, graph_out=graph_out,
                         graph_check=graph_check, turn_ffn=turn_ffn, ffn_up=ffn_up, ffn_down=ffn_down, kept=kept,
                         turn_moe=turn_moe, router=router)
            pe.wait_ge(consts, CONSTS)
            for name, *at in SCHEDULE:
                if name in steps:
                    steps[name](*at)

            pe.wait_ge(onehots_ready, 1)
            pe.wait_ge(down_read, len(PARTS))
            Os_flat = Os[:, :, :].rearrange("p e t -> p (e t)")
            pe.matmul(PS[:, 4, 0:E * T], ones[:, :], Os_flat, start=True, stop=True).then_inc(count_done, 1)
            pe.matmul(PS[:, 5, 0:E * T], before[:, :], Os_flat, start=True, stop=True).then_inc(rank_done, 1)
            pe.wait_ge(rh_ready, 1)
            for n in range(2 * T):
                if n % 4 == 0:
                    pe.wait_ge(ph_ready, n // 4 + 1)
                mm = pe.matmul(PS[:, 6, 0:2 * NL], places[:, n, :], RH[:, n, :], start=(n == 0), stop=(n == 2 * T - 1))
            mm.then_inc(list_done, 1)

            def turn_x(j, q):
                for k in range(2):
                    mm = pe.transpose(PS[:, 4, q * 256 + k * P:q * 256 + (k + 1) * P], xg[q][:, k * P:(k + 1) * P],
                                      ident[:, :])
                mm.then_inc(xgT_done, 1)

            def up(w, bank, q, at, ready):
                for k in range(2):
                    mm = pe.matmul(PS[:, bank + q, :], xgT[q][:, k, :], w[:, bass.ds(at + k * F, F)],
                                   start=(k == 0), stop=(k == 1))
                mm.then_inc(ready, 1)

            def turn_h(j, q):
                pe.wait_ge(gated, j + 1)
                for k in range(4):
                    mm = pe.transpose(PS[:, 5, k * P:(k + 1) * P], hh[q][:, k * P:(k + 1) * P], ident[:, :])
                mm.then_inc(hhT_done, 1)

            def down(j, q, at):
                pe.wait_ge(hhT_copied, j + 1)
                for k in range(4):
                    mm = pe.matmul(PS[:, 6 + q, 0:C], hhT[q][:, k * P:(k + 1) * P],
                                   e2[:, bass.ds(at + k * C, C)], start=(k == 0), stop=(k == 3))
                mm.then_inc(y_done, 1)

            def expert(j):
                return pe.value_load(eoff[0:1, bass.ds(j, 1)], min_val=0, max_val=(E - 1) * 1024)

            pe.wait_ge(eoff_ready, 1)
            pe.wait_ge(rank_done, 1)
            pe.wait_ge(list_ready, 1)
            pe.wait_ge(experts_loaded, 16 * 3 * E)
            pe.wait_ge(gathered[0], 16)
            turn_x(0, 0)
            pe.wait_ge(xgT_copied, 1)
            at = expert(0)
            up(e1, 0, 0, at, up1_done)
            pe.wait_ge(gathered[1], 16)
            turn_x(1, 1)
            up(e3, 2, 0, at, up3_done)

            def pair(i, first=False):
                for q in range(2):
                    j = i * 2 + (1 + q)
                    me, other = (q + 1) % 2, q
                    at = expert(j)
                    pe.wait_ge(xgT_copied, j + 1)
                    if q or not first:
                        pe.wait_ge(gated, j - 1)
                    up(e1, 0, me, at, up1_done)
                    if q or not first:
                        pe.wait_ge(hhT_copied, j - 1)
                    turn_h(j - 1, other)
                    pe.wait_ge(gathered[other], i * 16 + 32)
                    turn_x(j + 1, other)
                    up(e3, 2, me, at, up3_done)
                    last = expert(j - 1)
                    if not first:
                        pe.wait_ge(y_scaled, j - 2)
                    down(j - 1, other, last)

            pair(0, first=True)
            pairs = pairs_in_use(pe)
            with pe.Fori(1, pairs) as i:
                pair(i)
            pe.wait_ge(hhT_copied, pairs * 2)
            turn_h(pairs * 2, 0)
            pe.wait_ge(y_scaled, pairs * 2)
            down(pairs * 2, 0, expert(pairs * 2))


_OUT = "out_0_dram"


def kernel(**inputs):
    import numpy as np
    import concourse.bacc as bacc
    from concourse.bass_utils import run_bass_kernel_spmd as run

    i = {k: np.asarray(v) for k, v in inputs.items()}
    pad = IT * P - INTER

    def columns(v):
        return np.concatenate([v, np.zeros(pad, v.dtype)]).reshape(IT, P).T

    def by_head(layer):
        a = np.zeros((H, FO, 2, H), i["L0_xattn_a_self0"].dtype)
        for n, name in enumerate(("self", "neigh")):
            for h in range(H):
                a[h, :, n, h] = i[f"L0_xattn_a_{name}{layer}"][h]
        return a.reshape(H * FO, 2 * H)

    def expert(w, k):
        e, n, kp = w.shape
        return w.reshape(e, n, k, P).transpose(0, 3, 2, 1).reshape(e, P, k * n)

    arrays = {
        "x_in": i["x"].reshape(B * N, C),
        "ctx_in": i["ctx_512"].reshape(B * N, D),
        "ctxT_in": i["ctx_512"].reshape(B * N, D).T,
        "g_xattn": i["g_xattn"], "g_ffn": i["g_ffn"], "gamma": i["L1_xattn_gamma_raw"].reshape(1),
        "w0_in": i["L0_xattn_W0"].transpose(1, 0, 2).reshape(D, H * FO),
        "w0T_in": i["L0_xattn_W0"].transpose(0, 2, 1).reshape(H * FO, D),
        "b0_in": i["L0_xattn_b0"].reshape(2, P).T,
        "w1_in": i["L0_xattn_W1"].transpose(1, 0, 2).reshape(C, H * FO),
        "w1T_in": i["L0_xattn_W1"].transpose(0, 2, 1).reshape(H * FO, C),
        "a_in": np.stack([by_head("0"), by_head("1")]), "b1_in": i["L0_xattn_b1"],
        "gw_in": i["L0_ffn_gate_w"].T, "uw_in": i["L0_ffn_up_w"].T, "dw_in": i["L0_ffn_down_w"].T,
        "gs_in": columns(i["L0_ffn_gate_s"]), "us_in": columns(i["L0_ffn_up_s"]), "ds_in": i["L0_ffn_down_s"],
        "wq_in": i["L1_xattn_Wq"].T, "wk_in": i["L1_xattn_Wk"].T, "rg_in": i["L1_ffn_gate_w"].T,
        "e1_in": expert(i["L1_ffn_w1"], 2), "e3_in": expert(i["L1_ffn_w3"], 2),
        "e2_in": expert(i["L1_ffn_w2"], 4),
    }
    arrays = {k: np.ascontiguousarray(v) for k, v in arrays.items()}
    nc = bacc.Bacc("TRN2", target_bir_lowering=False, num_devices=1)
    args = [nc.dram_tensor(k, v.shape, mybir.dt.from_np(v.dtype), kind="ExternalInput").ap()
            for k, v in arrays.items()]
    args.append(nc.dram_tensor(_OUT, [B * N, C], F32, kind="ExternalOutput").ap())
    build(nc, *args)
    r = run(nc, [arrays], core_ids=[0])
    return r.results[0][_OUT].reshape(B, N, C)
```

```python
from contextlib import ExitStack

import concourse.bass as bass
from concourse import mybir

F32, I32, U32, BF16 = mybir.dt.float32, mybir.dt.int32, mybir.dt.uint32, mybir.dt.bfloat16
ALU = mybir.AluOpType
ACT = mybir.ActivationFunctionType
AX = mybir.AxisListType

P = 128
B, N, C = 4, 256, 256
T = B * N // P
D = 64
H, FO = 8, 32
WX = H * FO + 2 * H
INTER = 704
IT = -(-INTER // P)
E, F = 8, 512
TOPK = max(1, int(N * 0.3))
ROUNDS = -(-TOPK // 8)
GUESS, AIM, SLOPES = 0.524, TOPK - 9, (100.0, 140.0)
HUGE = 2.0 ** 100
SLOTS = 2 * B * N
NB = SLOTS // P + E - 1
NL = NB + 2
PAIRS_MIN, PAIRS_MAX = SLOTS // P // 2, (NB - 1) // 2
PAD = 4096
HT = T // 2
HN = HT * P
EPS = 1e-5
BIG = 1e10
LEAD, ULPS, LOGIT = 2e4, 2.0 ** -21, 2000.0


def rows(ap):
    n = 1
    for s in ap.shape:
        n *= s
    flat = ap if len(ap.shape) == 1 else ap.rearrange("a b -> (a b)")
    return flat.rearrange("(a n) -> a n", a=1).to_broadcast([P, n])


def build(nc, x_in, ctx_in, ctxT_in, g_xattn, g_ffn, gamma, w0_in, w0T_in, b0_in, w1_in, w1T_in, a_in, b1_in,
          gw_in, uw_in, dw_in, gs_in, us_in, ds_in, wq_in, wk_in, rg_in, e1_in, e3_in, e2_in,
          out, force_general=False):
    xn3_dram = nc.dram_tensor("xn3_rows", [B * N, C], F32, kind="Internal").ap()
    ctx = ExitStack()
    with ctx:
        def sb(name, shape, dt=F32):
            return ctx.enter_context(nc.sbuf_tensor(name, shape, dt))

        def sem(name):
            return ctx.enter_context(nc.semaphore(name))

        PS = ctx.enter_context(nc.psum_tensor("PS", [P, 8, 512], F32))

        ident = sb("ident", [P, P])
        ones = sb("ones", [P, P])
        before = sb("before", [P, P])
        iota_p = sb("iota_p", [P, P])
        iota_e = sb("iota_e", [P, E])
        iota_q = sb("iota_q", [P, E])
        iota_b = sb("iota_b", [P, NL])
        token = sb("token", [P, 2, 2 * T])
        nhalf = sb("nhalf", [P, HT])
        x = sb("x", [P, T, C])
        ctx_s = sb("ctx_s", [P, T, D])
        ctxT = sb("ctxT", [D, B * N])
        w0x = sb("w0x", [D, WX])
        w1x = sb("w1x", [P, 2, WX])
        b0 = sb("b0", [P, 2])
        b1x = sb("b1x", [P, WX])
        b1 = b1x[:, 0:C]
        gates = sb("gates", [P, 5])
        tg = sb("tg", [P, 5])
        cc = sb("cc", [P, 4])
        e1 = sb("e1", [P, E * 1024])
        e3 = sb("e3", [P, E * 1024])
        e2 = sb("e2", [P, E * 1024])
        gw = e1[:, 5 * 1024:5 * 1024 + 2 * INTER].rearrange("p (k n) -> p k n", k=2)
        uw = e3[:, 5 * 1024:5 * 1024 + 2 * INTER].rearrange("p (k n) -> p k n", k=2)
        dw = e2[:, 5 * 1024:5 * 1024 + IT * C].rearrange("p (k n) -> p k n", k=IT)
        gs = sb("gs", [P, IT])
        us = sb("us", [P, IT])
        hgs = sb("hgs", [P, IT])
        cgu = sb("cgu", [P, IT])
        dsr = sb("dsr", [P, C])
        wq = sb("wq", [D, D])
        wk = sb("wk", [D, D])
        rg = sb("rg", [P, 2, E])
        xr = x
        at = (7 * 1024, 3 * 1024)
        mask = [e1[:, a:a + 1024].rearrange("p (t c) -> p t c", t=HT) for a in (7 * 1024, 4 * 1024)]
        hot = [e3[:, a:a + 1024].rearrange("p (t c) -> p t c", t=HT) for a in at]
        hotT = [e2[:, a:a + 1024].rearrange("p (b m c) -> p b m c", b=2, m=2) for a in at]
        g0T = [sb("g0T", [D, HN]), e3[0:D, 4 * 1024:4 * 1024 + HN]]
        h0T = [sb("h0T", [P, 2, HN]), e2[:, 4 * 1024:5 * 1024].rearrange("p (k n) -> p k n", k=2)]
        feat = [sb("feat", [P, HT, WX]),
                e1[:, 2 * 1024:2 * 1024 + HT * WX].rearrange("p (t c) -> p t c", t=HT)]
        st0 = sb("st0", [P, T, 2 * H])
        zb = sb("zb", [P, HT * C])
        zc = sb("zc", [P, HT * C])
        xn = sb("xn", [P, HT, C])
        xnT = sb("xnT", [P, 2, 2, HN])
        th = sb("th", [P, 2, F])
        wbuf = sb("wbuf", [P, 2, F])
        hT = sb("hT", [P, IT, HN])
        w0T = wbuf[:, 0, 0:2 * D].rearrange("p (k n) -> p k n", k=2)
        avec = wbuf[:, 0, 2 * D:2 * D + 4 * 2 * H].rearrange("p (l k n) -> p l k n", l=2, k=2)
        w1T = wbuf[:, 1, :].rearrange("p (k n) -> p k n", k=2)
        z = [zb, zc]
        sim = sb("sim", [P, T, N])
        work = sb("work", [P, 2, N])
        a2 = sb("a2", [P, T, N])
        row_stat = sb("row_stat", [P, T, 6])
        row_mv = sb("row_mv", [P, T, 2])
        row_dev = sb("row_dev", [P, T])
        half_power = sb("half_power", [P, T])
        guess = sb("guess", [P, T])
        bar = sb("bar", [P, 4, T])
        signs = sb("signs", [P, T])
        step = sb("step", [P, T])
        above = sb("above", [P, T])
        top16 = sb("top16", [P, T, 16])
        found = sb("found", [P, 2, T])
        top8 = sb("top8", [P, 8])
        rs = sb("rs", [P, 3, HT])
        stat = sb("stat", [P, HT, 6])
        mv = sb("mv", [P, HT, 2])
        veps = sb("veps", [P, HT])
        rstd = sb("rstd", [P, HT])
        top = sb("top", [P, HT, 8])
        lead = sb("lead", [P, 2, HT])
        good = sb("good", [P, 2, HT + 2 * HT * 2 * H])
        gsm = sb("gsm", [P, 2 * HT * 2 * H])
        gmin = sb("gmin", [P, 2, 2])
        flag = sb("flag", [P, 3], I32)
        gctxT = sb("gctxT", [D, N])
        gfeat = feat[0][:, 0:2, :]
        gD = sb("gD", [P, 2, P])
        gEa = h0T[0][:, 0, :].rearrange("p (a n) -> p a n", a=2)
        gEb = h0T[0][:, 1, :].rearrange("p (a n) -> p a n", a=2)
        gnm = sb("gnm", [P, 2])
        gsum = sb("gsum", [P, 2])
        grs = sb("grs", [P, 2])
        gout = feat[0][:, 2:4, 0:C]
        sc = sb("sc", [P, T, E])
        mx8 = sb("mx8", [P, T, 8])
        ix8 = sb("ix8", [P, T, 8], U32)
        idxf = sb("idxf", [P, T, 2])
        O = sb("O", [P, 2, T, E])
        Os = sb("Os", [P, E, T])
        Dk = sb("Dk", [P, 2, T, E])
        Fk = sb("Fk", [P, 2, T, E])
        second = sb("second", [P, T, E])
        Ek = sb("Ek", [P, 2, T, E])
        ab = sb("ab", [P, T, E])
        mk = sb("mk", [P, 2 * T])
        nb = sb("nb", [P, E, E])
        nblk = sb("nblk", [P, E])
        incl = sb("incl", [P, E])
        base = sb("base", [P, E])
        one8 = sb("one8", [P, E])
        ecmp = sb("ecmp", [P, NL, E])
        which = ecmp[:, 0:T * 16 // E, :].rearrange("p a b -> p (a b)").rearrange("p (t n) -> p t n", t=T)
        eblk = sb("eblk", [P, NL])
        eoff = sb("eoff", [P, NL], I32)
        blocks = sb("blocks", [P, 2], I32)
        run = sb("run", [P, E, T])
        same_e = sb("same_e", [P, E, T])
        slf = sb("slf", [P, 2 * T])
        sli = sb("sli", [P, 2 * T], I32)
        sji = sb("sji", [P, 2 * T], I32)
        spi = sb("spi", [P, 2 * T], I32)
        sjf = sb("sjf", [P, 2 * T])
        spf = sb("spf", [P, 2 * T])
        RH = sb("RH", [P, 6, 2 * T, NL], BF16)
        places = sb("places", [P, 2 * T, P], BF16)
        parts = sb("parts", [P, 3, 2 * T], BF16)
        rest = sb("rest", [P, 2 * T])
        lst = sb("lst", [P, NL])
        tokens = sb("tokens", [P, NL])
        idsu = sb("idsu", [P, NL], U32)
        coef = sb("coef", [P, NL])
        gidx = [sb(f"gidx{q}", [P, 1], U32) for q in range(2)]
        sidx = [sb(f"sidx{q}", [P, 1], U32) for q in range(2)]
        xg = [zc[:, q * C:(q + 1) * C] for q in range(2)]
        hh = [hT[:, q, :] for q in range(2)]
        hhT = [hT[:, 2 + q, :] for q in range(2)]
        yv = [hT[:, 4, q * C:(q + 1) * C] for q in range(2)]
        xgT = [hT[:, 5, q * C:(q + 1) * C].rearrange("p (k n) -> p k n", k=2) for q in range(2)]

        x_loaded = [sem(f"x_loaded{h}") for h in range(2)]
        ctx_loaded = sem("ctx_loaded")
        qk_loaded = sem("qk_loaded")
        gates_loaded = sem("gates_loaded")
        logits_loaded = sem("logits_loaded")
        gat_loaded = sem("gat_loaded")
        ffn_loaded = sem("ffn_loaded")
        router_loaded = sem("router_loaded")
        experts_loaded = sem("experts_loaded")
        consts = sem("consts")
        gates_tanh = sem("gates_tanh")
        dve_done = sem("dve_done")
        act_done = sem("act_done")
        pool_done = sem("pool_done")
        pool_passed = sem("pool_passed")
        var_ready = sem("var_ready")
        rstd_ready = sem("rstd_ready")
        qk_done = sem("qk_done")
        qk_copied = sem("qk_copied")
        sim_done = sem("sim_done")
        sim_copied = sem("sim_copied")
        sig_ready = sem("sig_ready")
        row_var_ready = sem("row_var_ready")
        row_dev_ready = sem("row_dev_ready")
        guess_ready = sem("guess_ready")
        row_counted = sem("row_counted")
        found_ready = sem("found_ready")
        lost_counted = sem("lost_counted")
        lost_ready = sem("lost_ready")
        full_search = sem("full_search")
        a2_ready = sem("a2_ready")
        a2T_done = sem("a2T_done")
        x3_ready = sem("x3_ready")
        wa_done = sem("wa_done")
        wa_copied = sem("wa_copied")
        scales_ready = sem("scales_ready")
        st0_done = sem("st0_done")
        st0_copied = sem("st0_copied")
        hot_ready = sem("hot_ready")
        hotT_done = sem("hotT_done")
        hotT_copied = sem("hotT_copied")
        g0_done = sem("g0_done")
        g0_copied = sem("g0_copied")
        h0_done = sem("h0_done")
        h0_exp = sem("h0_exp")
        h0_ready = sem("h0_ready")
        feat_done = sem("feat_done")
        feat_ready = sem("feat_ready")
        out1_done = sem("out1_done")
        out1_read = sem("out1_read")
        out1_exp = sem("out1_exp")
        good_ready = sem("good_ready")
        graph_over = sem("graph_over")
        bad_counted = sem("bad_counted")
        flag_ready = sem("flag_ready")
        general = [sem(f"general{h}") for h in range(2)]
        xn_ready = sem("xn_ready")
        xnT_done = sem("xnT_done")
        xnT_copied = sem("xnT_copied")
        ffn_g_done = sem("ffn_g_done")
        ffn_u_done = sem("ffn_u_done")
        ffn_tanh = sem("ffn_tanh")
        ffn_h_ready = sem("ffn_h_ready")
        down_done = sem("down_done")
        down_read = sem("down_read")
        rows_stored = sem("rows_stored")
        out_stored = sem("out_stored")
        scores_done = sem("scores_done")
        scores_read = sem("scores_read")
        d_ready = sem("d_ready")
        ek_ready = sem("ek_ready")
        onehots_ready = sem("onehots_ready")
        count_done = sem("count_done")
        rank_done = sem("rank_done")
        rh_ready = sem("rh_ready")
        ph_ready = sem("ph_ready")
        eoff_ready = sem("eoff_ready")
        blocks_ready = sem("blocks_ready")
        list_done = sem("list_done")
        list_ready = sem("list_ready")
        coef_ready = sem("coef_ready")
        gidx_set = sem("gidx_set")
        gathered = [sem(f"gathered{q}") for q in range(2)]
        xgT_done = sem("xgT_done")
        xgT_copied = sem("xgT_copied")
        up1_done = sem("up1_done")
        up3_done = sem("up3_done")
        silu_tanh = sem("silu_tanh")
        w_ready = sem("w_ready")
        gated = sem("gated")
        hhT_done = sem("hhT_done")
        hhT_copied = sem("hhT_copied")
        y_done = sem("y_done")
        y_scaled = sem("y_scaled")
        sidx_set = sem("sidx_set")
        scattered = [sem(f"scattered{q}") for q in range(2)]

        CONSTS = 15
        BANK = (6, 4)
        WARM_UP, WARM_UP_FFN = 14, 8
        PARTS = ((0, HT), (HT, HT // 2), (HT + HT // 2, HT // 2))
        TURN_BANK = (6, 0, 2)
        SCHEDULE = [("pick", 0), ("queries", 0), ("pick", 1), ("graph_hot", 0), ("graph_first", 0),
                    ("graph_hidden", 0), ("hidden_elu", 0), ("sims", 0), ("graph_hot", 1), ("logits", 0),
                    ("graph_first", 1), ("spread", 0), ("scales", 0), ("graph_feat", 0), ("count", 0),
                    ("graph_hidden", 1), ("logit_check", 0), ("hidden_elu", 1), ("graph_out", 0), ("move", 1),
                    ("graph_feat", 1), ("count", 1), ("graph_elu", 0), ("move", 2), ("logit_check", 1),
                    ("graph_out", 1), ("graph_check", 0), ("norm_ffn", 0), ("sigmoids", 0), ("graph_elu", 1),
                    ("turn_ffn", 0), ("graph_check", 1), ("ffn_up", 0, 0), ("ffn_up", 0, 1), ("norm_ffn", 1),
                    ("ffn_up", 0, 2), ("ffn_up", 0, 3), ("ffn_up", 0, 4), ("turn_ffn", 1), ("ffn_up", 0, 5),
                    ("lost", 0), ("keep", 0), ("keep", 1), ("ffn_down", 0), ("kept", 0), ("ffn_up", 1, 0),
                    ("attn_stats", 0), ("ffn_up", 1, 1), ("attn", 0), ("moe_stats", 0), ("norm_moe", 0),
                    ("ffn_up", 1, 2), ("ffn_up", 1, 3), ("choices", 0), ("turn_moe", 0), ("ffn_up", 1, 4),
                    ("router", 0), ("ffn_up", 1, 5), ("kept", 1), ("ffn_down", 1), ("attn_stats", 1),
                    ("ffn_down", 2), ("attn_stats", 2), ("attn", 1), ("attn", 2), ("moe_stats", 1),
                    ("moe_stats", 2), ("norm_moe", 1), ("turn_moe", 1), ("turn_moe", 2), ("norm_moe", 2),
                    ("router", 1), ("router", 2), ("choices", 1), ("choices", 2)]
        order = lambda names: {stage: n for n, stage in enumerate(s for s in SCHEDULE if s[0] in names)}
        LN = order(("pick", "norm_ffn", "attn_stats", "moe_stats"))
        XT = order(("turn_ffn", "turn_moe"))

        HEAD_STEPS = 12
        PRE_STEPS, MID_STEPS, POST_STEPS = 3, 7, 5
        BATCH_STEPS = PRE_STEPS + MID_STEPS + POST_STEPS + 2 * H * HEAD_STEPS

        def pairs_in_use(engine):
            engine.wait_ge(blocks_ready, 1)
            return engine.value_load(blocks[0:1, 1:2], min_val=PAIRS_MIN, max_val=PAIRS_MAX)

        block = ctx.enter_context(nc.Block())

        @block.sync
        def _(sp):
            xv = x_in.rearrange("(t p) c -> p t c", p=P)
            sp.dma_start(x[:, 0:HT, :], xv[:, 0:HT, :]).then_inc(x_loaded[0], 16)
            sp.dma_start(ctxT[:, :], ctxT_in).then_inc(qk_loaded, 16)
            sp.dma_start(ctx_s[:, :, :], ctx_in.rearrange("(t p) d -> p t d", p=P)).then_inc(ctx_loaded, 16)
            sp.dma_start(w0x[:, 0:H * FO], w0_in).then_inc(gat_loaded, 16)
            sp.dma_start(w1x[:, :, 0:H * FO], w1_in.rearrange("(k p) n -> p k n", p=P)).then_inc(gat_loaded, 16)
            sp.dma_start(b0[:, :], b0_in).then_inc(gat_loaded, 16)
            sp.dma_start(b1, rows(b1_in)).then_inc(gat_loaded, 16)
            sp.dma_start(x[:, HT:T, :], xv[:, HT:T, :]).then_inc(x_loaded[1], 16)
            full = INTER // P
            for w, src in ((gw, gw_in), (uw, uw_in)):
                sp.dma_start(w[:, :, :], src.rearrange("(k p) n -> p k n", p=P)).then_inc(ffn_loaded, 16)
            for v, src in ((gs, gs_in), (us, us_in)):
                sp.dma_start(v[:, :], src).then_inc(ffn_loaded, 16)
            sp.dma_start(dw[:, 0:full, :], dw_in[0:full * P, :].rearrange("(k p) n -> p k n", p=P))\
              .then_inc(ffn_loaded, 16)
            sp.dma_start(dw[0:INTER - full * P, full, :], dw_in[full * P:INTER, :]).then_inc(ffn_loaded, 16)
            sp.dma_start(dsr[:, :], rows(ds_in)).then_inc(ffn_loaded, 16)
            sp.dma_start(rg[:, :, :], rg_in.rearrange("(k p) n -> p k n", p=P)).then_inc(router_loaded, 16)
            def load_expert(e):
                for w, src in ((e1, e1_in), (e3, e3_in), (e2, e2_in)):
                    sp.dma_start(w[:, e * 1024:(e + 1) * 1024], src[e]).then_inc(experts_loaded, 16)

            for e in range(2):
                load_expert(e)
            sp.wait_ge(graph_over, 2)
            for e in (2, 3, 4, 7):
                load_expert(e)
            for p, (t, n) in enumerate(PARTS):
                if p == 1:
                    sp.wait_ge(down_done, len(PARTS))
                    load_expert(5)
                    load_expert(6)
                sp.wait_ge(x3_ready, p + 1)
                sp.dma_start(out.rearrange("(t p) c -> p t c", p=P)[:, t:t + n, :],
                             xr[:, t:t + n, :]).then_inc(out_stored, 16)
                sp.wait_ge(xn_ready, XT["turn_moe", p] + 1)
                sp.dma_start(xn3_dram.rearrange("(t p) c -> p t c", p=P)[:, t:t + n, :],
                             xn[:, t % HT:t % HT + n, :]).then_inc(rows_stored, 16)
            sp.wait_ge(out_stored, 16 * len(PARTS))
            sp.wait_ge(rows_stored, 16 * len(PARTS))

        @block.gpsimd
        def _(pool):
            done = [0]

            def own(ins):
                done[0] += 1
                ins.then_inc(pool_done, 1)
                pool.wait_ge(pool_done, done[0])

            pool.memset(ones[:, :], 1.0).then_inc(consts, 1)
            pool.memset(nhalf[:, :], -0.5).then_inc(consts, 1)
            pool.memset(one8[:, :], 1.0).then_inc(consts, 1)
            own(pool.memset(ident[:, :], 0.0))
            pool.affine_select(out=ident[:, :], in_=ident[:, :], compare_op=ALU.not_equal, fill=1.0,
                               base=0, pattern=[[-1, P]], channel_multiplier=1).then_inc(consts, 1)
            own(pool.memset(before[:, :], 1.0))
            pool.affine_select(out=before[:, :], in_=before[:, :], compare_op=ALU.is_gt, fill=0.0,
                               base=0, pattern=[[1, P]], channel_multiplier=-1).then_inc(consts, 1)
            small = dict(allow_small_or_imprecise_dtypes=True)
            pool.iota(iota_p[:, :], [[1, P]], base=0, channel_multiplier=0, **small).then_inc(consts, 1)
            pool.iota(iota_e[:, :], [[1, E]], base=0, channel_multiplier=0, **small).then_inc(consts, 1)
            pool.iota(iota_q[:, :], [[P, E]], base=0, channel_multiplier=0, **small).then_inc(consts, 1)
            pool.iota(iota_b[:, :], [[1, NL]], base=0, channel_multiplier=0, **small).then_inc(consts, 1)
            own(pool.memset(same_e[:, :, :], 1.0))
            pool.memset(same_e[:, :, 0], 0.0).then_inc(consts, 1)
            pool.iota(token[:, 0, :], [[0, 2], [1, T]], base=1, channel_multiplier=0, **small).then_inc(consts, 1)
            pool.iota(token[:, 1, :], [[0, 2 * T]], base=0, channel_multiplier=1, **small).then_inc(consts, 1)
            pool.memset(zc[:, 0:2 * C], 0.0).then_inc(consts, 1)
            pool.memset(half_power[:, :], 0.5).then_inc(consts, 1)
            pool.memset(b1x[:, C:WX], 0.0).then_inc(consts, 1)
            pool.wait_ge(consts, CONSTS)
            for (name, i), n in LN.items():
                if (name, i) == ("norm_ffn", 0):
                    pool.wait_ge(row_var_ready, 1)
                    pool.tensor_tensor(row_dev[:, :], row_mv[:, :, 1], half_power[:, :], ALU.pow)\
                        .then_inc(row_dev_ready, 1)
                first, tiles = (PARTS[i][0] % HT, PARTS[i][1]) if name in ("attn_stats", "moe_stats") else (0, HT)
                pool.wait_ge(var_ready, n + 1)
                pool.tensor_tensor(rstd[:, first:first + tiles], veps[:, first:first + tiles],
                                   nhalf[:, 0:tiles], ALU.pow).then_inc(rstd_ready, 1)

            def gather(j, q):
                pool.tensor_copy(gidx[q][:, :], idsu[:, bass.ds(j, 1)]).then_inc(gidx_set, 1)
                pool.wait_ge(gidx_set, j + 1)
                pool.sem_inc(pool_passed)
                pool.indirect_dma_start(
                    out=xg[q], out_offset=None, in_=xn3_dram,
                    in_offset=bass.IndirectOffsetOnAxis(ap=gidx[q][:, 0:1], axis=0),
                    bounds_check=bound, oob_is_err=False).then_inc(gathered[q], 16)

            def scatter(j, q):
                pool.tensor_copy(sidx[q][:, :], idsu[:, bass.ds(j, 1)]).then_inc(sidx_set, 1)
                pool.wait_ge(sidx_set, j + 1)
                pool.wait_ge(y_scaled, j + 1)
                pool.sem_inc(pool_passed)
                pool.indirect_dma_start(
                    out=out, out_offset=bass.IndirectOffsetOnAxis(ap=sidx[q][:, 0:1], axis=0),
                    in_=yv[q], in_offset=None,
                    bounds_check=bound, oob_is_err=False, compute_op=ALU.add).then_inc(scattered[q], 16)

            bound = pool.to_reg(B * N - 1)
            pool.wait_ge(list_ready, 1)
            pool.wait_ge(rows_stored, 16 * len(PARTS))
            pool.wait_ge(out_stored, 16 * len(PARTS))
            gather(0, 0)
            gather(1, 1)
            pool.wait_ge(xgT_done, 1)
            pool.wait_ge(gathered[0], 16)
            gather(2, 0)

            def pair(i, first=False):
                j = i * 2 + 1
                pool.wait_ge(xgT_done, j + 1)
                pool.wait_ge(gathered[1], i * 16 + 16)
                gather(j + 2, 1)
                if not first:
                    pool.wait_ge(scattered[1], i * 16)
                scatter(j - 1, 0)
                pool.wait_ge(xgT_done, j + 2)
                pool.wait_ge(gathered[0], i * 16 + 32)
                gather(j + 3, 0)
                pool.wait_ge(scattered[0], i * 16 + 16)
                scatter(j, 1)

            pair(0, first=True)
            pairs = pairs_in_use(pool)
            with pool.Fori(1, pairs) as i:
                pair(i)
            pool.wait_ge(scattered[1], pairs * 16)
            scatter(pairs * 2, 0)
            pool.wait_ge(scattered[0], pairs * 16 + 16)
            pool.wait_ge(gathered[0], pairs * 16 + 32)

        @block.scalar
        def _(act):
            copy = ACT.Copy

            act.dma_start(wq[:, :], wq_in).then_inc(qk_loaded, 16)
            act.dma_start(wk[:, :], wk_in).then_inc(qk_loaded, 16)
            act.dma_start(gates[:, 0:2], rows(g_xattn)).then_inc(gates_loaded, 16)
            act.dma_start(gates[:, 2:4], rows(g_ffn)).then_inc(gates_loaded, 16)
            act.dma_start(gates[:, 4:5], rows(gamma)).then_inc(gates_loaded, 16)
            act.dma_start(avec, a_in.rearrange("l (k p) n -> p l k n", p=P)).then_inc(logits_loaded, 16)
            act.dma_start(w0T, w0T_in.rearrange("(k p) n -> p k n", p=P)).then_inc(logits_loaded, 16)
            act.dma_start(w1T, w1T_in.rearrange("(k p) n -> p k n", p=P)).then_inc(logits_loaded, 16)
            act.wait_ge(gates_loaded, 48)
            act.activation(tg[:, 0:4], gates[:, 0:4], ACT.Tanh)
            act.activation(tg[:, 4:5], gates[:, 4:5], ACT.Tanh, scale=0.5).then_inc(gates_tanh, 1)

            def queries(h):
                for q in range(2):
                    act.wait_ge(qk_done, q + 1)
                    act.activation(th[0:D, q, :], PS[0:D, q, :], copy).then_inc(qk_copied, 1)
                for q in range(2):
                    act.wait_ge(qk_done, q + 3)
                    act.activation(hT[0:D, q, :], PS[0:D, 2 + q, :], copy).then_inc(qk_copied, 1)

            def sims(h):
                for q in range(4):
                    act.wait_ge(sim_done, q + 1)
                    act.activation(sim[:, 2 * q:2 * q + 2, :], PS[:, q, :].rearrange("p (a n) -> p a n", a=2),
                                   copy, scale=1.0 / 16.0).then_inc(sim_copied, 1)

            def logits(h):
                act.wait_ge(wa_done, 1)
                act.activation(w0x[:, H * FO:WX], PS[0:D, 0, 0:2 * H], copy)
                act.activation(w1x[:, :, H * FO:WX], PS[:, 0, 2 * H:6 * H].rearrange("p (k n) -> p k n", k=2),
                               copy).then_inc(wa_copied, 1)
                act.wait_ge(st0_done, 1)
                act.activation(st0[:, :, :], PS[:, 1, 0:T * 2 * H].rearrange("p (t n) -> p t n", t=T),
                               copy).then_inc(st0_copied, 1)

            def count(n):
                act.wait_ge(guess_ready, n + 1)
                for t in range(T):
                    ins = act.activation(a2[:, t, :], sim[:, t, :], ACT.Sign, bias=bar[:, n, t:t + 1],
                                         accum_out=signs[:, t:t + 1])
                ins.then_inc(row_counted, 1)

            def sigmoids(h):
                act.wait_ge(row_counted, 2)
                act.activation(a2[:, :, :], sim[:, :, :], ACT.Tanh, scale=0.5).then_inc(act_done, 1)
                act.wait_ge(act_done, 1)
                act.activation(a2[:, :, :], a2[:, :, :], copy, bias=1.0).then_inc(sig_ready, 1)

            def graph_hot(h):
                for b in range(2):
                    act.wait_ge(hotT_done, 2 * h + b + 1)
                    act.activation(hotT[h][:, b, :, :], PS[:, BANK[h] + b, :].rearrange("p (m n) -> p m n", m=2),
                                   copy).then_inc(hotT_copied, 1)

            def graph_first(h):
                act.wait_ge(g0_done, h + 1)
                act.activation(g0T[h][:, :], PS[0:D, BANK[h], :], copy).then_inc(g0_copied, 1)

            def graph_hidden(h):
                act.wait_ge(gat_loaded, 16 * 4)
                act.wait_ge(h0_done, h + 1)
                for k in range(2):
                    ins = act.activation(z[h][:, k * HN:(k + 1) * HN], PS[:, BANK[h] + k, :], ACT.Exp,
                                         bias=b0[:, k:k + 1])
                ins.then_inc(h0_exp, 1)

            def graph_out(h):
                act.wait_ge(out1_done, h + 1)
                act.activation(z[h][:, :], PS[:, BANK[h]:BANK[h] + 2, :].rearrange("p b n -> p (b n)"),
                               ACT.Exp).then_inc(out1_exp, 1)

            def general_path(h):
                sem_g = general[h]
                with act.Fori(0, 2) as b:
                    start = b * BATCH_STEPS + 1
                    for at in (PRE_STEPS, PRE_STEPS + H * HEAD_STEPS + MID_STEPS):
                        with act.Fori(0, H) as hd:
                            act.wait_ge(sem_g, start + hd * HEAD_STEPS + (at + 6))
                            act.activation(gEa[:, 0, :], gEb[:, 0, :], ACT.Exp, bias=gnm[:, 0:1],
                                           accum_out=gsum[:, 0:1])
                            act.activation(gEa[:, 1, :], gEb[:, 1, :], ACT.Exp, bias=gnm[:, 1:2],
                                           accum_out=gsum[:, 1:2]).then_inc(sem_g, 1)
                        act.wait_ge(sem_g, start + (at + H * HEAD_STEPS + 2))
                        act.activation(gEb[:, :, :], gEa[:, :, :], ACT.Exp).then_inc(sem_g, 1)
                act.wait_ge(sem_g, 1 + 2 * BATCH_STEPS)

            def graph_check(h):
                act.wait_ge(flag_ready, h + 1)
                r = act.value_load(flag[0:1, h:h + 1], min_val=0, max_val=1)
                with act.If(r):
                    general_path(h)

            def turn_ffn(h):
                act.wait_ge(xnT_done, XT["turn_ffn", h] + 1)
                act.activation(xnT[:, h, :, :], PS[:, 6:8, :], copy).then_inc(xnT_copied, 1)

            def turn_moe(p):
                t, n = PARTS[p]
                bank, at = TURN_BANK[p], (t % HT) * P
                act.wait_ge(xnT_done, XT["turn_moe", p] + 1)
                act.wait_ge(ffn_u_done, IT * (t // HT + 1))
                act.activation(xnT[:, t // HT, :, at:at + n * P], PS[:, bank:bank + 2, 0:n * P], copy)\
                   .then_inc(xnT_copied, 1)

            def ffn_up(h, it):
                n = h * IT + it
                M = min(P, INTER - it * P)
                act.wait_ge(ffn_g_done, n + 1)
                if n == 0:
                    act.wait_ge(scales_ready, 1)
                if n >= 2:
                    act.wait_ge(ffn_h_ready, n - 1)
                act.activation(th[0:M, n % 2, :], PS[0:M, n % 2, :], ACT.Tanh,
                               scale=hgs[0:M, it:it + 1]).then_inc(ffn_tanh, 1)

            steps = dict(queries=queries, sims=sims, count=count, logits=logits, sigmoids=sigmoids,
                         graph_hot=graph_hot, graph_first=graph_first, graph_hidden=graph_hidden, graph_out=graph_out,
                         graph_check=graph_check, turn_ffn=turn_ffn, ffn_up=ffn_up, turn_moe=turn_moe)
            for name, *at in SCHEDULE:
                if name in steps:
                    steps[name](*at)
            act.wait_ge(d_ready, 1)
            act.activation(Ek[:, :, :, :].rearrange("p k t e -> p (k t e)"),
                           Dk[:, :, :, :].rearrange("p k t e -> p (k t e)"), ACT.Exp, scale=-1.0)\
               .then_inc(ek_ready, 1)

            def copy_xgT(j, q):
                act.wait_ge(xgT_done, j + 1)
                act.activation(xgT[q], PS[:, 4, q * 256:(q + 1) * 256].rearrange("p (k n) -> p k n", k=2),
                               copy).then_inc(xgT_copied, 1)

            def silu(j, q):
                act.wait_ge(up1_done, j + 1)
                act.activation(th[:, q, :], PS[:, q, :], ACT.Tanh, scale=0.5).then_inc(silu_tanh, 1)

            def copy_hhT(j, q):
                act.wait_ge(hhT_done, j + 1)
                act.activation(hhT[q], PS[:, 5, :], copy).then_inc(hhT_copied, 1)

            def scale_y(j, q):
                act.wait_ge(y_done, j + 1)
                act.wait_ge(coef_ready, 1)
                act.activation(yv[q], PS[:, 6 + q, 0:C], copy,
                               scale=coef[:, bass.ds(j, 1)]).then_inc(y_scaled, 1)

            copy_xgT(0, 0)
            silu(0, 0)
            copy_xgT(1, 1)

            def pair(i, first=False):
                for q in range(2):
                    j = i * 2 + (1 + q)
                    me, other = (q + 1) % 2, q
                    if q or not first:
                        act.wait_ge(gated, j - 1)
                    silu(j, me)
                    copy_hhT(j - 1, other)
                    act.wait_ge(up3_done, j)
                    copy_xgT(j + 1, other)
                    if not first:
                        act.wait_ge(scattered[other], i * 16)
                    scale_y(j - 1, other)

            pair(0, first=True)
            pairs = pairs_in_use(act)
            with act.Fori(1, pairs) as i:
                pair(i)
            copy_hhT(pairs * 2, 0)
            act.wait_ge(scattered[0], pairs * 16)
            scale_y(pairs * 2, 0)

        @block.vector
        def _(dve):
            done = [0]

            def own(ins):
                done[0] += 1
                ins.then_inc(dve_done, 1)
                dve.wait_ge(dve_done, done[0])

            def mark(ins):
                done[0] += 1
                ins.then_inc(dve_done, 1)
                return done[0]

            def after(n):
                dve.wait_ge(dve_done, n)

            def stats(src, tiles=HT, at=0):
                for i in range(tiles):
                    ins = dve.bn_stats(stat[:, at + i, :], src[:, i, :])
                own(ins)
                for i in range(tiles):
                    ins = dve.bn_aggr(mv[:, at + i, :], stat[:, at + i, :])
                own(ins)
                dve.tensor_scalar(veps[:, at:at + tiles], mv[:, at:at + tiles, 1], EPS, None, ALU.add)\
                   .then_inc(var_ready, 1)

            def deviations(n):
                search(FILL.get(("deviation", n), 0))
                dve.wait_ge(rstd_ready, n + 1)

            FILL = {("move", 2): 3, ("deviation", LN["norm_ffn", 0]): 1, ("graph_check", 1): 6,
                    ("ffn_up", 0, 0): 4, ("ffn_up", 0, 1): 2, ("ffn_up", 0, 2): 2, ("ffn_up", 0, 3): 4,
                    ("ffn_up", 0, 4): 5, ("ffn_up", 0, 5): 3, ("ffn_up", 1, 5): 1}

            def half(t, h):
                return t[:, h * HT:(h + 1) * HT, :]

            def spread(h):
                dve.wait_ge(sim_copied, 4)
                for t in range(T):
                    ins = dve.bn_stats(row_stat[:, t, :], sim[:, t, :])
                own(ins)
                for t in range(T):
                    ins = dve.bn_aggr(row_mv[:, t, :], row_stat[:, t, :])
                ins.then_inc(row_var_ready, 1)
                dve.wait_ge(row_dev_ready, 1)
                own(dve.scalar_tensor_tensor(out=guess[:, :], in0=row_dev[:, :], scalar=-GUESS, in1=row_mv[:, :, 0],
                                             op0=ALU.mult, op1=ALU.subtract))
                dve.tensor_copy(bar[:, 0, :], guess[:, :]).then_inc(guess_ready, 1)

            def move(n):
                dve.wait_ge(row_counted, n)
                own(dve.tensor_scalar(step[:, :], signs[:, :], 0.5 / SLOPES[n - 1],
                                      (N / 2 - AIM) / SLOPES[n - 1], ALU.mult, ALU.add))
                own(dve.tensor_tensor(step[:, :], step[:, :], row_dev[:, :], ALU.mult))
                own(dve.tensor_tensor(guess[:, :], guess[:, :], step[:, :], ALU.subtract))
                dve.tensor_copy(bar[:, n, :], guess[:, :]).then_inc(guess_ready, 1)

            def below():
                own(dve.tensor_scalar(guess[:, :], guess[:, :], -1.0, None, ALU.mult))
                for t in range(0, T, 2):
                    pair = ((0, t), (1, t + 1))
                    for q, i in pair:
                        n = mark(dve.tensor_scalar(work[:, q, :], sim[:, i, :], guess[:, i:i + 1], 0.0, ALU.is_ge,
                                                   ALU.add, accum_out=above[:, i:i + 1]))
                    yield
                    after(n)
                    for q, i in pair:
                        n = mark(dve.scalar_tensor_tensor(out=work[:, q, :], in0=work[:, q, :], scalar=-HUGE,
                                                          in1=sim[:, i, :], op0=ALU.mult, op1=ALU.add))
                    yield
                    after(n)
                    for q, i in pair:
                        n = mark(dve.max(out=top16[:, i, 0:8], in_=work[:, q, :]))
                    yield
                    after(n)
                    for q, i in pair:
                        n = mark(dve.match_replace(out=work[:, q, :], in_to_replace=top16[:, i, 0:8],
                                                   in_values=work[:, q, :], imm_value=-HUGE))
                    yield
                    after(n)
                    for q, i in pair:
                        n = mark(dve.max(out=top16[:, i, 8:16], in_=work[:, q, :]))
                    yield
                    after(n)
                own(dve.tensor_scalar(above[:, :], above[:, :], -1.0, float(TOPK - 1), ALU.mult, ALU.add))
                own(dve.tensor_tensor(which[:, :, :], iota_p[:, 0:16].unsqueeze(1).to_broadcast([P, T, 16]),
                                      above[:, :].unsqueeze(2).to_broadcast([P, T, 16]), ALU.is_equal))
                own(dve.tensor_reduce(found[:, 0, :], which[:, :, :], AX.X, ALU.add))
                own(dve.tensor_tensor(which[:, :, :], which[:, :, :], top16[:, :, :], ALU.mult))
                own(dve.tensor_reduce(bar[:, 3, :], which[:, :, :], AX.X, ALU.add))
                own(dve.tensor_reduce(found[:, 1, 0:1], found[:, 0, :], AX.X, ALU.min))
                dve.tensor_scalar(found[:, 1, 1:2], found[:, 1, 0:1], -1.0, 1.0 if not force_general else 2.0,
                                  ALU.mult, ALU.add).then_inc(found_ready, 1)
                yield

            searching = below()
            STEPS = 5 * (T // 2) + 1
            steps_done = [0]

            def search(n):
                while n and steps_done[0] < STEPS:
                    next(searching)
                    steps_done[0] += 1
                    n -= 1

            def search_in_full():
                one = 2 * ROUNDS
                for t in range(T):
                    for r in range(ROUNDS):
                        src = work[:, 0, :] if r else sim[:, t, :]
                        if t or r:
                            dve.wait_ge(full_search, t * one + 2 * r)
                        dve.max(out=top8[:, :], in_=src).then_inc(full_search, 1)
                        dve.wait_ge(full_search, t * one + 2 * r + 1)
                        if r < ROUNDS - 1:
                            dve.match_replace(out=work[:, 0, :], in_to_replace=top8[:, :], in_values=src,
                                              imm_value=-HUGE).then_inc(full_search, 1)
                    k = (TOPK - 1) % 8
                    dve.tensor_copy(bar[:, 3, t:t + 1], top8[:, k:k + 1]).then_inc(full_search, 1)
                dve.wait_ge(full_search, T * one)

            def keep(h):
                if h == 0:
                    search(STEPS)
                    dve.wait_ge(lost_counted, 1)
                    dve.tensor_scalar(flag[:, 2:3], PS[:, 6, 0:1], 1.0, None, ALU.min).then_inc(lost_ready, 1)
                    dve.wait_ge(lost_ready, 1)
                    with dve.If(dve.value_load(flag[0:1, 2:3], min_val=0, max_val=1)):
                        search_in_full()
                    dve.wait_ge(sig_ready, 1)
                for t in range(h * HT, (h + 1) * HT):
                    dve.scalar_tensor_tensor(out=a2[:, t, :], in0=sim[:, t, :], scalar=bar[:, 3, t:t + 1],
                                             in1=a2[:, t, :], op0=ALU.is_ge, op1=ALU.mult).then_inc(a2_ready, 1)

            def pick(h):
                if h == 0:
                    dve.wait_ge(consts, CONSTS)
                dve.wait_ge(x_loaded[h], 16)
                stats(half(x, h))
                deviations(LN["pick", h])
                for i in range(HT):
                    ins = dve.tensor_scalar(mask[h][:, i, :], x[:, h * HT + i, :], mv[:, i, 0:1],
                                            rstd[:, i:i + 1], ALU.subtract, ALU.mult)
                own(ins)
                flat = mask[h].rearrange("p a b -> p (a b)")
                own(dve.tensor_scalar(flat, flat, 1.0, BIG, ALU.subtract, ALU.mult))
                for i in range(HT):
                    ins = dve.max(out=top[:, i, :], in_=mask[h][:, i, :])
                own(ins)
                for i in range(HT):
                    ins = dve.tensor_scalar(hot[h][:, i, :], mask[h][:, i, :], top[:, i, 0:1], None, ALU.is_ge)
                    ins.then_inc(hot_ready, 1)
                own(dve.scalar_tensor_tensor(out=lead[:, 0, :], in0=top[:, :, 0], scalar=-1.0,
                                             in1=top[:, :, 0], op0=ALU.mult, op1=ALU.max))
                dve.tensor_tensor(lead[:, 1, :], top[:, :, 0], top[:, :, 1], ALU.subtract)
                own(dve.tensor_scalar(lead[:, 0, :], lead[:, 0, :], ULPS, LEAD, ALU.mult, ALU.add))
                own(dve.tensor_tensor(good[:, h, 0:HT], lead[:, 1, :], lead[:, 0, :], ALU.is_gt))

            def scales(h):
                dve.wait_ge(gates_tanh, 1)
                own(dve.tensor_scalar(cc[:, 0:1], tg[:, 4:5], 0.5, 0.5, ALU.mult, ALU.add))
                own(dve.tensor_scalar(cc[:, 1:2], cc[:, 0:1], -1.0, 1.0, ALU.mult, ALU.add))
                own(dve.tensor_tensor(cc[:, 2:3], cc[:, 1:2], tg[:, 1:2], ALU.mult))
                own(dve.tensor_scalar(cc[:, 3:4], cc[:, 0:1], tg[:, 1:2], 0.25, ALU.mult, ALU.mult))
                dve.wait_ge(ffn_loaded, 16 * 7)
                own(dve.tensor_scalar(hgs[:, :], gs[:, :], 0.5, None, ALU.mult))
                own(dve.tensor_tensor(cgu[:, :], hgs[:, :], us[:, :], ALU.mult))
                dve.tensor_scalar(dsr[:, :], dsr[:, :], tg[:, 2:3], None, ALU.mult).then_inc(scales_ready, 1)

            def hidden_elu(h):
                dve.wait_ge(h0_exp, h + 1)
                own(dve.tensor_scalar(z[h][:, :], z[h][:, :], 1.0, 1.0, ALU.min, ALU.subtract))
                for k in range(2):
                    ins = dve.scalar_tensor_tensor(out=h0T[h][:, k, :], in0=PS[:, BANK[h] + k, :],
                                                   scalar=b0[:, k:k + 1], in1=z[h][:, k * HN:(k + 1) * HN],
                                                   op0=ALU.add, op1=ALU.max)
                ins.then_inc(h0_ready, 1)

            def graph_feat(h):
                dve.wait_ge(gat_loaded, 16 * 4)
                for i in range(HT):
                    dve.wait_ge(feat_done, HT * h + i + 1)
                    dve.tensor_tensor(feat[h][:, i, :], PS[:, BANK[h] + i % 2, 0:WX], b1x[:, :], ALU.add)\
                       .then_inc(feat_ready, 1)

            def logit_check(h):
                dve.wait_ge(feat_ready, HT * (h + 1))
                dve.wait_ge(st0_copied, 1)
                n = HT * 2 * H
                own(dve.scalar_tensor_tensor(out=gsm[:, 0:n].rearrange("p (t n) -> p t n", t=HT),
                                             in0=half(st0, h), scalar=-1.0, in1=half(st0, h),
                                             op0=ALU.mult, op1=ALU.max))
                own(dve.scalar_tensor_tensor(out=gsm[:, n:2 * n].rearrange("p (t n) -> p t n", t=HT),
                                             in0=feat[h][:, :, H * FO:WX], scalar=-1.0, in1=feat[h][:, :, H * FO:WX],
                                             op0=ALU.mult, op1=ALU.max))
                own(dve.tensor_scalar(good[:, h, HT:HT + 2 * n], gsm[:, :], LOGIT, None, ALU.is_le))
                own(dve.tensor_reduce(gmin[:, h, 0:1], good[:, h, :], AX.X, ALU.min))
                dve.tensor_scalar(gmin[:, h, 1:2], gmin[:, h, 0:1], -1.0, 1.0 if not force_general else 2.0,
                                  ALU.mult, ALU.add).then_inc(good_ready, 1)

            def graph_elu(h):
                dve.wait_ge(out1_exp, h + 1)
                own(dve.tensor_scalar(z[h][:, :], z[h][:, :], 1.0, 1.0, ALU.min, ALU.subtract))
                own(dve.tensor_tensor(z[h][:, :], PS[:, BANK[h]:BANK[h] + 2, :].rearrange("p b n -> p (b n)"),
                                      z[h][:, :], ALU.max))

            def add_graph(h):
                xh = half(xr, h).rearrange("p t c -> p (t c)")
                dve.scalar_tensor_tensor(out=xh, in0=z[h][:, :], scalar=tg[:, 0:1], in1=xh,
                                         op0=ALU.mult, op1=ALU.add).then_inc(graph_over, 1)
                dve.wait_ge(graph_over, h + 1)

            def general_path(h):
                g = general[h]
                dve.memset(gnm[:, :], 0.0).then_inc(g, 1)

                def step(at, ins):
                    ins.then_inc(g, 1)

                def heads(start, at, b):
                    with dve.Fori(0, H) as hd:
                        k = start + hd * HEAD_STEPS + at
                        dve.wait_ge(g, k)
                        for m in range(2):
                            ins = dve.tensor_scalar(gD[:, m, :], ident[:, :],
                                                    gfeat[:, m, bass.ds(hd + (H * FO + H), 1)], None, ALU.mult)
                        ins.then_inc(g, 1)
                        dve.wait_ge(g, k + 2)
                        for m in range(2):
                            ins = dve.tensor_scalar(gEa[:, m, :], PS[:, 6, 0:N],
                                                    gfeat[:, m, bass.ds(hd + H * FO, 1)], None, ALU.add)
                        ins.then_inc(g, 1)
                        dve.wait_ge(g, k + 3)
                        dve.scalar_tensor_tensor(out=gEb[:, :, :], in0=gEa[:, :, :], scalar=0.2, in1=gEa[:, :, :],
                                                 op0=ALU.mult, op1=ALU.max).then_inc(g, 1)
                        dve.wait_ge(g, k + 4)
                        dve.tensor_tensor(gEb[:, :, :].rearrange("p a b -> p (a b)"),
                                          gEb[:, :, :].rearrange("p a b -> p (a b)"),
                                          mask[h].rearrange("p a b -> p (a b)")[:, bass.ds(b * (2 * N), 2 * N)],
                                          ALU.add).then_inc(g, 1)
                        dve.wait_ge(g, k + 5)
                        dve.tensor_reduce(gnm[:, :], gEb[:, :, :], AX.X, ALU.max, negate=True).then_inc(g, 1)
                        dve.wait_ge(g, k + 7)
                        dve.reciprocal(grs[:, :], gsum[:, :]).then_inc(g, 1)
                        dve.wait_ge(g, k + 9)
                        dve.tensor_copy(gEb[:, :, :], PS[:, 7, :].rearrange("p (a b) -> p a b", a=2)).then_inc(g, 1)
                        dve.wait_ge(g, k + 11)
                        for m in range(2):
                            ins = dve.tensor_scalar(gout[:, m, bass.ds(hd * FO, FO)],
                                                    PS[:, 6, m * FO:(m + 1) * FO], grs[:, m:m + 1], None, ALU.mult)
                        ins.then_inc(g, 1)

                with dve.Fori(0, 2) as b:
                    start = b * BATCH_STEPS + 1
                    dve.wait_ge(g, start)
                    dve.tensor_copy(gctxT[:, :], ctxT[:, bass.ds(b * N + h * HN, N)]).then_inc(g, 1)
                    dve.wait_ge(g, start + 2)
                    dve.tensor_copy(gfeat[:, :, :], PS[:, 6:8, 0:WX]).then_inc(g, 1)
                    heads(start, PRE_STEPS, b)
                    k = start + (PRE_STEPS + H * HEAD_STEPS)
                    dve.wait_ge(g, k + 1)
                    for m in range(2):
                        ins = dve.tensor_scalar(gEa[:, m, :], PS[:, 6, m * N:(m + 1) * N], b0[:, m:m + 1], 0.0,
                                                ALU.add, ALU.min)
                    ins.then_inc(g, 1)
                    dve.wait_ge(g, k + 3)
                    dve.tensor_scalar(gEa[:, :, :], gEb[:, :, :], -1.0, None, ALU.add).then_inc(g, 1)
                    dve.wait_ge(g, k + 4)
                    for m in range(2):
                        ins = dve.scalar_tensor_tensor(out=gout[:, m, :], in0=PS[:, 6, m * N:(m + 1) * N],
                                                       scalar=b0[:, m:m + 1], in1=gEa[:, m, :],
                                                       op0=ALU.add, op1=ALU.max)
                    ins.then_inc(g, 1)
                    dve.wait_ge(g, k + 6)
                    dve.tensor_copy(gfeat[:, :, :], PS[:, 6:8, 0:WX]).then_inc(g, 1)
                    heads(start, PRE_STEPS + H * HEAD_STEPS + MID_STEPS, b)
                    k = start + (PRE_STEPS + 2 * H * HEAD_STEPS + MID_STEPS)
                    dve.wait_ge(g, k)
                    dve.tensor_tensor(gout[:, :, :], gout[:, :, :], b1.unsqueeze(1).to_broadcast([P, 2, C]),
                                      ALU.add).then_inc(g, 1)
                    dve.wait_ge(g, k + 1)
                    dve.tensor_scalar(gEa[:, :, :], gout[:, :, :], 0.0, None, ALU.min).then_inc(g, 1)
                    dve.wait_ge(g, k + 3)
                    dve.tensor_scalar(gEa[:, :, :], gEb[:, :, :], -1.0, None, ALU.add).then_inc(g, 1)
                    dve.wait_ge(g, k + 4)
                    dve.tensor_tensor(z[h][:, bass.ds(b * (2 * C), 2 * C)].rearrange("p (a c) -> p a c", a=2),
                                      gEa[:, :, :], gout[:, :, :], ALU.max).then_inc(g, 1)
                dve.wait_ge(g, 1 + 2 * BATCH_STEPS)

            def graph_check(h):
                dve.wait_ge(bad_counted, h + 1)
                dve.tensor_scalar(flag[:, h:h + 1], PS[:, 3, 0:1], 1.0, None, ALU.min).then_inc(flag_ready, 1)
                dve.wait_ge(flag_ready, h + 1)
                r = dve.value_load(flag[0:1, h:h + 1], min_val=0, max_val=1)
                with dve.If(r):
                    general_path(h)
                add_graph(h)

            def normalise(t, tiles):
                for i in range(t % HT, t % HT + tiles):
                    ins = dve.tensor_scalar(xn[:, i, :], xr[:, t - t % HT + i, :], mv[:, i, 0:1], rstd[:, i:i + 1],
                                            ALU.subtract, ALU.mult)
                return ins

            def norm_ffn(h):
                if h == 1:
                    dve.wait_ge(xnT_done, 1)
                stats(half(xr, h))
                deviations(LN["norm_ffn", h])
                normalise(h * HT, HT).then_inc(xn_ready, 1)

            def ffn_up(h, it):
                n = h * IT + it
                M = min(P, INTER - it * P)
                dve.wait_ge(ffn_tanh, n + 1)
                own(dve.scalar_tensor_tensor(out=wbuf[0:M, n % 2, :], in0=th[0:M, n % 2, :], scalar=1.0,
                                             in1=PS[0:M, n % 2, :], op0=ALU.add, op1=ALU.mult))
                dve.wait_ge(ffn_u_done, n + 1)
                if h == 1:
                    dve.wait_ge(down_done, 1)
                dve.scalar_tensor_tensor(out=hT[0:M, it, :], in0=wbuf[0:M, n % 2, :], scalar=cgu[0:M, it:it + 1],
                                         in1=PS[0:M, 2 + n % 2, :], op0=ALU.mult, op1=ALU.mult)\
                   .then_inc(ffn_h_ready, 1)

            def ffn_down(p):
                t, n = PARTS[p]
                bank = 4 + (t % HT) // 2
                y = z[0][:, 0:n * C]
                xp = xr[:, t:t + n, :].rearrange("p t c -> p (t c)")
                dve.wait_ge(down_done, p + 1)
                dve.tensor_tensor(y.rearrange("p (t c) -> p t c", t=n),
                                  PS[:, bank:bank + n // 2, :].rearrange("p b (t c) -> p (b t) c", t=2),
                                  dsr[:, :].unsqueeze(1).to_broadcast([P, n, C]), ALU.mult).then_inc(down_read, 1)
                dve.wait_ge(down_read, p + 1)
                own(dve.tensor_tensor(xp, xp, y, ALU.add))

            def attn_stats(p):
                t, n = PARTS[p]
                stats(xr[:, t:t + n, :], n, t % HT)

            def kept(h):
                dve.wait_ge(a2T_done, h + 1)
                own(dve.tensor_tensor(z[1][:, :], half(a2, h).rearrange("p t c -> p (t c)"),
                                      PS[:, 6:8, :].rearrange("p b c -> p (b c)"), ALU.add))

            def attn(p):
                t, n = PARTS[p]
                deviations(LN["attn_stats", p])
                cols = slice(t % HT, t % HT + n)
                own(dve.tensor_scalar(rs[:, 0, 0:n], rstd[:, cols], cc[:, 2:3], None, ALU.mult))
                dve.scalar_tensor_tensor(out=rs[:, 1, 0:n], in0=mv[:, cols, 0], scalar=-1.0, in1=rs[:, 0, 0:n],
                                         op0=ALU.mult, op1=ALU.mult)
                own(dve.tensor_scalar(rs[:, 2, 0:n], rs[:, 0, 0:n], 1.0, None, ALU.add))
                for i in range(n):
                    ins = dve.tensor_scalar(xr[:, t + i, :], xr[:, t + i, :], rs[:, 2, i:i + 1],
                                            rs[:, 1, i:i + 1], ALU.mult, ALU.add)
                own(ins)
                xp = xr[:, t:t + n, :].rearrange("p t c -> p (t c)")
                dve.scalar_tensor_tensor(out=xp, in0=z[1][:, (t % HT) * C:(t % HT + n) * C],
                                         scalar=cc[:, 3:4], in1=xp, op0=ALU.mult, op1=ALU.add)\
                   .then_inc(x3_ready, 1)
                dve.wait_ge(x3_ready, p + 1)

            def moe_stats(p):
                t, n = PARTS[p]
                stats(xr[:, t:t + n, :], n, t % HT)

            def norm_moe(p):
                t, n = PARTS[p]
                if p == 0:
                    dve.wait_ge(xnT_done, XT["turn_ffn", 1] + 1)
                else:
                    dve.wait_ge(rows_stored, 16)
                    dve.wait_ge(xnT_done, XT["turn_moe", 0] + 1)
                deviations(LN["moe_stats", p])
                normalise(t, n).then_inc(xn_ready, 1)

            def choices(p):
                t0, n = PARTS[p]
                dve.wait_ge(scores_done, p + 1)
                dve.tensor_copy(sc[:, t0:t0 + n, :], PS[:, TURN_BANK[p], 0:n * E].rearrange("p (t e) -> p t e", t=n))\
                   .then_inc(scores_read, 1)
                dve.wait_ge(scores_read, p + 1)
                for t in range(t0, t0 + n):
                    ins = dve.max(out=mx8[:, t, :], in_=sc[:, t, :])
                own(ins)
                for t in range(t0, t0 + n):
                    ins = dve.max_index(out=ix8[:, t, :], in_max=mx8[:, t, :], in_values=sc[:, t, :])
                own(ins)

            steps = dict(pick=pick, spread=spread, move=move, keep=keep, kept=kept, scales=scales,
                         hidden_elu=hidden_elu, graph_feat=graph_feat,
                         logit_check=logit_check, graph_elu=graph_elu, graph_check=graph_check, norm_ffn=norm_ffn, ffn_up=ffn_up,
                         ffn_down=ffn_down, attn_stats=attn_stats, attn=attn, moe_stats=moe_stats, norm_moe=norm_moe,
                         choices=choices)
            for stage in SCHEDULE:
                name, *at = stage
                if name in steps:
                    steps[name](*at)
                search(FILL.get(stage, 0))

            own(dve.tensor_copy(idxf[:, :, :], ix8[:, :, 0:2]))
            by_choice = lambda ap: ap.rearrange("p t k -> p k t").unsqueeze(3).to_broadcast([P, 2, T, E])
            flat4 = lambda a: a[:, :, :, :].rearrange("p k t e -> p (k t e)")
            both = lambda a: a.unsqueeze(1).to_broadcast([P, 2, T, E])
            for k in range(2):
                ins = dve.tensor_tensor(O[:, k], iota_e[:, :].unsqueeze(1).to_broadcast([P, T, E]),
                                        idxf[:, :, k].unsqueeze(2).to_broadcast([P, T, E]), ALU.is_equal)
            own(ins)
            dve.tensor_tensor(Os[:, :, :].rearrange("p e t -> p t e"), O[:, 0], O[:, 1], ALU.add)\
               .then_inc(onehots_ready, 1)
            for k in range(2):
                ins = dve.tensor_tensor(Dk[:, k], mx8[:, :, k].unsqueeze(2).to_broadcast([P, T, E]), sc[:, :, :],
                                        ALU.subtract)
            own(ins)
            dve.tensor_scalar(flat4(Dk), flat4(Dk), 0.0, None, ALU.max).then_inc(d_ready, 1)
            dve.wait_ge(d_ready, 1)
            own(dve.tensor_scalar(second[:, :, :], O[:, 0], 0.5, None, ALU.is_lt))
            dve.wait_ge(count_done, 1)
            own(dve.tensor_tensor_scan(run[:, :, :].rearrange("p e t -> p (e t)"),
                                       same_e[:, :, :].rearrange("p e t -> p (e t)"),
                                       PS[:, 4, 0:E * T], 0.0, ALU.mult, ALU.add))
            own(dve.tensor_tensor(nb[:, :, :], run[:, :, T - 1].unsqueeze(2).to_broadcast([P, E, E]),
                                  iota_q[:, :].unsqueeze(1).to_broadcast([P, E, E]), ALU.is_gt))
            own(dve.tensor_reduce(nblk[:, :], nb[:, :, :], AX.X, ALU.add))
            own(dve.tensor_tensor_scan(incl[:, :], one8[:, :], nblk[:, :], 0.0, ALU.mult, ALU.add))
            own(dve.tensor_tensor(base[:, :], incl[:, :], nblk[:, :], ALU.subtract))
            own(dve.tensor_tensor(run[:, :, :].rearrange("p e t -> p (e t)"),
                                  run[:, :, :].rearrange("p e t -> p (e t)"), PS[:, 4, 0:E * T], ALU.subtract))
            own(dve.scalar_tensor_tensor(out=run[:, :, :], in0=base[:, :].unsqueeze(2).to_broadcast([P, E, T]),
                                         scalar=float(P), in1=run[:, :, :], op0=ALU.mult, op1=ALU.add))
            dve.wait_ge(rank_done, 1)
            own(dve.tensor_tensor(run[:, :, :].rearrange("p e t -> p (e t)"),
                                  run[:, :, :].rearrange("p e t -> p (e t)"), PS[:, 5, 0:E * T], ALU.add))
            for k in range(2):
                ins = dve.tensor_tensor(O[:, k], O[:, k], run[:, :, :].rearrange("p e t -> p t e"), ALU.mult)
            own(ins)
            own(dve.tensor_reduce(slf[:, :], O[:, :, :, :].rearrange("p k t e -> p (k t) e"), AX.X, ALU.add))
            own(dve.tensor_copy(sli[:, :], slf[:, :]))
            dve.tensor_scalar(sji[:, :], sli[:, :], 7, None, ALU.logical_shift_right)
            own(dve.tensor_scalar(spi[:, :], sli[:, :], P - 1, None, ALU.bitwise_and))
            dve.tensor_copy(sjf[:, :], sji[:, :])
            own(dve.tensor_copy(spf[:, :], spi[:, :]))
            own(dve.tensor_tensor(RH[:, 0], iota_b[:, :].unsqueeze(1).to_broadcast([P, 2 * T, NL]),
                                  sjf[:, :].unsqueeze(2).to_broadcast([P, 2 * T, NL]), ALU.is_equal))
            for n in range(2):
                ins = dve.tensor_tensor(RH[:, 1 + n], RH[:, 0], token[:, n, :].unsqueeze(2).to_broadcast([P, 2 * T, NL]),
                                        ALU.mult)
            ins.then_inc(rh_ready, 1)
            for n in range(0, 2 * T, 4):
                dve.tensor_tensor(places[:, n:n + 4, :], iota_p[:, :].unsqueeze(1).to_broadcast([P, 4, P]),
                                  spf[:, n:n + 4].unsqueeze(2).to_broadcast([P, 4, P]), ALU.is_equal)\
                   .then_inc(ph_ready, 1)
            dve.wait_ge(list_done, 1)
            dve.tensor_scalar(lst[:, :], PS[:, 6, 0:NL], 0.5, float(PAD), ALU.is_lt, ALU.mult)
            own(dve.tensor_scalar(tokens[:, :], PS[:, 6, 0:NL], float(P), float(P), ALU.mult, ALU.subtract))
            own(dve.tensor_tensor(lst[:, :], lst[:, :], tokens[:, :], ALU.add))
            dve.tensor_tensor(idsu[:, :], lst[:, :], PS[:, 6, NL:2 * NL], ALU.add).then_inc(list_ready, 1)
            own(dve.tensor_tensor(ecmp[:, :, :], iota_b[:, :].unsqueeze(2).to_broadcast([P, NL, E]),
                                  incl[:, :].unsqueeze(1).to_broadcast([P, NL, E]), ALU.is_ge))
            own(dve.tensor_reduce(eblk[:, :], ecmp[:, :, :], AX.X, ALU.add))
            dve.tensor_scalar(eoff[:, :], eblk[:, :], float(E - 1), 1024.0, ALU.min, ALU.mult).then_inc(eoff_ready, 1)
            own(dve.tensor_copy(blocks[:, 0:1], incl[:, E - 1:E]))
            dve.tensor_scalar(blocks[:, 1:2], blocks[:, 0:1], 1, None, ALU.logical_shift_right)\
               .then_inc(blocks_ready, 1)
            own(dve.scalar_tensor_tensor(out=ab[:, :, :], in0=sc[:, :, :], scalar=-1.0, in1=sc[:, :, :],
                                         op0=ALU.mult, op1=ALU.max))
            for k in range(2):
                ins = dve.tensor_tensor(Fk[:, k], mx8[:, :, k].unsqueeze(2).to_broadcast([P, T, E]), ab[:, :, :],
                                        ALU.max)
            own(ins)
            own(dve.scalar_tensor_tensor(out=flat4(Fk), in0=flat4(Fk), scalar=0.02, in1=flat4(Dk),
                                         op0=ALU.mult, op1=ALU.is_ge))
            own(dve.tensor_tensor(Fk[:, 1], second[:, :, :], Fk[:, 1], ALU.mult))
            dve.wait_ge(ek_ready, 1)
            own(dve.tensor_tensor(flat4(Ek), flat4(Ek), flat4(Fk), ALU.mult))
            own(dve.tensor_reduce(mk[:, :], Ek[:, :, :, :].rearrange("p k t e -> p (k t) e"), AX.X, ALU.add))
            own(dve.reciprocal(mk[:, :], mk[:, :]))
            own(dve.tensor_scalar(mk[:, :], mk[:, :], tg[:, 3:4], 0.5, ALU.mult, ALU.mult))
            own(dve.tensor_copy(parts[:, 0, :], mk[:, :]))
            own(dve.tensor_tensor(rest[:, :], mk[:, :], parts[:, 0, :], ALU.subtract))
            own(dve.tensor_copy(parts[:, 1, :], rest[:, :]))
            own(dve.tensor_tensor(parts[:, 2, :], rest[:, :], parts[:, 1, :], ALU.subtract))
            for n in range(3):
                ins = dve.tensor_tensor(RH[:, 3 + n], RH[:, 0], parts[:, n, :].unsqueeze(2).to_broadcast([P, 2 * T, NL]),
                                        ALU.mult)
            ins.then_inc(rh_ready, 1)
            dve.wait_ge(list_done, 2)
            own(dve.tensor_copy(coef[:, :], PS[:, 7, 0:NL]))
            for n in range(1, 3):
                ins = dve.tensor_tensor(coef[:, :], coef[:, :], PS[:, 7, n * NL:(n + 1) * NL], ALU.add)
                if n == 1:
                    own(ins)
            ins.then_inc(coef_ready, 1)

            def gate(j, me):
                dve.wait_ge(silu_tanh, j + 1)
                dve.scalar_tensor_tensor(out=wbuf[:, me, :], in0=th[:, me, :], scalar=1.0, in1=PS[:, me, :],
                                         op0=ALU.add, op1=ALU.mult).then_inc(w_ready, 1)
                dve.wait_ge(w_ready, j + 1)
                dve.wait_ge(up3_done, j + 1)
                dve.tensor_tensor(hh[me], wbuf[:, me, :], PS[:, 2 + me, :], ALU.mult).then_inc(gated, 1)

            gate(0, 0)

            def pair(i, first=False):
                for q in range(2):
                    j = i * 2 + (1 + q)
                    if q or not first:
                        dve.wait_ge(hhT_done, j - 1)
                    gate(j, (q + 1) % 2)

            pair(0, first=True)
            with dve.Fori(1, pairs_in_use(dve)) as i:
                pair(i)

        @block.tensor
        def _(pe):
            def open_clock_gate(n):
                for _ in range(n):
                    pe.matmul(PS[:, 7, 0:P], ones[:, :], ident[:, :], start=True, stop=True)

            def queries(h):
                pe.wait_ge(qk_loaded, 48)
                for n, w in ((0, wq), (1, wk)):
                    for q in range(2):
                        pe.matmul(PS[0:D, 2 * n + q, :], w[:, :], ctxT[:, q * 512:(q + 1) * 512],
                                  start=True, stop=True).then_inc(qk_done, 1)

            def sims(h):
                pe.wait_ge(qk_copied, 4)
                for t in range(T):
                    b = t // 2
                    mm = pe.matmul(PS[:, t // 2, (t % 2) * N:(t % 2 + 1) * N],
                                   th[0:D, t // HT, (t % HT) * P:(t % HT + 1) * P],
                                   hT[0:D, b // 2, (b % 2) * N:(b % 2 + 1) * N], start=True, stop=True)
                    if t % 2:
                        mm.then_inc(sim_done, 1)

            def logits(h):
                pe.wait_ge(logits_loaded, 48)
                pe.wait_ge(sim_copied, 2)
                for k in range(2):
                    pe.matmul(PS[0:D, 0, 0:2 * H], w0T[:, k, :], avec[:, 0, k, :], start=(k == 0), stop=(k == 1))
                for f in range(2):
                    for k in range(2):
                        mm = pe.matmul(PS[:, 0, (f + 1) * 2 * H:(f + 2) * 2 * H], w1T[:, k, f * P:(f + 1) * P],
                                       avec[:, 1, k, :], start=(k == 0), stop=(k == 1))
                mm.then_inc(wa_done, 1)
                pe.wait_ge(wa_copied, 1)
                for t in range(T):
                    mm = pe.matmul(PS[:, 1, t * 2 * H:(t + 1) * 2 * H], ctxT[:, t * P:(t + 1) * P],
                                   w0x[:, H * FO:WX], start=True, stop=True)
                mm.then_inc(st0_done, 1)

            def graph_hot(h):
                for b in range(2):
                    pe.wait_ge(hot_ready, HT * h + 2 * b + 2)
                    for m in range(2):
                        for n in range(2):
                            mm = pe.transpose(PS[:, BANK[h] + b, m * 256 + n * P:m * 256 + (n + 1) * P],
                                              hot[h][:, 2 * b + n, m * P:(m + 1) * P], ident[:, :])
                    mm.then_inc(hotT_done, 1)

            def graph_first(h):
                pe.wait_ge(ctx_loaded, 16)
                pe.wait_ge(hotT_copied, 2 * h + 2)
                for b in range(2):
                    for m in range(2):
                        mm = pe.matmul(PS[0:D, BANK[h], b * 256:(b + 1) * 256], ctx_s[:, h * HT + 2 * b + m, :],
                                       hotT[h][:, b, m, :], start=(m == 0), stop=(m == 1))
                mm.then_inc(g0_done, 1)

            def graph_hidden(h):
                pe.wait_ge(g0_copied, h + 1)
                pe.wait_ge(gat_loaded, 16 * 4)
                for k in range(2):
                    mm = pe.matmul(PS[:, BANK[h] + k, :], w0x[:, k * P:(k + 1) * P], g0T[h][:, :], start=True, stop=True)
                mm.then_inc(h0_done, 1)

            def graph_feat(h):
                pe.wait_ge(h0_ready, h + 1)
                for i in range(HT):
                    if i >= 2:
                        pe.wait_ge(feat_ready, HT * h + i - 1)
                    for k in range(2):
                        mm = pe.matmul(PS[:, BANK[h] + i % 2, 0:WX], h0T[h][:, k, i * P:(i + 1) * P], w1x[:, k, :],
                                       start=(k == 0), stop=(k == 1))
                    mm.then_inc(feat_done, 1)

            def graph_out(h):
                pe.wait_ge(feat_ready, HT * (h + 1))
                for i in range(HT):
                    b, n = i // 2, i % 2
                    for m in range(2):
                        mm = pe.matmul(PS[:, BANK[h] + b, n * 256:(n + 1) * 256],
                                       hotT[h][:, b, m, n * P:(n + 1) * P],
                                       feat[h][:, 2 * b + m, 0:H * FO], start=(m == 0), stop=(m == 1))
                mm.then_inc(out1_done, 1)

            def general_path(h):
                g = general[h]

                def heads(start, at):
                    with pe.Fori(0, H) as hd:
                        k = start + hd * HEAD_STEPS + at
                        pe.wait_ge(g, k + 1)
                        for m in range(2):
                            mm = pe.matmul(PS[:, 6, m * P:(m + 1) * P], ones[:, :], gD[:, m, :], start=True, stop=True)
                        mm.then_inc(g, 1)
                        pe.wait_ge(g, k + 8)
                        for m in range(2):
                            for n in range(2):
                                mm = pe.transpose(PS[:, 7, m * 256 + n * P:m * 256 + (n + 1) * P],
                                                  gEa[:, n, m * P:(m + 1) * P], ident[:, :])
                        mm.then_inc(g, 1)
                        pe.wait_ge(g, k + 10)
                        for n in range(2):
                            for m in range(2):
                                mm = pe.matmul(PS[:, 6, n * FO:(n + 1) * FO], gEb[:, m, n * P:(n + 1) * P],
                                               gfeat[:, m, bass.ds(hd * FO, FO)], start=(m == 0), stop=(m == 1))
                        mm.then_inc(g, 1)

                with pe.Fori(0, 2) as b:
                    start = b * BATCH_STEPS + 1
                    pe.wait_ge(g, start + 1)
                    for m in range(2):
                        mm = pe.matmul(PS[:, 6 + m, 0:WX], gctxT[:, m * P:(m + 1) * P], w0x[:, :],
                                       start=True, stop=True)
                    mm.then_inc(g, 1)
                    heads(start, PRE_STEPS)
                    k = start + (PRE_STEPS + H * HEAD_STEPS)
                    pe.wait_ge(g, k)
                    for m in range(2):
                        for n in range(2):
                            mm = pe.transpose(PS[:, 6, m * 256 + n * P:m * 256 + (n + 1) * P],
                                              gout[:, n, m * P:(m + 1) * P], ident[:, :])
                    mm.then_inc(g, 1)
                    pe.wait_ge(g, k + 5)
                    for m in range(2):
                        for kk in range(2):
                            mm = pe.matmul(PS[:, 6 + m, 0:WX], gout[:, kk, m * P:(m + 1) * P], w1x[:, kk, :],
                                           start=(kk == 0), stop=(kk == 1))
                    mm.then_inc(g, 1)
                    heads(start, PRE_STEPS + H * HEAD_STEPS + MID_STEPS)
                pe.wait_ge(g, 1 + 2 * BATCH_STEPS)

            def graph_check(h):
                pe.wait_ge(good_ready, h + 1)
                pe.wait_ge(sim_copied, 4)
                pe.matmul(PS[:, 3, 0:1], ones[:, :], gmin[:, h, 1:2], start=True, stop=True).then_inc(bad_counted, 1)
                if h == 1:
                    pe.wait_ge(xnT_copied, 1)
                pe.wait_ge(flag_ready, h + 1)
                r = pe.value_load(flag[0:1, h:h + 1], min_val=0, max_val=1)
                with pe.If(r):
                    general_path(h)

            def turn_tokens(n, bank, at, tiles):
                pe.wait_ge(xn_ready, n + 1)
                for i in range(tiles):
                    for k in range(2):
                        mm = pe.transpose(PS[:, bank + k, i * P:(i + 1) * P], xn[:, at + i, k * P:(k + 1) * P],
                                          ident[:, :])
                mm.then_inc(xnT_done, 1)

            def turn_ffn(h):
                if h == 0:
                    open_clock_gate(WARM_UP_FFN)
                turn_tokens(XT["turn_ffn", h], 6, 0, HT)
                if h == 0:
                    pe.wait_ge(ffn_loaded, 16 * 7)

            def ffn_up(h, it):
                n = h * IT + it
                M = min(P, INTER - it * P)
                if n >= 2:
                    pe.wait_ge(ffn_h_ready, n - 1)
                if it == 0:
                    pe.wait_ge(xnT_copied, XT["turn_ffn", h] + 1)
                for w, bank, ready in ((gw, n % 2, ffn_g_done), (uw, 2 + n % 2, ffn_u_done)):
                    for k in range(2):
                        mm = pe.matmul(PS[0:M, bank, :], w[:, k, it * P:it * P + M], xnT[:, h, k, :],
                                       start=(k == 0), stop=(k == 1))
                    mm.then_inc(ready, 1)

            def ffn_down(p):
                t, n = PARTS[p]
                pe.wait_ge(ffn_h_ready, IT * (t // HT + 1))
                if p == 1:
                    pe.wait_ge(down_read, 1)
                for i in range(t % HT, t % HT + n):
                    for it in range(IT):
                        K = min(P, INTER - it * P)
                        mm = pe.matmul(PS[:, 4 + i // 2, (i % 2) * 256:(i % 2 + 1) * 256],
                                       hT[0:K, it, i * P:(i + 1) * P], dw[0:K, it, :],
                                       start=(it == 0), stop=(it == IT - 1))
                mm.then_inc(down_done, 1)

            def lost(h):
                pe.wait_ge(xnT_copied, XT["turn_ffn", 1] + 1)
                pe.wait_ge(found_ready, 1)
                pe.matmul(PS[:, 6, 0:1], ones[:, :], found[:, 1, 1:2], start=True, stop=True).then_inc(lost_counted, 1)

            def kept(h):
                pe.wait_ge(xnT_copied, XT["turn_ffn", 1] + 1)
                if h == 1:
                    pe.wait_ge(scores_read, 1)
                pe.wait_ge(a2_ready, HT * (h + 1))
                for b in range(2):
                    for m in range(2):
                        for n in range(2):
                            mm = pe.transpose(PS[:, 6 + b, m * 256 + n * P:m * 256 + (n + 1) * P],
                                              a2[:, h * HT + 2 * b + n, m * P:(m + 1) * P], ident[:, :])
                mm.then_inc(a2T_done, 1)

            def turn_moe(p):
                t, n = PARTS[p]
                turn_tokens(XT["turn_moe", p], TURN_BANK[p], t % HT, n)

            def router(p):
                t, n = PARTS[p]
                pe.wait_ge(xnT_copied, XT["turn_moe", p] + 1)
                pe.wait_ge(router_loaded, 16)
                for i in range(n):
                    at = (t % HT + i) * P
                    for k in range(2):
                        mm = pe.matmul(PS[:, TURN_BANK[p], i * E:(i + 1) * E], xnT[:, t // HT, k, at:at + P],
                                       rg[:, k, :], start=(k == 0), stop=(k == 1))
                mm.then_inc(scores_done, 1)

            steps = dict(queries=queries, sims=sims, logits=logits, graph_hot=graph_hot, graph_first=graph_first,
                         graph_hidden=graph_hidden, graph_feat=graph_feat, graph_out=graph_out,
                         graph_check=graph_check, turn_ffn=turn_ffn, ffn_up=ffn_up, ffn_down=ffn_down, lost=lost, kept=kept,
                         turn_moe=turn_moe, router=router)
            pe.wait_ge(consts, CONSTS)
            open_clock_gate(WARM_UP)
            for name, *at in SCHEDULE:
                if name in steps:
                    steps[name](*at)

            pe.wait_ge(onehots_ready, 1)
            pe.wait_ge(down_read, len(PARTS))
            Os_flat = Os[:, :, :].rearrange("p e t -> p (e t)")
            pe.matmul(PS[:, 4, 0:E * T], ones[:, :], Os_flat, start=True, stop=True).then_inc(count_done, 1)
            pe.matmul(PS[:, 5, 0:E * T], before[:, :], Os_flat, start=True, stop=True).then_inc(rank_done, 1)
            def block_list(v, first, n_cols):
                pe.wait_ge(rh_ready, v + 1)
                for n in range(2 * T):
                    if n % 4 == 0:
                        pe.wait_ge(ph_ready, n // 4 + 1)
                    mm = pe.matmul(PS[:, 6 + v, 0:n_cols * NL].rearrange("p (a b) -> p a b", a=n_cols),
                                   places[:, n, :], RH[:, first:first + n_cols, n, :],
                                   start=(n == 0), stop=(n == 2 * T - 1))
                mm.then_inc(list_done, 1)

            block_list(0, 1, 2)

            def turn_x(j, q):
                for k in range(2):
                    mm = pe.transpose(PS[:, 4, q * 256 + k * P:q * 256 + (k + 1) * P], xg[q][:, k * P:(k + 1) * P],
                                      ident[:, :])
                mm.then_inc(xgT_done, 1)

            def up(w, bank, q, at, ready):
                for k in range(2):
                    mm = pe.matmul(PS[:, bank + q, :], xgT[q][:, k, :], w[:, bass.ds(at + k * F, F)],
                                   start=(k == 0), stop=(k == 1))
                mm.then_inc(ready, 1)

            def turn_h(j, q):
                pe.wait_ge(gated, j + 1)
                for k in range(4):
                    mm = pe.transpose(PS[:, 5, k * P:(k + 1) * P], hh[q][:, k * P:(k + 1) * P], ident[:, :])
                mm.then_inc(hhT_done, 1)

            def down(j, q, at):
                pe.wait_ge(hhT_copied, j + 1)
                for k in range(4):
                    mm = pe.matmul(PS[:, 6 + q, 0:C], hhT[q][:, k * P:(k + 1) * P],
                                   e2[:, bass.ds(at + k * C, C)], start=(k == 0), stop=(k == 3))
                mm.then_inc(y_done, 1)

            def expert(j):
                return pe.value_load(eoff[0:1, bass.ds(j, 1)], min_val=0, max_val=(E - 1) * 1024)

            pe.wait_ge(eoff_ready, 1)
            pe.wait_ge(rank_done, 1)
            pe.wait_ge(list_ready, 1)
            pe.wait_ge(experts_loaded, 16 * 3 * E)
            at = expert(0)
            pe.wait_ge(gathered[0], 16)
            turn_x(0, 0)
            pe.wait_ge(xgT_copied, 1)
            up(e1, 0, 0, at, up1_done)
            block_list(1, 3, 3)
            pe.wait_ge(gathered[1], 16)
            turn_x(1, 1)
            up(e3, 2, 0, at, up3_done)

            def pair(i, first=False):
                for q in range(2):
                    j = i * 2 + (1 + q)
                    me, other = (q + 1) % 2, q
                    at = expert(j)
                    pe.wait_ge(xgT_copied, j + 1)
                    if q or not first:
                        pe.wait_ge(gated, j - 1)
                    up(e1, 0, me, at, up1_done)
                    if q or not first:
                        pe.wait_ge(hhT_copied, j - 1)
                    turn_h(j - 1, other)
                    pe.wait_ge(gathered[other], i * 16 + 32)
                    turn_x(j + 1, other)
                    up(e3, 2, me, at, up3_done)
                    last = expert(j - 1)
                    if not first:
                        pe.wait_ge(y_scaled, j - 2)
                    elif q:
                        pe.wait_ge(coef_ready, 1)
                    down(j - 1, other, last)

            pair(0, first=True)
            pairs = pairs_in_use(pe)
            with pe.Fori(1, pairs) as i:
                pair(i)
            pe.wait_ge(hhT_copied, pairs * 2)
            turn_h(pairs * 2, 0)
            pe.wait_ge(y_scaled, pairs * 2)
            down(pairs * 2, 0, expert(pairs * 2))


_OUT = "out_0_dram"


def kernel(**inputs):
    import numpy as np
    import concourse.bacc as bacc
    from concourse.bass_utils import run_bass_kernel_spmd as run

    i = {k: np.asarray(v) for k, v in inputs.items()}
    pad = IT * P - INTER

    def columns(v):
        return np.concatenate([v, np.zeros(pad, v.dtype)]).reshape(IT, P).T

    def by_head(layer):
        a = np.zeros((H, FO, 2, H), i["L0_xattn_a_self0"].dtype)
        for n, name in enumerate(("self", "neigh")):
            for h in range(H):
                a[h, :, n, h] = i[f"L0_xattn_a_{name}{layer}"][h]
        return a.reshape(H * FO, 2 * H)

    def expert(w, k):
        e, n, kp = w.shape
        return w.reshape(e, n, k, P).transpose(0, 3, 2, 1).reshape(e, P, k * n)

    arrays = {
        "x_in": i["x"].reshape(B * N, C),
        "ctx_in": i["ctx_512"].reshape(B * N, D),
        "ctxT_in": i["ctx_512"].reshape(B * N, D).T,
        "g_xattn": i["g_xattn"], "g_ffn": i["g_ffn"], "gamma": i["L1_xattn_gamma_raw"].reshape(1),
        "w0_in": i["L0_xattn_W0"].transpose(1, 0, 2).reshape(D, H * FO),
        "w0T_in": i["L0_xattn_W0"].transpose(0, 2, 1).reshape(H * FO, D),
        "b0_in": i["L0_xattn_b0"].reshape(2, P).T,
        "w1_in": i["L0_xattn_W1"].transpose(1, 0, 2).reshape(C, H * FO),
        "w1T_in": i["L0_xattn_W1"].transpose(0, 2, 1).reshape(H * FO, C),
        "a_in": np.stack([by_head("0"), by_head("1")]), "b1_in": i["L0_xattn_b1"],
        "gw_in": i["L0_ffn_gate_w"].T, "uw_in": i["L0_ffn_up_w"].T, "dw_in": i["L0_ffn_down_w"].T,
        "gs_in": columns(i["L0_ffn_gate_s"]), "us_in": columns(i["L0_ffn_up_s"]), "ds_in": i["L0_ffn_down_s"],
        "wq_in": i["L1_xattn_Wq"].T, "wk_in": i["L1_xattn_Wk"].T, "rg_in": i["L1_ffn_gate_w"].T,
        "e1_in": expert(i["L1_ffn_w1"], 2), "e3_in": expert(i["L1_ffn_w3"], 2),
        "e2_in": expert(i["L1_ffn_w2"], 4),
    }
    arrays = {k: np.ascontiguousarray(v) for k, v in arrays.items()}
    nc = bacc.Bacc("TRN2", target_bir_lowering=False, num_devices=1)
    args = [nc.dram_tensor(k, v.shape, mybir.dt.from_np(v.dtype), kind="ExternalInput").ap()
            for k, v in arrays.items()]
    args.append(nc.dram_tensor(_OUT, [B * N, C], F32, kind="ExternalOutput").ap())
    build(nc, *args)
    r = run(nc, [arrays], core_ids=[0])
    return r.results[0][_OUT].reshape(B, N, C)
```
